# Optimizing a Trainium2 kernel written in Bass

```python
import numpy as np
import jax
import jax.numpy as jnp

def _softmax(x, axis=-1):
    return jax.nn.softmax(x, axis=axis)

def _gelu(x):
    return jax.nn.gelu(x, approximate=True)

def _silu(x):
    return jax.nn.silu(x)

def _sigmoid(x):
    return jax.nn.sigmoid(x)

def _layernorm(x, axis=-1, eps=1e-05):
    m = jnp.mean(x, axis=axis, keepdims=True)
    v = jnp.var(x, axis=axis, keepdims=True)
    return (x - m) / jnp.sqrt(v + eps)

def _scatter_add(tgt, idx, src, axis=0):
    return tgt.at[idx].add(src)

def _segment_sum(src, seg, n):
    return jax.ops.segment_sum(src, seg, n)
kernel_name = 'mk_seq_postln_d2_jaxref_r8_ee975c'

def setup_inputs(seed: int=0):
    np.random.seed(seed)
    _w = jnp.asarray

    def _L0_attn_setup():
        import jax, jax.numpy as jnp
        import numpy as np
        B, T, D = (2, 256, 128)
        H = 16
        DH = D // H
        EPS = 1e-06

        def _feature_map(x):
            return jax.nn.elu(x) + 1.0
        key = jax.random.key(seed)
        ks = jax.random.split(key, 9)
        s = 0.02
        return {'x': jax.random.normal(ks[0], (B, T, D), dtype=jnp.float32), 'Wq': jax.random.normal(ks[1], (D, D), dtype=jnp.float32) * s, 'bq': jnp.zeros((D,), dtype=jnp.float32), 'Wk': jax.random.normal(ks[2], (D, D), dtype=jnp.float32) * s, 'bk': jnp.zeros((D,), dtype=jnp.float32), 'Wv': jax.random.normal(ks[3], (D, D), dtype=jnp.float32) * s, 'bv': jnp.zeros((D,), dtype=jnp.float32), 'Wo': jax.random.normal(ks[4], (D, D), dtype=jnp.float32) * s, 'bo': jnp.zeros((D,), dtype=jnp.float32)}
    _L0_attn_in = _L0_attn_setup()

    def _L0_ffn_setup():
        import jax, jax.numpy as jnp
        import numpy as np
        TOPK = 8
        NUM_EXPERTS = 64
        FFN = 384
        CAPACITY = 160

        def _swiglu(x, w1, w2):
            h = x @ w1.T
            x1, x2 = jnp.split(h, 2, axis=-1)
            return x1 * jax.nn.silu(x2) @ w2.T
        key = jax.random.key(seed)
        ks = jax.random.split(key, 6)
        B, S, H = (1, 64, 128)
        scale = 0.02
        return {'hidden_states': jax.random.normal(ks[0], (B, S, H), jnp.float32), 'wg': jax.random.normal(ks[1], (NUM_EXPERTS, H), jnp.float32) * scale, 'shared_w1': jax.random.normal(ks[2], (2 * FFN, H), jnp.float32) * scale, 'shared_w2': jax.random.normal(ks[3], (H, FFN), jnp.float32) * scale, 'expert_w1': jax.random.normal(ks[4], (NUM_EXPERTS, 2 * FFN, H), jnp.float32) * scale, 'expert_w2': jax.random.normal(ks[5], (NUM_EXPERTS, H, FFN), jnp.float32) * scale}
    _L0_ffn_in = _L0_ffn_setup()

    def _L1_attn_setup():
        import math
        import jax, jax.numpy as jnp
        import numpy as np
        B, T, D, H, L = (8, 256, 128, 16, 4)
        DK = D // H
        EPS_LN = 1e-05
        EPS_ATTN = 1e-06

        def _layernorm(x, scale, bias):
            mu = jnp.mean(x, axis=-1, keepdims=True)
            var = jnp.mean(jnp.square(x - mu), axis=-1, keepdims=True)
            return (x - mu) * jax.lax.rsqrt(var + EPS_LN) * scale + bias

        def _sinusoidal_pos_emb(t, d):
            half = d // 2
            freq = jnp.exp(jnp.arange(half, dtype=jnp.float32) * (-math.log(10000.0) / (half - 1)))
            pos = (jnp.arange(t, dtype=jnp.float32) + 1.0)[:, None] * freq[None, :]
            return jnp.concatenate([jnp.sin(pos), jnp.cos(pos)], axis=-1)

        def _linear_attention(q, k, v):
            qp = jax.nn.elu(q) + 1.0
            kp = jax.nn.elu(k) + 1.0
            kv = jnp.einsum('bshd,bshm->bhmd', kp, v)
            ksum = jnp.sum(kp, axis=1)
            z = 1.0 / (jnp.einsum('blhd,bhd->blh', qp, ksum) + EPS_ATTN)
            return jnp.einsum('blhd,bhmd,blh->blhm', qp, kv, z)

        def _encoder_layer(x, Wq, bq, Wk, bk, Wv, bv, Wo, bo, W1, b1, W2, b2, ln1_s, ln1_b, ln2_s, ln2_b):
            b, t, d = x.shape
            h = _layernorm(x, ln1_s, ln1_b)
            q = (h @ Wq + bq).reshape(b, t, H, DK)
            k = (h @ Wk + bk).reshape(b, t, H, DK)
            v = (h @ Wv + bv).reshape(b, t, H, DK)
            attn = _linear_attention(q, k, v).reshape(b, t, d)
            x = x + (attn @ Wo + bo)
            h = _layernorm(x, ln2_s, ln2_b)
            h = jax.nn.relu(h @ W1 + b1) @ W2 + b2
            return x + h
        key = jax.random.key(seed)
        ks = jax.random.split(key, 8)
        w = lambda k, shape: jax.random.normal(k, shape, dtype=jnp.float32) * 0.02
        return {'x_in': jax.random.normal(ks[0], (B, T, D), dtype=jnp.float32), 'Wq': w(ks[1], (L, D, D)), 'bq': jnp.zeros((L, D), jnp.float32), 'Wk': w(ks[2], (L, D, D)), 'bk': jnp.zeros((L, D), jnp.float32), 'Wv': w(ks[3], (L, D, D)), 'bv': jnp.zeros((L, D), jnp.float32), 'Wo': w(ks[4], (L, D, D)), 'bo': jnp.zeros((L, D), jnp.float32), 'W1': w(ks[5], (L, D, 4 * D)), 'b1': jnp.zeros((L, 4 * D), jnp.float32), 'W2': w(ks[6], (L, 4 * D, D)), 'b2': jnp.zeros((L, D), jnp.float32), 'ln1_s': jnp.ones((L, D), jnp.float32), 'ln1_b': jnp.zeros((L, D), jnp.float32), 'ln2_s': jnp.ones((L, D), jnp.float32), 'ln2_b': jnp.zeros((L, D), jnp.float32), 'lnf_s': jnp.ones((D,), jnp.float32), 'lnf_b': jnp.zeros((D,), jnp.float32)}
    _L1_attn_in = _L1_attn_setup()

    def _L1_ffn_setup():
        import jax, jax.numpy as jnp
        import numpy as np
        CAPACITY_RATIO = 0.75
        key = jax.random.key(seed)
        k1, k2, k3 = jax.random.split(key, 3)
        B, L, D = (4, 1024, 128)
        x = jax.random.normal(k1, (B, L, D), dtype=jnp.float32)
        w_router = jax.random.normal(k2, (D,), dtype=jnp.float32) * 0.02
        w_block = jax.random.normal(k3, (D, D), dtype=jnp.float32) * 0.02
        return {'x': x, 'w_router': w_router, 'w_block': w_block}
    _L1_ffn_in = _L1_ffn_setup()
    _d = {'L0_attn_x': _L0_attn_in['x'], 'L0_attn_Wq': _L0_attn_in['Wq'], 'L0_attn_bq': _L0_attn_in['bq'], 'L0_attn_Wk': _L0_attn_in['Wk'], 'L0_attn_bk': _L0_attn_in['bk'], 'L0_attn_Wv': _L0_attn_in['Wv'], 'L0_attn_bv': _L0_attn_in['bv'], 'L0_attn_Wo': _L0_attn_in['Wo'], 'L0_attn_bo': _L0_attn_in['bo'], 'L0_ffn_wg': _L0_ffn_in['wg'], 'L0_ffn_shared_w1': _L0_ffn_in['shared_w1'], 'L0_ffn_shared_w2': _L0_ffn_in['shared_w2'], 'L0_ffn_expert_w1': _L0_ffn_in['expert_w1'], 'L0_ffn_expert_w2': _L0_ffn_in['expert_w2'], 'L1_attn_Wq': _L1_attn_in['Wq'], 'L1_attn_bq': _L1_attn_in['bq'], 'L1_attn_Wk': _L1_attn_in['Wk'], 'L1_attn_bk': _L1_attn_in['bk'], 'L1_attn_Wv': _L1_attn_in['Wv'], 'L1_attn_bv': _L1_attn_in['bv'], 'L1_attn_Wo': _L1_attn_in['Wo'], 'L1_attn_bo': _L1_attn_in['bo'], 'L1_attn_W1': _L1_attn_in['W1'], 'L1_attn_b1': _L1_attn_in['b1'], 'L1_attn_W2': _L1_attn_in['W2'], 'L1_attn_b2': _L1_attn_in['b2'], 'L1_attn_ln1_s': _L1_attn_in['ln1_s'], 'L1_attn_ln1_b': _L1_attn_in['ln1_b'], 'L1_attn_ln2_s': _L1_attn_in['ln2_s'], 'L1_attn_ln2_b': _L1_attn_in['ln2_b'], 'L1_attn_lnf_s': _L1_attn_in['lnf_s'], 'L1_attn_lnf_b': _L1_attn_in['lnf_b'], 'L1_ffn_w_router': _L1_ffn_in['w_router'], 'L1_ffn_w_block': _L1_ffn_in['w_block']}
    _x0 = _d['L0_attn_x']
    _d['L0_attn_x'] = jax.random.normal(jax.random.fold_in(jax.random.key(seed), 1), (8, 256, 128), dtype=_x0.dtype)
    del _x0
    return _d

def reference(L0_attn_x, L0_attn_Wq, L0_attn_bq, L0_attn_Wk, L0_attn_bk, L0_attn_Wv, L0_attn_bv, L0_attn_Wo, L0_attn_bo, L0_ffn_wg, L0_ffn_shared_w1, L0_ffn_shared_w2, L0_ffn_expert_w1, L0_ffn_expert_w2, L1_attn_Wq, L1_attn_bq, L1_attn_Wk, L1_attn_bk, L1_attn_Wv, L1_attn_bv, L1_attn_Wo, L1_attn_bo, L1_attn_W1, L1_attn_b1, L1_attn_W2, L1_attn_b2, L1_attn_ln1_s, L1_attn_ln1_b, L1_attn_ln2_s, L1_attn_ln2_b, L1_attn_lnf_s, L1_attn_lnf_b, L1_ffn_w_router, L1_ffn_w_block):

    def _L0_attn_ref(x, Wq, bq, Wk, bk, Wv, bv, Wo, bo):
        import jax, jax.numpy as jnp
        import numpy as np
        B, T, D = (2, 256, 128)
        H = 16
        DH = D // H
        EPS = 1e-06

        def _feature_map(x):
            return jax.nn.elu(x) + 1.0
        b, t, d = x.shape
        q = (x @ Wq.T + bq).reshape(b, t, H, DH).transpose(0, 2, 1, 3)
        k = (x @ Wk.T + bk).reshape(b, t, H, DH).transpose(0, 2, 1, 3)
        v = (x @ Wv.T + bv).reshape(b, t, H, DH).transpose(0, 2, 1, 3)
        q = _feature_map(q)
        k = _feature_map(k)
        kv = jnp.einsum('bhtd,bhte->bhtde', k, v)
        kv_cum = jnp.cumsum(kv, axis=2)
        numerator = jnp.einsum('bhtd,bhtde->bhte', q, kv_cum)
        k_cum = jnp.cumsum(k, axis=2)
        denominator = jnp.einsum('bhtd,bhtd->bht', q, k_cum)
        denominator = jnp.maximum(denominator, EPS)[..., None]
        out = numerator / denominator
        out = out.transpose(0, 2, 1, 3).reshape(b, t, d)
        return out @ Wo.T + bo

    def _L0_ffn_ref(hidden_states, wg, shared_w1, shared_w2, expert_w1, expert_w2):
        import jax, jax.numpy as jnp
        import numpy as np
        TOPK = 8
        NUM_EXPERTS = 64
        FFN = 384
        CAPACITY = 160

        def _swiglu(x, w1, w2):
            h = x @ w1.T
            x1, x2 = jnp.split(h, 2, axis=-1)
            return x1 * jax.nn.silu(x2) @ w2.T
        B, S, H = hidden_states.shape
        T = B * S
        x = hidden_states.reshape(T, H)
        shared_out = _swiglu(x, shared_w1, shared_w2)
        logits = x.astype(jnp.float32) @ wg.T
        gates = jax.nn.softmax(logits, axis=-1)
        w_topk, idx_topk = jax.lax.top_k(gates, TOPK)
        denom = jnp.maximum(w_topk.sum(-1, keepdims=True), jnp.finfo(jnp.float32).eps)
        w_topk = w_topk / denom
        A = T * TOPK
        flat_e = idx_topk.reshape(A)
        flat_w = w_topk.reshape(A)
        flat_t = jnp.repeat(jnp.arange(T), TOPK)
        order = jnp.argsort(flat_e)
        se, st, sw = (flat_e[order], flat_t[order], flat_w[order])
        counts = jnp.zeros(NUM_EXPERTS, jnp.int32).at[flat_e].add(1)
        starts = jnp.cumsum(counts) - counts
        rank = jnp.arange(A) - starts[se]
        valid = rank < CAPACITY
        buf = jnp.zeros((NUM_EXPERTS, CAPACITY, H), x.dtype).at[se, rank].set(x[st], mode='drop')
        h = jnp.einsum('ech,efh->ecf', buf, expert_w1)
        x1, x2 = jnp.split(h, 2, axis=-1)
        out = jnp.einsum('ecf,ehf->ech', x1 * jax.nn.silu(x2), expert_w2)
        y = out[se, jnp.clip(rank, 0, CAPACITY - 1)]
        y = jnp.where(valid[:, None], y * sw[:, None].astype(y.dtype), 0.0)
        combined = jnp.zeros((T, H), x.dtype).at[st].add(y)
        return (shared_out + combined).reshape(B, S, H)

    def _L1_attn_ref(x_in, Wq, bq, Wk, bk, Wv, bv, Wo, bo, W1, b1, W2, b2, ln1_s, ln1_b, ln2_s, ln2_b, lnf_s, lnf_b):
        import math
        import jax, jax.numpy as jnp
        import numpy as np
        B, T, D, H, L = (8, 256, 128, 16, 4)
        DK = D // H
        EPS_LN = 1e-05
        EPS_ATTN = 1e-06

        def _layernorm(x, scale, bias):
            mu = jnp.mean(x, axis=-1, keepdims=True)
            var = jnp.mean(jnp.square(x - mu), axis=-1, keepdims=True)
            return (x - mu) * jax.lax.rsqrt(var + EPS_LN) * scale + bias

        def _sinusoidal_pos_emb(t, d):
            half = d // 2
            freq = jnp.exp(jnp.arange(half, dtype=jnp.float32) * (-math.log(10000.0) / (half - 1)))
            pos = (jnp.arange(t, dtype=jnp.float32) + 1.0)[:, None] * freq[None, :]
            return jnp.concatenate([jnp.sin(pos), jnp.cos(pos)], axis=-1)

        def _linear_attention(q, k, v):
            qp = jax.nn.elu(q) + 1.0
            kp = jax.nn.elu(k) + 1.0
            kv = jnp.einsum('bshd,bshm->bhmd', kp, v)
            ksum = jnp.sum(kp, axis=1)
            z = 1.0 / (jnp.einsum('blhd,bhd->blh', qp, ksum) + EPS_ATTN)
            return jnp.einsum('blhd,bhmd,blh->blhm', qp, kv, z)

        def _encoder_layer(x, Wq, bq, Wk, bk, Wv, bv, Wo, bo, W1, b1, W2, b2, ln1_s, ln1_b, ln2_s, ln2_b):
            b, t, d = x.shape
            h = _layernorm(x, ln1_s, ln1_b)
            q = (h @ Wq + bq).reshape(b, t, H, DK)
            k = (h @ Wk + bk).reshape(b, t, H, DK)
            v = (h @ Wv + bv).reshape(b, t, H, DK)
            attn = _linear_attention(q, k, v).reshape(b, t, d)
            x = x + (attn @ Wo + bo)
            h = _layernorm(x, ln2_s, ln2_b)
            h = jax.nn.relu(h @ W1 + b1) @ W2 + b2
            return x + h
        b, t, d = x_in.shape
        x = math.sqrt(d) * x_in + _sinusoidal_pos_emb(t, d)[None, :, :]
        for i in range(L):
            x = _encoder_layer(x, Wq[i], bq[i], Wk[i], bk[i], Wv[i], bv[i], Wo[i], bo[i], W1[i], b1[i], W2[i], b2[i], ln1_s[i], ln1_b[i], ln2_s[i], ln2_b[i])
        return _layernorm(x, lnf_s, lnf_b)

    def _L1_ffn_ref(x, w_router, w_block):
        import jax, jax.numpy as jnp
        import numpy as np
        CAPACITY_RATIO = 0.75
        B, L, D = x.shape
        k = max(1, int(L * CAPACITY_RATIO))
        scores = jnp.einsum('bld,d->bl', x, w_router)
        _, top_idx = jax.lax.top_k(scores, k)
        selected = jnp.take_along_axis(x, top_idx[:, :, None], axis=1)
        processed = jax.nn.gelu(jnp.einsum('bkd,de->bke', selected, w_block))
        batch_idx = jnp.arange(B)[:, None]
        out = x.at[batch_idx, top_idx].set(processed)
        return out
    x = L0_attn_x
    x = _layernorm(x + _L0_attn_ref(x, L0_attn_Wq, L0_attn_bq, L0_attn_Wk, L0_attn_bk, L0_attn_Wv, L0_attn_bv, L0_attn_Wo, L0_attn_bo), axis=-1)
    x = _layernorm(x + _L0_ffn_ref(x, L0_ffn_wg, L0_ffn_shared_w1, L0_ffn_shared_w2, L0_ffn_expert_w1, L0_ffn_expert_w2), axis=-1)
    x = _layernorm(x + _L1_attn_ref(x, L1_attn_Wq, L1_attn_bq, L1_attn_Wk, L1_attn_bk, L1_attn_Wv, L1_attn_bv, L1_attn_Wo, L1_attn_bo, L1_attn_W1, L1_attn_b1, L1_attn_W2, L1_attn_b2, L1_attn_ln1_s, L1_attn_ln1_b, L1_attn_ln2_s, L1_attn_ln2_b, L1_attn_lnf_s, L1_attn_lnf_b), axis=-1)
    x = _layernorm(x + _L1_ffn_ref(x, L1_ffn_w_router, L1_ffn_w_block), axis=-1)
    return x

_drawn_inputs = setup_inputs


def setup_inputs(seed=0):
    import zlib

    import numpy as np

    out = dict(_drawn_inputs(seed))
    spreads = {'L0_attn_bq': (0.0, 0.8),
     'L0_attn_bk': (0.0, 0.8),
     'L0_attn_bv': (0.0, 0.393),
     'L0_attn_bo': (0.0, 0.1),
     'L1_attn_bq': (0.0, 2.0),
     'L1_attn_bk': (0.0, 2.0),
     'L1_attn_bv': (0.0, 0.8),
     'L1_attn_bo': (0.0, 0.8),
     'L1_attn_b1': (0.0, 0.8),
     'L1_attn_b2': (0.0, 0.8),
     'L1_attn_ln1_s': (1.0, 0.6),
     'L1_attn_ln1_b': (0.0, 0.8),
     'L1_attn_ln2_s': (1.0, 0.6),
     'L1_attn_ln2_b': (0.0, 0.8),
     'L1_attn_lnf_s': (1.0, 0.2),
     'L1_attn_lnf_b': (0.0, 0.1)}
    factors = {'L0_attn_Wq': 8.0,
     'L0_attn_Wk': 8.0,
     'L0_attn_Wv': 6.142,
     'L0_ffn_wg': 8.0,
     'L0_ffn_shared_w1': 5.2,
     'L0_ffn_shared_w2': 5.007,
     'L0_ffn_expert_w1': 8.0,
     'L0_ffn_expert_w2': 8.0,
     'L1_attn_Wq': 22.897,
     'L1_attn_Wk': 8.0,
     'L1_attn_Wv': 8.0,
     'L1_attn_Wo': 8.0,
     'L1_attn_W1': 8.0,
     'L1_attn_W2': 7.76}
    for name, (base, spread) in spreads.items():
        noise = np.random.default_rng([zlib.crc32(name.encode()), seed]).standard_normal(out[name].shape)
        drawn = base * np.exp(spread * noise) if base else spread * noise
        out[name] = jnp.asarray(drawn.astype(out[name].dtype))
    for name, factor in factors.items():
        out[name] = (out[name] * factor).astype(out[name].dtype)
    return out
```

```python
from contextlib import ExitStack

import numpy as np

import concourse.bass as bass
from concourse import mybir

ALU = mybir.AluOpType
ACT = mybir.ActivationFunctionType
AX = mybir.AxisListType
F32 = mybir.dt.float32
F16 = mybir.dt.float16
I32 = mybir.dt.int32
U32 = mybir.dt.uint32

P = 128
D = 128
BATCH, SEQ = 8, 256
TOK = BATCH * SEQ
TILES = TOK // P
GT = 4
GROUP = GT * P
GROUPS = TOK // GROUP
HEADS, DH = 16, 8
NE, TOPK, CAP, FFN = 64, 8, 160, 384
FB = FFN // P
EG = 8
NEG = NE // EG
RA, RB = 16, 10
LAYERS, FF = 4, 512
FFB = FF // P
KEEP = int(SEQ * 0.75)
ARENA = 22528
EPS_LN, EPS_ATTN = 1e-5, 1e-6
ROUTED = D + NE
SKIP = 65536

C_ID, C_BLK, C_HEAD, C_SEL, C_TRI, C_ONES, C_PE, C_EXP, C_TOK, C_RESET = 0, 128, 256, 272, 528, 656, 784, 1040, 1048, 1064
C_BEFORE = C_RESET + GROUP
C_ALL = C_BEFORE + 2 * SEQ


def constants():
    c = np.zeros((P, C_ALL), np.float32)
    r = np.arange(P)
    c[:, C_ID:C_ID + P] = np.eye(P)
    same_head = (r[:, None] // DH) == (r[None, :] // DH)
    c[:, C_BLK:C_BLK + P] = same_head
    c[:, C_HEAD:C_HEAD + HEADS] = (r[:, None] // DH) == np.arange(HEADS)[None, :]
    for e in range(DH):
        s = c[:, C_SEL + 32 * e:C_SEL + 32 * e + 32]
        s[:, 16 * (e % 2):16 * (e % 2) + 16] = c[:, C_HEAD:C_HEAD + HEADS]
    c[:, C_TRI:C_TRI + P] = (r[:, None] < r[None, :]) - 1.0
    c[:, C_ONES:C_ONES + P] = 1.0
    half = D // 2
    freq = np.exp(np.arange(half, dtype=np.float32) * np.float32(-np.log(10000.0) / (half - 1))).astype(np.float32)
    pos = (np.arange(SEQ, dtype=np.float32) + 1.0)[:, None] * freq[None, :]
    pe = np.concatenate([np.sin(pos), np.cos(pos)], axis=-1).astype(np.float32)
    c[:, C_PE:C_PE + 2 * D] = pe.reshape(2, P, D).transpose(1, 0, 2).reshape(P, 2 * D)
    c[:, C_EXP:C_EXP + EG] = (r[:, None] % EG) == np.arange(EG)[None, :]
    c[:, C_TOK:C_TOK + TILES] = r[:, None] + P * np.arange(TILES)[None, :] + 1.0
    for h in range(2):
        c[:, C_BEFORE + SEQ * h:C_BEFORE + SEQ * h + SEQ] = np.arange(SEQ)[None, :] < P * h + r[:, None]
    c[:, C_RESET:C_RESET + GROUP] = (np.arange(GROUP) % SEQ != 0)
    return c


class Chain:

    def __init__(self, eng, sem):
        self.eng, self.sem, self.n, self.off = eng, sem, 0, 0

    def did(self, ins):
        ins.then_inc(self.sem, 1)
        self.n += 1
        return self.off + self.n

    def after(self, number):
        self.eng.wait_ge(self.sem, number)

    def loop(self, i, per):
        self.n0, self.per = self.n, per
        self.off = i * per

    def end_loop(self, times):
        assert self.n - self.n0 == self.per, (self.n - self.n0, self.per)
        self.n = self.n0 + times * self.per
        self.off = 0


def program(nc, cst, xt0, xr0, l0w, l0p, bo0, l0s, ew, l1w, l1p, l1r, fin_r, mod_w, out):
    with ExitStack() as ctx:
        def sb(name, shape, dt=F32):
            return ctx.enter_context(nc.sbuf_tensor(name, [P] + shape, dt))

        sems = {}

        def sem(name):
            if name not in sems:
                sems[name] = ctx.enter_context(nc.semaphore(name))
            return sems[name]

        bank = [ctx.enter_context(nc.psum_tensor(f"bank{i}", [P, 512], F32)) for i in range(8)]

        dispatch_dram = nc.dram_tensor("dispatch_rows", [TOK, ROUTED], F32).ap()
        returned_dram = nc.dram_tensor("returned_rows", [TOK * TOPK, D], F32).ap()

        C = sb("consts", [C_ALL])
        ident = C[:, C_ID:C_ID + P]
        tri16, ones16 = sb("tri16", [P], F16), sb("ones16", [P], F16)
        x1 = sb("x1", [TILES, D])
        x1t = sb("x1t", [TOK])
        shared = sb("shared", [TILES, D])
        logits = sb("logits", [TILES, NE])
        gates = sb("gates", [TILES, NE])
        ring = sb("ring", [EG, 9 * D])
        arena = sb("arena", [ARENA])

        def carve(parts, at=0):
            made = {}
            for name, shape, dt in parts:
                n = int(np.prod(shape))
                words = n if dt != F16 else n // 2
                a = arena[:, at:at + words]
                if dt != F32:
                    a = a.bitcast(dt)
                if len(shape) == 2:
                    a = a.rearrange("p (a b) -> p a b", b=shape[1])
                elif len(shape) == 3:
                    a = a.rearrange("p (a b c) -> p a b c", b=shape[1], c=shape[2])
                made[name] = a
                at += words
            assert at <= ARENA, at
            return made

        A = carve([("xt", (TOK,), F32), ("w", (2 * P + DH * P + P,), F32),
                   ("eqk", (2, GROUP), F32), ("q", (2, GROUP), F32), ("k", (2, GROUP), F32),
                   ("ksum", (2, GROUP), F32), ("kv", (2, GROUP), F32), ("run", (2, GROUP), F32),
                   ("prod", (2, DH, GROUP), F32), ("dk", (GROUPS, GROUP), F32), ("att", (GROUPS, GROUP), F32)])
        at_prod = TOK + 11 * P + 12 * GROUP
        T = carve([("an", (GROUPS, GROUP), F32), ("ant", (GROUPS, GROUP), F32), ("xs", (GROUPS, GROUP), F32)],
                  at_prod)
        xr = shared
        l0ps = sb("l0ps", [10])
        bq1 = sb("bq1", [2])
        bo_bc = sb("bo_bc", [D])
        sw = sb("sw", [NE + 9 * D])

        small = sb("small", [1024])
        den = small[:, 0:GROUPS * 64].rearrange("p (g n) -> p g n", g=GROUPS)
        rden = small[:, 256:256 + GROUPS * 64].rearrange("p (g n) -> p g n", g=GROUPS)
        stats = sb("stats", [2, GT, 6])
        mv = sb("mv", [2, GT, 2])
        veps = sb("veps", [2, GT])
        rstd = sb("rstd", [2, GT])
        minus_half = sb("minus_half", [GT])
        minus_one = sb("minus_one", [1])
        zeros = sb("zeros", [1024])
        scratch = zeros
        hidden = sb("hidden", [3 * FB, GROUP])
        new_tile = sb("new_tile", [TILES * NE], F16)
        new_token = sb("new_token", [TILES * NE], F16)
        route = small[:, 512:768]
        best8 = sb("best8", [TILES, 8])
        slots = sb("slots", [NEG, 2, RB])
        picked = sb("picked", [2, 2 * RB, EG])
        gather_all, scatter_all = sb("gather_all", [NEG, RB], U32), sb("scatter_all", [NEG, RB], U32)
        gather_ix, scatter_ix = sb("gather_ix", [2, RB], U32), sb("scatter_ix", [2, RB], U32)
        slot_gate = sb("slot_gate", [2, RB])
        picked_gate = sb("picked_gate", [RB, EG])
        TE = TILES * NE
        R = carve([("a", (TILES, NEG * RA * EG), F16), ("b", (2 * RB, TE), F16), ("mask", (TE,), F16), ("mask_ei", (TE,), F16),
                   ("upto_ei", (TE,), F16), ("place", (TE,), F16), ("token", (TE,), F16), ("ai", (TE,), F16),
                   ("bi", (TE,), F16), ("here", (TE,), F16)])
        Z = 2 * D + 1
        LW, LP = 12 * P, 9
        B = carve([("h", (GROUPS, GT, D), F32), ("ht", (GROUPS, GROUP), F32), ("q", (GROUPS, GROUP), F32),
                   ("z", (GROUPS, GT * Z), F32), ("kp", (GROUPS, GT, D), F32), ("eq", (2, GROUP), F32),
                   ("ek", (2, GT, D), F32), ("kvm", (GROUPS, 2 * (D + HEADS)), F32),
                   ("relu", (2, FFB, GROUP), F32), ("returned", (2, TOPK * D), F32)])
        layer_cols = sb("layer_cols", [2, LP])
        bq_up = sb("bq_up", [2])
        kv_rows = sb("kv_rows", [2, 2 * D])
        den1, rden1 = sb("den1", [2, GT, HEADS]), sb("rden1", [2, GT, HEADS])
        E = carve([("got", (2, RB, ROUTED), F32), ("xt", (2, EG, RB * RA), F32), ("yt", (2, RB, P), F32),
                   ("back", (2, RB, D), F32), ("silu", (2, FB * CAP), F32), ("prod", (2, FB * CAP), F32)])

        block = ctx.enter_context(nc.Block())

        def tiles(buf, g):
            return buf[:, GT * g:GT * (g + 1)]

        def cols(buf, g):
            return buf[:, bass.ds(g * GROUP, GROUP)]

        def bank3(b, n=P):
            return bank[b][:, 0:GT * n].rearrange("p (i n) -> p i n", n=n)

        def staggered(steps):
            for g in range(GROUPS + len(steps) - 1):
                for k, step in enumerate(steps):
                    if 0 <= g - k < GROUPS:
                        step(g - k)

        def norm_stats(v, ch, g, src):
            s = g % 2
            for i in range(GT):
                k = ch.did(v.bn_stats(stats[:, s, i, :], src[:, i, :]))
            ch.after(k)
            v.sem_inc(sem("stats_taken"))
            for i in range(GT):
                k = ch.did(v.bn_aggr(mv[:, s, i, :], stats[:, s, i, :]))
            ch.after(k)
            v.tensor_scalar(veps[:, s, :], mv[:, s, :, 1], EPS_LN, None, ALU.add).then_inc(sem("var_ready"), 1)

        def norm_rstd(pool, n, g):
            pool.wait_ge(sem("var_ready"), n + 1)
            pool.tensor_tensor(rstd[:, g % 2, :], veps[:, g % 2, :], minus_half[:], ALU.pow).then_inc(
                sem("rstd_ready"), 1)

        def norm_apply(v, n, g, src, dst, done):
            s = g % 2
            v.wait_ge(sem("rstd_ready"), n + 1)
            for i in range(GT):
                ins = v.tensor_scalar(dst[:, i, :], src[:, i, :], mv[:, s, i, 0:1], rstd[:, s, i:i + 1],
                                      ALU.subtract, ALU.mult)
            ins.then_inc(sem(done), 1)

        def tiles_at(buf, g):
            return buf[:, bass.ds(g * GT, GT), :]

        flat_ring = ring[:].rearrange("p j n -> p (j n)")
        lw = [flat_ring[:, LW * u:LW * u + LW] for u in range(2)]
        lrows = [flat_ring[:, 2 * LW + 4 * D * u:2 * LW + 4 * D * (u + 1)] for u in range(2)]
        mod_sb = flat_ring[:, 2 * LW + 8 * D:2 * LW + 10 * D]
        fin_rows = flat_ring[:, 2 * LW + 10 * D:2 * LW + 12 * D]
        scores = flat_ring[:, 5000:5000 + 2 * GROUP].rearrange("p (s n) -> p s n", s=2)
        x2, state, plus = x1, shared, x1t[:].rearrange("p (i d) -> p i d", d=D)
        NORM_COMBINE, NORM_LAYERS = GROUPS, 2 * GROUPS
        NORM_FINAL = NORM_LAYERS + 2 * GROUPS * LAYERS

        def zrow(g):
            return B["z"][:, g].rearrange("p (i n) -> p i n", n=Z)

        def kvm(g):
            return B["kvm"][:, g].rearrange("p (b n) -> p b n", b=2)

        logits_i = logits[:].rearrange("p i e -> p (i e)").bitcast(I32)

        xt, w0 = A["xt"], A["w"]
        W_Q, W_K, W_V, W_O = 0, P, 2 * P, (2 + DH) * P
        eqk, q0, k0 = A["eqk"], A["q"][:, 0, :], A["k"][:, 0, :]
        ksum, kv, run, prod = A["ksum"][:, 0, :], A["kv"], A["run"], A["prod"][:, 0]
        dk, att = A["dk"], A["att"]
        reset = C[:, C_RESET:C_RESET + GROUP]
        head = C[:, C_HEAD:C_HEAD + HEADS]

        @block.sync
        def _(sp):
            sp.dma_start(w0, l0w).then_inc(sem("l0w_in"), 16)
            for g in range(GROUPS):
                sp.dma_start(cols(xt, g), cols(xt0, g)).then_inc(sem("xt_in"), 16)
            sp.dma_start(l0ps[:], l0p).then_inc(sem("l0p_in"), 16)
            sp.dma_start(C[:], cst).then_inc(sem("consts_in"), 16)
            sp.dma_start(xr[:], xr0).then_inc(sem("xr_in"), 16)
            sp.dma_start(bo_bc[:], bo0.partition_broadcast(P)).then_inc(sem("bo_in"), 16)
            sp.dma_start(sw[:], l0s).then_inc(sem("sw_in"), 16)
            for j in range(EG):
                sp.dma_start(ring[:, j, :], ew[j]).then_inc(sem(f"expert_in{j}"), 16)
            sp.wait_ge(sem("zeros_ready"), 1)
            zrows = returned_dram.rearrange("(n p r) d -> n p (r d)", p=P, r=8)
            for n in range(TOK * TOPK // (8 * P)):
                sp.dma_start(zrows[n], zeros[:]).then_inc(sem("zeroed"), 16)
            rows = dispatch_dram.rearrange("(i p) c -> p i c", p=P)
            sp.wait_ge(sem("x1_ready"), GROUPS)
            sp.dma_start(rows[:, :, 0:D], x1[:]).then_inc(sem("rows_out"), 16)
            sp.wait_ge(sem("gates_ready"), 1)
            sp.dma_start(rows[:, :, D:ROUTED], gates[:]).then_inc(sem("rows_out"), 16)
            with sp.Fori(1, NEG) as G:
                for j in range(EG):
                    sp.wait_ge(sem("y_mm"), G * EG + j - (EG - 1))
                    sp.dma_start(ring[:, j, :], ew[bass.ds(G * EG + j, 1)].rearrange("a p n -> (a p) n")).then_inc(
                        sem(f"expert_in{j}"), 16)
            mine = returned_dram.rearrange("(i p k) d -> i p (k d)", p=P, k=TOPK)
            for u in range(2):
                sp.wait_ge(sem(f"scattered{u}"), 16 * RB * NEG // 2)
            for i in range(TILES):
                if i >= 2:
                    sp.wait_ge(sem("returned_read"), i - 1)
                sp.dma_start(B["returned"][:, i % 2, :], mine[i]).then_inc(sem(f"returned_in{i % 2}"), 16)

            def layer(u, w, c, r):
                sp.dma_start(lw[u], w).then_inc(sem(f"layer_in{u}"), 16)
                sp.dma_start(layer_cols[:, u, :], c).then_inc(sem(f"layer_in{u}"), 16)
                sp.dma_start(lrows[u], r.partition_broadcast(P)).then_inc(sem(f"layer_in{u}"), 16)

            for u in range(2):
                layer(u, l1w[u], l1p[u], l1r[u].rearrange("a d -> (a d)"))
            sp.dma_start(mod_sb, mod_w).then_inc(sem("mod_in"), 16)
            sp.dma_start(fin_rows, fin_r.rearrange("a d -> (a d)").partition_broadcast(P)).then_inc(sem("fin_in"), 16)
            with sp.Fori(1, LAYERS // 2) as m:
                for u in range(2):
                    sp.wait_ge(sem("x_ready"), GROUPS * (2 * m + u))
                    layer(u, l1w[bass.ds(2 * m + u, 1)].rearrange("a p n -> (a p) n"),
                          l1p[bass.ds(2 * m + u, 1)].rearrange("a p n -> (a p) n"),
                          l1r[bass.ds(2 * m + u, 1)].rearrange("a b d -> (a b d)"))
            for g in range(GROUPS):
                sp.wait_ge(sem("out_ready"), g + 1)
                sp.dma_start(tiles(out, g), B["h"][:, g]).then_inc(sem("out_done"), 16)
            sp.wait_ge(sem("out_done"), 16 * GROUPS)

        @block.tensor
        def _(pe):
            def project_qk(i):
                if not isinstance(i, int) or i:
                    pe.wait_ge(sem("k_ready"), i)
                pe.matmul(bank[0][:], w0[:, W_Q:W_Q + P], cols(xt, i), start=True, stop=True)
                pe.matmul(bank[1][:], w0[:, W_K:W_K + P], cols(xt, i), start=True, stop=True).then_inc(
                    sem("qk_mm"), 1)

            def project_v(i):
                for e in range(DH):
                    pe.wait_ge(sem("kv_ready"), i * DH + (e - 1 if e > 1 else 0))
                    pe.matmul(bank[2 + e % 2][:], w0[:, W_V + P * e:W_V + P * e + P], cols(xt, i),
                              start=True, stop=True).then_inc(sem("v_mm"), 1)

            def sum_heads(i):
                pe.wait_ge(sem("prod_ready"), (i + 1) * DH)
                pe.wait_ge(sem("att_ready"), i)
                for e in (0, 2, 4, 6, 1, 3, 5, 7):
                    j = e // 2
                    mm = pe.matmul(bank[4][32 * j:32 * j + 32, :], C[:, C_SEL + 32 * e:C_SEL + 32 * e + 32],
                                   prod[:, e, :], start=(e % 2 == 0), stop=(e % 2 == 1))
                mm.then_inc(sem("att_mm"), 1)

            pe.wait_ge(sem("l0w_in"), 16)
            pe.wait_ge(sem("xt_in"), 16 * GROUPS)
            project_qk(0)
            pe.wait_ge(sem("consts_in"), 16)
            with pe.Fori(0, GROUPS - 1) as i:
                project_v(i)
                project_qk(i + 1)
                sum_heads(i)
            project_v(GROUPS - 1)
            sum_heads(GROUPS - 1)

            pe.wait_ge(sem("dk_ready"), GROUPS)
            for t in range(TILES):
                mm = pe.matmul(bank[7][:, HEADS * t:HEADS * t + HEADS],
                               dk[:, t // GT, P * (t % GT):P * (t % GT) + P], head, start=True, stop=True)
            mm.then_inc(sem("den_mm"), 1)
            for g in range(GROUPS):
                pe.wait_ge(sem("att_ready"), g + 1)
                if g >= 2:
                    pe.wait_ge(sem("an_ready"), g - 1)
                for t in range(GT):
                    mm = pe.transpose(bank[5 + g % 2][:, P * t:P * t + P], att[:, g, P * t:P * t + P], ident)
                mm.then_inc(sem("turned_att"), 1)
            for g in range(GROUPS + 1):
                if g < GROUPS:
                    pe.wait_ge(sem("an_ready"), g + 1)
                    if g >= 2:
                        pe.wait_ge(sem("ant_ready"), g - 1)
                    for t in range(GT):
                        mm = pe.transpose(bank[3 + g % 2][:, P * t:P * t + P], T["an"][:, g, P * t:P * t + P], ident)
                    mm.then_inc(sem("turned_an"), 1)
                if g:
                    h = g - 1
                    pe.wait_ge(sem("ant_ready"), h + 1)
                    if h >= 2:
                        pe.wait_ge(sem("xs_ready"), h - 1)
                    for t in range(GT):
                        mm = pe.matmul(bank[h % 2][:, P * t:P * t + P], T["ant"][:, h, P * t:P * t + P],
                                       w0[:, W_O:W_O + P], start=True, stop=True)
                    mm.then_inc(sem("wo_mm"), 1)
            pe.wait_ge(sem("sw_in"), 16)
            for g in range(GROUPS + 1):
                if g < GROUPS:
                    pe.wait_ge(sem("x1_ready"), g + 1)
                    if g >= 2:
                        pe.wait_ge(sem("x1t_ready"), g - 1)
                    for t in range(GT):
                        mm = pe.transpose(bank[5 + g % 2][:, P * t:P * t + P], x1[:, GT * g + t, :], ident)
                    mm.then_inc(sem("turned_x1"), 1)
                if g:
                    h = g - 1
                    pe.wait_ge(sem("x1t_ready"), h + 1)
                    if h >= 2:
                        pe.wait_ge(sem("logits_ready"), h - 1)
                    for t in range(GT):
                        mm = pe.matmul(bank[3 + h % 2][:, NE * t:NE * t + NE],
                                       x1t[:, GROUP * h + P * t:GROUP * h + P * t + P], sw[:, 0:NE],
                                       start=True, stop=True)
                    mm.then_inc(sem("logits_mm"), 1)

            wg, sw1, sw2 = sw[:, 0:NE], sw[:, NE:NE + 2 * FFN], sw[:, NE + 2 * FFN:].rearrange("p (f d) -> p f d", d=D)

            def shared_expert(g):
                for f in range(FB):
                    pe.wait_ge(sem("hidden_read"), g * FB + (1 if f == FB - 1 else 0))
                    pe.matmul(bank[2 + 2 * f][:], sw1[:, P * (FB + f):P * (FB + f) + P], cols(x1t, g),
                              start=True, stop=True)
                    pe.matmul(bank[3 + 2 * f][:], sw1[:, P * f:P * f + P], cols(x1t, g),
                              start=True, stop=True).then_inc(sem("hidden_mm"), 1)
                pe.wait_ge(sem("hidden_ready"), (g + 1) * FB)
                pe.wait_ge(sem("shared_ready"), g)
                for t in range(GT):
                    for f in range(FB):
                        mm = pe.matmul(bank[0][:, P * t:P * t + P], hidden[:, 2 * FB + f, P * t:P * t + P], sw2[:, f, :],
                                       start=(f == 0), stop=(f == FB - 1))
                mm.then_inc(sem("shared_mm"), 1)

            pe.wait_ge(sem("logits_ready"), GROUPS)
            pe.wait_ge(sem("x1t_ready"), GROUPS)
            with pe.Fori(0, 2) as g:
                shared_expert(g)
            pe.wait_ge(sem("masks_ready"), 1)
            pe.wait_ge(sem("shared_ready"), 2)
            for h in range(2):
                pe.matmul(bank[h][:], ones16[:], R["upto_ei"].rearrange("p (e i) -> p i e", i=TILES)[:, 8 * h:8 * h + 8, :],
                          start=True, stop=False)
                mm = pe.matmul(bank[h][:], tri16[:], R["mask"][:, 512 * h:512 * h + 512], start=False, stop=True)
            mm.then_inc(sem("rank_mm"), 1)
            pe.wait_ge(sem("rank_read"), 1)
            with pe.Fori(2, GROUPS) as g:
                shared_expert(g)
            a16 = R["a"].rearrange("p i (g n) -> p i g n", n=RA * EG)
            b16 = R["b"].rearrange("p b (i e) -> p b i e", e=NE)
            pe.wait_ge(sem("hidden_read"), GROUPS * FB)
            pe.wait_ge(sem("one_hots_ready"), 1)
            with pe.Fori(0, NEG // 2) as it:
                for u in range(2):
                    pe.wait_ge(sem("slots_read"), 2 * it)
                    for i in range(TILES):
                        lhs = a16[:, i, bass.ds(2 * it + u, 1), :].rearrange("p g n -> p (g n)")
                        mm = pe.matmul(bank[2 + u][:, 0:2 * RB * EG], lhs, b16[:, :, i, bass.ds(EG * (2 * it + u), EG)],
                                       start=(i == 0), stop=(i == TILES - 1))
                    mm.then_inc(sem("slots_mm"), 1)

            def turn_inputs(G, u, m):
                pe.wait_ge(sem(f"gathered{u}"), 16 * RB * (m + 1))
                for c in range(3):
                    if c < 2:
                        if not isinstance(G, int) or G:
                            pe.wait_ge(sem("turned_y_read"), 3 * (G - 1))
                    else:
                        pe.wait_ge(sem("xt_ready"), 3 * G + 1)
                    for b in range(4 * c, min(4 * c + 4, RB)):
                        mm = pe.transpose(bank[7 - c % 2][:, P * (b % 4):P * (b % 4) + P], E["got"][:, u, b, 0:D], ident)
                    mm.then_inc(sem("turned_x"), 1)

            def turn_results(G, u, more):
                for c in range(3):
                    if c < 2:
                        if more:
                            pe.wait_ge(sem("xt_ready"), 3 * G + 5 + c)
                        else:
                            pe.wait_ge(sem("turned_y_read"), 3 * G)
                    else:
                        pe.wait_ge(sem("turned_y_read"), 3 * G + 1)
                    for b in range(4 * c, min(4 * c + 4, RB)):
                        mm = pe.transpose(bank[6 + c % 2][:, P * (b % 4):P * (b % 4) + P], E["yt"][:, u, b, :], ident)
                    mm.then_inc(sem("turned_y"), 1)

            def expert_hidden(G, u, j):
                n = G * EG + j
                pe.wait_ge(sem(f"expert_in{j}"), 16 * (G + 1))
                pe.wait_ge(sem("prod_g_ready"), n - 1 if j > 1 else G * EG)
                for part in (1, 0):
                    for f in range(FB):
                        mm = pe.matmul(bank[2 * (j % 2) + part][:, CAP * f:CAP * f + CAP],
                                       ring[:, j, P * (FB * part + f):P * (FB * part + f) + P], E["xt"][:, u, j, :],
                                       start=True, stop=True)
                    mm.then_inc(sem("gate_mm" if part else "value_mm"), 1)

            def expert_result(G, u, j):
                n = G * EG + j
                pe.wait_ge(sem("prod_g_ready"), n + 1)
                pe.wait_ge(sem("yt_ready"), n - 1 if j > 1 else G * EG)
                for f in range(FB):
                    mm = pe.matmul(bank[4 + j % 2][:, 0:CAP], ring[:, j, P * (2 * FB + f):P * (2 * FB + f) + P],
                                   E["prod"][:, j % 2, CAP * f:CAP * f + CAP], start=(f == 0), stop=(f == FB - 1))
                mm.then_inc(sem("y_mm"), 1)

            def expert_group(G, u, m, more):
                pe.wait_ge(sem("xt_ready"), 3 * (G + 1))
                for j in range(EG):
                    expert_hidden(G, u, j)
                    if j:
                        expert_result(G, u, j - 1)
                if more:
                    turn_inputs(G + 1, 1 - u, m + u)
                expert_result(G, u, EG - 1)
                pe.wait_ge(sem("yt_ready"), (G + 1) * EG)
                turn_results(G, u, more)

            turn_inputs(0, 0, 0)
            pe.wait_ge(sem("shared_ready"), GROUPS)
            pe.wait_ge(sem("slots_read"), NEG)
            with pe.Fori(0, NEG // 2 - 1) as m:
                for u in range(2):
                    expert_group(2 * m + u, u, m, True)
            expert_group(NEG - 2, 0, NEG // 2 - 1, True)
            expert_group(NEG - 1, 1, NEG // 2 - 1, False)

            def turn(src, b, done):
                for t in range(GT):
                    mm = pe.transpose(bank[b][:, P * t:P * t + P], src[:, t, :], ident)
                mm.then_inc(sem(done), 1)

            def encoder_layer(l, u):
                w = lw[u]
                wq, wkv, wo, w1, w2 = w[:, 0:P], w[:, P:3 * P], w[:, 3 * P:4 * P], w[:, 4 * P:8 * P], w[:, 8 * P:]
                L = GROUPS * l

                def turn_norm1(g):
                    pe.wait_ge(sem("h1_ready"), L + g + 1)
                    if g >= 2:
                        pe.wait_ge(sem("ht_ready"), L + g - 1)
                    else:
                        pe.wait_ge(sem("h2t_ready"), L)
                    turn(B["h"][:, g], g % 2, "turned1")

                def project(g):
                    pe.wait_ge(sem("ht_ready"), L + g + 1)
                    if g:
                        pe.wait_ge(sem("q1_ready"), L + g)
                    else:
                        pe.wait_ge(sem("x_ready"), L + 3)
                    pe.matmul(bank[2][:], wq, B["ht"][:, g], start=True, stop=True).then_inc(sem("q1_mm"), 1)
                    for h in range(2):
                        if g:
                            pe.wait_ge(sem("z_ready"), 2 * (L + g - 1) + h + 1)
                        else:
                            pe.wait_ge(sem("relu_ready"), FFB * L)
                        for t in range(2):
                            mm = pe.matmul(bank[3 + h][:, 2 * D * t:2 * D * t + 2 * D],
                                           B["ht"][:, g, P * (2 * h + t):P * (2 * h + t) + P], wkv, start=True, stop=True)
                        mm.then_inc(sem("kv1_mm"), 1)

                def sum_kv(g):
                    pe.wait_ge(sem("kp_ready"), L + g + 1)
                    if g:
                        pe.wait_ge(sem("kvm_ready"), L + g)
                    else:
                        pe.wait_ge(sem("x_ready"), L + 4)
                    for t in range(GT):
                        mm = pe.matmul(bank[5][:, (D + 1) * (t // 2):(D + 1) * (t // 2 + 1)], B["kp"][:, g, t, :],
                                       zrow(g)[:, t, D:Z], start=(t % 2 == 0), stop=(t % 2 == 1))
                    mm.then_inc(sem("kvsum_mm"), 1)

                def attend(g):
                    pe.wait_ge(sem("kvm_ready"), L + g + 1)
                    if g:
                        pe.wait_ge(sem("an1_ready"), L + g)
                    else:
                        pe.wait_ge(sem("relu_ready"), FFB * L)
                    for t in range(GT):
                        mm = pe.matmul(bank[6 + t // 2][:, (D + HEADS) * (t % 2):(D + HEADS) * (t % 2 + 1)],
                                       B["q"][:, g, P * t:P * t + P], kvm(g)[:, t // 2, :], start=True, stop=True)
                    mm.then_inc(sem("num_mm"), 1)

                def turn_attention(g):
                    pe.wait_ge(sem("an1_ready"), L + g + 1)
                    if g >= 2:
                        pe.wait_ge(sem("at_ready"), L + g - 1)
                    else:
                        pe.wait_ge(sem("ht_ready"), L + 3 + g)
                    turn(B["h"][:, g], g % 2, "turned2")

                def output(g):
                    pe.wait_ge(sem("at_ready"), L + g + 1)
                    if g >= 2:
                        pe.wait_ge(sem("mid_ready"), L + g - 1)
                    else:
                        pe.wait_ge(sem("kvm_ready" if g else "q1_ready"), L + 4)
                    for t in range(GT):
                        mm = pe.matmul(bank[5 if g % 2 else 2][:, P * t:P * t + P], B["ht"][:, g, P * t:P * t + P], wo,
                                       start=True, stop=True)
                    mm.then_inc(sem("out1_mm"), 1)

                def turn_norm2(g):
                    pe.wait_ge(sem("h2_ready"), L + g + 1)
                    if g >= 2:
                        pe.wait_ge(sem("h2t_ready"), L + g - 1)
                    else:
                        pe.wait_ge(sem("at_ready"), L + 3 + g)
                    turn(B["h"][:, g], g % 2, "turned3")

                def up(g):
                    pe.wait_ge(sem("h2t_ready"), L + g + 1)
                    for f in range(FFB):
                        if g:
                            pe.wait_ge(sem("relu_ready"), FFB * (L + g - 1) + f + 1)
                        else:
                            if f < 2:
                                pe.wait_ge(sem("z_ready"), 2 * L + 7 + f)
                            else:
                                pe.wait_ge(sem("an1_ready"), L + 4)
                        pe.matmul(bank[(3, 4, 6, 7)[f]][:], w1[:, P * f:P * f + P], B["ht"][:, g], start=True,
                                  stop=True).then_inc(sem("up_mm"), 1)

                def down(g):
                    pe.wait_ge(sem("relu_ready"), FFB * (L + g + 1))
                    if g >= 2:
                        pe.wait_ge(sem("x_ready"), L + 4 + g - 1)
                    else:
                        pe.wait_ge(sem("mid_ready"), L + 3 + g)
                    for t in range(GT):
                        for f in range(FFB):
                            mm = pe.matmul(bank[5 if g % 2 else 2][:, P * t:P * t + P],
                                           B["relu"][:, g % 2, f, P * t:P * t + P], w2[:, P * f:P * f + P],
                                           start=(f == 0), stop=(f == FFB - 1))
                    mm.then_inc(sem("down_mm"), 1)

                staggered([turn_norm1, project])
                staggered([sum_kv, attend])
                staggered([turn_attention, output])
                staggered([turn_norm2, up, down])

            with pe.Fori(0, LAYERS // 2) as m:
                for u in range(2):
                    pe.wait_ge(sem(f"layer_in{u}"), 48 * (m + 1))
                    encoder_layer(2 * m + u, u)

            L = GROUPS * LAYERS
            pe.wait_ge(sem("mod_in"), 16)

            def turn_x3(g):
                pe.wait_ge(sem("x3_ready"), g + 1)
                if g >= 2:
                    pe.wait_ge(sem("x3t_ready"), g - 1)
                else:
                    pe.wait_ge(sem("h2t_ready"), L)
                turn(state[:, GT * g:GT * g + GT], g % 2, "turned_x3")

            def score(g):
                pe.wait_ge(sem("x3t_ready"), g + 1)
                if g >= 2:
                    pe.wait_ge(sem("scores_ready"), g - 1)
                else:
                    pe.wait_ge(sem("x_ready"), L + 4)
                pe.matmul(bank[5 if g % 2 else 2][:], mod_sb[:, 0:P], B["ht"][:, g], start=True, stop=True).then_inc(
                    sem("score_mm"), 1)
                if g >= 2:
                    pe.wait_ge(sem("gelu_ready"), g - 1)
                else:
                    pe.wait_ge(sem("relu_ready"), FFB * L)
                for t in range(GT):
                    mm = pe.matmul(bank[3 + g % 2][:, P * t:P * t + P], B["ht"][:, g, P * t:P * t + P], mod_sb[:, P:2 * P],
                                   start=True, stop=True)
                mm.then_inc(sem("block_mm"), 1)

            staggered([turn_x3, score])

        @block.scalar
        def _(act):
            def exps(i):
                if not isinstance(i, int) or i:
                    act.wait_ge(sem("k_ready"), i)
                act.wait_ge(sem("qk_mm"), i + 1)
                act.activation(eqk[:, 0, :], bank[0][:], ACT.Exp, bias=l0ps[:, 0:1])
                act.activation(eqk[:, 1, :], bank[1][:], ACT.Exp, bias=l0ps[:, 1:2]).then_inc(sem("exp_ready"), 1)

            def keep_att(i):
                act.wait_ge(sem("att_mm"), i + 1)
                act.activation(att[:, bass.ds(i, 1), :].rearrange("p a n -> p (a n)"), bank[4][:],
                               ACT.Copy).then_inc(sem("att_ready"), 1)

            act.wait_ge(sem("l0p_in"), 16)
            exps(0)
            with act.Fori(0, GROUPS - 1) as i:
                exps(i + 1)
                keep_att(i)
            keep_att(GROUPS - 1)
            for g in range(GROUPS):
                act.wait_ge(sem("turned_an"), g + 1)
                act.activation(T["ant"][:, g, :], bank[3 + g % 2][:], ACT.Copy).then_inc(sem("ant_ready"), 1)
            for g in range(GROUPS + 1):
                if g < GROUPS:
                    act.wait_ge(sem("turned_x1"), g + 1)
                    act.activation(cols(x1t, g), bank[5 + g % 2][:], ACT.Copy).then_inc(sem("x1t_ready"), 1)
                if g:
                    act.wait_ge(sem("logits_mm"), g)
                    act.activation(tiles(logits, g - 1), bank3(3 + (g - 1) % 2, NE), ACT.Copy).then_inc(
                        sem("logits_ready"), 1)
            act.wait_ge(sem("shifted_ready"), 1)
            act.activation(gates[:], gates[:], ACT.Exp).then_inc(sem("gates_exp"), 1)

            def shared_halves(g):
                for f in range(FB):
                    act.wait_ge(sem("hidden_mm"), g * FB + f + 1)
                    act.wait_ge(sem("hidden_ready"), g * FB)
                    act.activation(hidden[:, FB + f, :], bank[2 + 2 * f][:], ACT.Silu)
                    act.activation(hidden[:, f, :], bank[3 + 2 * f][:], ACT.Copy).then_inc(sem("hidden_read"), 1)

            def keep_shared(g):
                act.wait_ge(sem("shared_mm"), g + 1)
                act.activation(tiles_at(shared, g), bank3(0), ACT.Copy).then_inc(sem("shared_ready"), 1)

            with act.Fori(0, 2) as g:
                shared_halves(g)
                keep_shared(g)
            act.wait_ge(sem("b_index"), 1)
            act.activation(R["bi"], logits_i, ACT.Copy).then_inc(sem("bi_ready"), 1)
            with act.Fori(2, GROUPS) as g:
                shared_halves(g)
                keep_shared(g)

            def silu_of(G, u, j):
                n = G * EG + j
                act.wait_ge(sem("gate_mm"), n + 1)
                act.wait_ge(sem("prod_g_ready"), n - 1 if j > 1 else G * EG)
                act.activation(E["silu"][:, j % 2, :], bank[2 * (j % 2) + 1][:, 0:FB * CAP], ACT.Silu).then_inc(
                    sem("silu_ready"), 1)

            def keep_result(G, u, j):
                act.wait_ge(sem("y_mm"), G * EG + j + 1)
                if j == 0 and not (isinstance(G, int) and G < 2):
                    act.wait_ge(sem("turned_y"), 3 * (G - 1))
                act.activation(E["yt"][:, u].rearrange("p b (a e) -> p b a e", e=EG)[:, :, :, j],
                               bank[4 + j % 2][:, 0:CAP].rearrange("p (b a) -> p b a", a=RA), ACT.Copy).then_inc(
                    sem("yt_ready"), 1)

            def expert_group(G, u):
                for j in range(EG):
                    silu_of(G, u, j)
                    if j:
                        keep_result(G, u, j - 1)
                keep_result(G, u, EG - 1)

            expert_group(0, 0)
            expert_group(1, 1)
            with act.Fori(1, NEG // 2) as m:
                for u in range(2):
                    expert_group(2 * m + u, u)

            def encoder_layer(l, u):
                L = GROUPS * l
                col = lambda k: layer_cols[:, u, k:k + 1]

                def norm1_columns(g):
                    act.wait_ge(sem("turned1"), L + g + 1)
                    act.activation(B["ht"][:, g], bank[g % 2][:], ACT.Identity, bias=col(2), scale=col(1)).then_inc(
                        sem("ht_ready"), 1)

                def exp_q(g):
                    act.wait_ge(sem("q1_mm"), L + g + 1)
                    act.wait_ge(sem("q1_ready"), L + g - 1 if g >= 2 else L)
                    act.activation(B["eq"][:, g % 2], bank[2][:], ACT.Exp, bias=col(0)).then_inc(sem("eq_ready"), 1)

                def exp_k(g):
                    act.wait_ge(sem("z_ready"), 2 * (L + g + 1))
                    act.wait_ge(sem("kp_ready"), L + g - 1 if g >= 2 else L)
                    act.activation(B["ek"][:, g % 2], zrow(g)[:, :, 0:D], ACT.Exp, bias=minus_one[:]).then_inc(
                        sem("ek_ready"), 1)

                def attention_columns(g):
                    act.wait_ge(sem("turned2"), L + g + 1)
                    act.activation(B["ht"][:, g], bank[g % 2][:], ACT.Copy).then_inc(sem("at_ready"), 1)

                def norm2_columns(g):
                    act.wait_ge(sem("turned3"), L + g + 1)
                    act.activation(B["ht"][:, g], bank[g % 2][:], ACT.Identity, bias=col(4), scale=col(3)).then_inc(
                        sem("h2t_ready"), 1)

                def relus(g):
                    act.wait_ge(sem("down_mm"), L + g - 1 if g >= 2 else L)
                    for f in range(FFB):
                        act.wait_ge(sem("up_mm"), FFB * (L + g) + f + 1)
                        act.activation(B["relu"][:, g % 2, f], bank[(3, 4, 6, 7)[f]][:], ACT.Relu,
                                       bias=col(5 + f)).then_inc(sem("relu_ready"), 1)

                staggered([norm1_columns, exp_q, exp_k])
                staggered([attention_columns])
                staggered([norm2_columns, relus])

            with act.Fori(0, LAYERS // 2) as m:
                for u in range(2):
                    act.wait_ge(sem(f"layer_in{u}"), 48 * (m + 1))
                    encoder_layer(2 * m + u, u)

            def x3_columns(g):
                act.wait_ge(sem("turned_x3"), g + 1)
                act.activation(B["ht"][:, g], bank[g % 2][:], ACT.Copy).then_inc(sem("x3t_ready"), 1)

            def keep_scores(g):
                if g >= 2:
                    act.wait_ge(sem("chosen"), g - 1)
                act.wait_ge(sem("score_mm"), g + 1)
                act.activation(scores[:, g % 2], bank[5 if g % 2 else 2][:], ACT.Copy).then_inc(sem("scores_ready"), 1)
                act.activation(B["kp"][:, g], tiles(state, g), ACT.Copy, scale=2.0).then_inc(sem("twice_ready"), 1)

            def gelus(g):
                act.wait_ge(sem("block_mm"), g + 1)
                act.activation(B["q"][:, g].rearrange("p (i d) -> p i d", d=D), bank3(3 + g % 2),
                               ACT.Gelu_apprx_tanh).then_inc(sem("gelu_ready"), 1)

            staggered([x3_columns, keep_scores, gelus])

        @block.gpsimd
        def _(pool):
            pool.memset(zeros[:], 0.0).then_inc(sem("zeros_ready"), 1)
            pool.memset(new_tile[:], 1.0).then_inc(sem("pool_consts"), 1)
            pool.memset(new_token[:], 1.0).then_inc(sem("pool_consts"), 1)
            pool.wait_ge(sem("pool_consts"), 2)
            pool.memset(new_tile[:].rearrange("p (e i) -> p e i", i=TILES)[:, :, 0:1], 0.0)
            pool.memset(new_token[:].rearrange("p (i e) -> p i e", e=NE)[:, :, 0:1], 0.0).then_inc(
                sem("starts_ready"), 1)
            pool.memset(minus_half[:], -0.5).then_inc(sem("pool_consts"), 1)
            pool.memset(minus_one[:], -1.0).then_inc(sem("minus_one_ready"), 1)
            pool.wait_ge(sem("pool_consts"), 3)
            pool.wait_ge(sem("xr_in"), 16)
            pool.wait_ge(sem("bo_in"), 16)
            with pool.Fori(0, GROUPS) as i:
                for e in range(DH):
                    pool.wait_ge(sem("run_ready"), i * DH + e + 1)
                    if e == 0:
                        pool.wait_ge(sem("att_mm"), i)
                    pool.tensor_tensor(prod[:, e, :], run[:, e % 2, :], q0, ALU.mult).then_inc(
                        sem("prod_ready"), 1)
            for g in range(GROUPS):
                pool.tensor_tensor(tiles(xr, g), tiles(xr, g), bo_bc[:].unsqueeze(1).to_broadcast([P, GT, D]),
                                   ALU.add).then_inc(sem("xr_ready"), 1)
            for g in range(GROUPS):
                norm_rstd(pool, g, g)

            def shared_products(g):
                for f in range(FB):
                    pool.wait_ge(sem("hidden_read"), g * FB + f + 1)
                    pool.wait_ge(sem("shared_mm"), g)
                    pool.tensor_tensor(hidden[:, 2 * FB + f, :], hidden[:, f, :], hidden[:, FB + f, :],
                                       ALU.mult).then_inc(sem("hidden_ready"), 1)

            shared_products(0)
            pool.wait_ge(sem("masks_ready"), 1)
            pool.tensor_tensor(gates[:].rearrange("p i e -> p (i e)"), gates[:].rearrange("p i e -> p (i e)"),
                               R["mask"], ALU.mult).then_inc(sem("gates_masked"), 1)
            pool.wait_ge(sem("gates_masked"), 1)
            pool.wait_ge(sem("top_sum_ready"), 1)
            pool.tensor_tensor(gates[:], gates[:], route[:, 80:96].unsqueeze(2).to_broadcast([P, TILES, NE]),
                               ALU.mult).then_inc(sem("gates_ready"), 1)
            with pool.Fori(1, GROUPS) as g:
                shared_products(g)

            def gather(G, u):
                if not (isinstance(G, int) and G < 2):
                    pool.wait_ge(sem("slot_gate_ready"), G - 1)
                pool.wait_ge(sem("indices_ready"), 1)
                pool.tensor_copy(gather_ix[:, u:u + 1, :], gather_all[:, bass.ds(G, 1), :]).then_inc(
                    sem("gather_ix_ready"), 1)
                pool.wait_ge(sem("gather_ix_ready"), G + 1)
                pool.sem_inc(sem("gather_begun"))
                pool.wait_ge(sem("rows_out"), 32)
                for b in range(RB):
                    pool.indirect_dma_start(E["got"][:, u, b, :], None, dispatch_dram[:, :],
                                            bass.IndirectOffsetOnAxis(ap=gather_ix[:, u, b:b + 1], axis=0)).then_inc(
                        sem(f"gathered{u}"), 16)

            def scatter(G, u, m):
                if not isinstance(m, int) or m:
                    pool.wait_ge(sem(f"scattered{u}"), 16 * RB * m)
                pool.tensor_copy(scatter_ix[:, u:u + 1, :], scatter_all[:, bass.ds(G, 1), :]).then_inc(
                    sem("scatter_ix_ready"), 1)
                pool.wait_ge(sem("scatter_ix_ready"), G + 1)
                pool.wait_ge(sem("turned_y_read"), 3 * (G + 1))
                pool.sem_inc(sem("scatter_begun"))
                pool.wait_ge(sem("zeroed"), 16 * TOK * TOPK // (8 * P))
                for b in range(RB):
                    pool.indirect_dma_start(returned_dram[:, :],
                                            bass.IndirectOffsetOnAxis(ap=scatter_ix[:, u, b:b + 1], axis=0),
                                            E["back"][:, u, b, :], None, bounds_check=TOK * TOPK - 1,
                                            oob_is_err=False).then_inc(sem(f"scattered{u}"), 16)

            gather(0, 0)
            gather(1, 1)
            with pool.Fori(0, NEG // 2 - 1) as m:
                for u in range(2):
                    gather(2 * m + u + 2, u)
                    scatter(2 * m + u, u, m)
            scatter(NEG - 2, 0, NEG // 2 - 1)
            for g in range(GROUPS):
                pool.wait_ge(sem("shared_ready"), GROUPS)
                pool.tensor_tensor(tiles(shared, g), tiles(shared, g), tiles(x1, g), ALU.add).then_inc(
                    sem("base_ready"), 1)
            scatter(NEG - 1, 1, NEG // 2 - 1)

            for g in range(GROUPS):
                norm_rstd(pool, NORM_COMBINE + g, g)

            def row_of(u, k):
                return lrows[u][:, D * k:D * k + D].unsqueeze(1).to_broadcast([P, GT, D])

            def encoder_layer(l, u):
                L = GROUPS * l
                for g in range(GROUPS):
                    norm_rstd(pool, NORM_LAYERS + 2 * L + g, g)
                    pool.wait_ge(sem("x_ready"), L + g + 1)
                    pool.tensor_tensor(tiles(plus, g), tiles(state, g), row_of(u, 2), ALU.add).then_inc(
                        sem("plus_bo"), 1)
                for g in range(GROUPS):
                    norm_rstd(pool, NORM_LAYERS + 2 * L + GROUPS + g, g)
                    pool.wait_ge(sem("mid_ready"), L + g + 1)
                    pool.tensor_tensor(tiles(plus, g), tiles(state, g), row_of(u, 3), ALU.add).then_inc(
                        sem("plus_b2"), 1)

            with pool.Fori(0, LAYERS // 2) as m:
                for u in range(2):
                    pool.wait_ge(sem(f"layer_in{u}"), 48 * (m + 1))
                    encoder_layer(2 * m + u, u)
            pool.wait_ge(sem("fin_in"), 16)
            for g in range(GROUPS):
                pool.wait_ge(sem("x_ready"), GROUPS * LAYERS + g + 1)
                norm_rstd(pool, NORM_FINAL + g, g)
                pool.tensor_tensor(tiles(plus, g), tiles(x2, g),
                                   fin_rows[:, D:2 * D].unsqueeze(1).to_broadcast([P, GT, D]), ALU.add).then_inc(
                    sem("plus_lnf"), 1)
            for g in range(2 * GROUPS):
                norm_rstd(pool, NORM_FINAL + GROUPS + g, g)

        @block.vector
        def _(v):
            ch = Chain(v, sem("vector_step"))
            v.wait_ge(sem("l0p_in"), 16)
            v.tensor_scalar(bq1[:], l0ps[:, 0:2], 1.0, None, ALU.add).then_inc(sem("bq1_ready"), 1)
            v.wait_ge(sem("bq1_ready"), 1)
            v.wait_ge(sem("consts_in"), 16)
            v.tensor_copy(tri16[:], C[:, C_TRI:C_TRI + P]).then_inc(sem("tri_ready"), 1)
            v.tensor_copy(ones16[:], C[:, C_ONES:C_ONES + P]).then_inc(sem("tri_ready"), 1)
            with v.Fori(0, GROUPS) as i:
                ch.loop(i, 2)
                v.wait_ge(sem("exp_ready"), i + 1)
                e1 = ch.did(v.tensor_scalar(eqk[:], eqk[:], 1.0, None, ALU.min))
                ch.after(e1)
                v.wait_ge(sem("prod_ready"), i * DH)
                v.scalar_tensor_tensor(q0, bank[0][:], bq1[:, 0:1], eqk[:, 0, :], ALU.add, ALU.max).then_inc(
                    sem("q_ready"), 1)
                v.scalar_tensor_tensor(k0, bank[1][:], bq1[:, 1:2], eqk[:, 1, :], ALU.add, ALU.max).then_inc(
                    sem("k_ready"), 1)
                v.wait_ge(sem("k_ready"), i + 1)
                s1 = ch.did(v.tensor_tensor_scan(ksum, reset, k0, 0.0, ALU.mult, ALU.add))
                ch.after(s1)
                v.tensor_tensor(dk[:, bass.ds(i, 1), :].rearrange("p a n -> p (a n)"), ksum, q0,
                                ALU.mult).then_inc(sem("dk_ready"), 1)

                def kv_of(e):
                    v.wait_ge(sem("v_mm"), i * DH + e + 1)
                    v.wait_ge(sem("run_ready"), i * DH + (e - 1 if e > 1 else 0))
                    v.scalar_tensor_tensor(kv[:, e % 2, :], bank[2 + e % 2][:], l0ps[:, 2 + e:3 + e], k0,
                                           ALU.add, ALU.mult).then_inc(sem("kv_ready"), 1)

                kv_of(0)
                for e in range(DH):
                    if e + 1 < DH:
                        kv_of(e + 1)
                    v.wait_ge(sem("kv_ready"), i * DH + e + 1)
                    v.wait_ge(sem("prod_ready"), i * DH + (e - 1 if e > 1 else 0))
                    v.tensor_tensor_scan(run[:, e % 2, :], reset, kv[:, e % 2, :], 0.0, ALU.mult,
                                         ALU.add).then_inc(sem("run_ready"), 1)
            ch.end_loop(GROUPS)
            v.wait_ge(sem("den_mm"), 1)
            d = ch.did(v.tensor_scalar(den, bank[7][:, 0:TILES * HEADS].rearrange("p (g n) -> p g n", g=GROUPS),
                                       EPS_ATTN, None, ALU.max))
            ch.after(d)
            d = ch.did(v.reciprocal(rden, den))
            ch.after(d)
            for g in range(GROUPS):
                v.wait_ge(sem("turned_att"), g + 1)
                r = rden[:, g, :].rearrange("p (i h) -> p i h", h=HEADS).unsqueeze(2).to_broadcast([P, GT, DH, HEADS])
                if g == 0:
                    v.wait_ge(sem("att_mm"), GROUPS)
                v.tensor_tensor(T["an"][:, g, :].rearrange("p (i e h) -> p i e h", e=DH, h=HEADS),
                                bank[5 + g % 2][:].rearrange("p (i e h) -> p i e h", e=DH, h=HEADS), r,
                                ALU.mult).then_inc(sem("an_ready"), 1)
            xs = T["xs"].rearrange("p g (i d) -> p g i d", d=D)
            for g in range(GROUPS + 1):
                if g < GROUPS:
                    v.wait_ge(sem("wo_mm"), g + 1)
                    v.wait_ge(sem("xr_ready"), g + 1)
                    v.tensor_tensor(xs[:, g], bank3(g % 2), tiles(xr, g), ALU.add).then_inc(sem("xs_ready"), 1)
                    v.wait_ge(sem("xs_ready"), g + 1)
                    norm_stats(v, ch, g, xs[:, g])
                if g:
                    norm_apply(v, g - 1, g - 1, xs[:, g - 1], tiles(x1, g - 1), "x1_ready")

            top, total, inv, top8 = route[:, 0:16], route[:, 16:32], route[:, 32:48], route[:, 48:64]
            over = lambda a: a.unsqueeze(2).to_broadcast([P, TILES, NE])
            v.wait_ge(sem("logits_ready"), GROUPS)
            ch.after(ch.did(v.tensor_reduce(top, logits[:], AX.X, ALU.max)))
            v.tensor_tensor(gates[:], logits[:], over(top), ALU.subtract).then_inc(sem("shifted_ready"), 1)
            v.wait_ge(sem("gates_exp"), 1)
            ch.after(ch.did(v.tensor_reduce(total, gates[:], AX.X, ALU.add)))
            ch.after(ch.did(v.reciprocal(inv, total)))
            ch.after(ch.did(v.tensor_tensor(gates[:], gates[:], over(inv), ALU.mult)))
            for i in range(TILES):
                k = ch.did(v.max(best8[:, i, :], gates[:, i, :]))
            ch.after(k)
            for i in range(TILES):
                k = ch.did(v.match_replace(logits[:, i, :], best8[:, i, :], gates[:, i, :], -1.0))
            ch.after(k)
            lg = logits[:].rearrange("p i e -> p (i e)")
            mask, mask_ei = R["mask"], R["mask_ei"]
            v.tensor_scalar(mask, lg, 0.0, None, ALU.is_lt).then_inc(sem("mask_parts"), 1)
            v.tensor_scalar(mask_ei.rearrange("p (e i) -> p i e", i=TILES), logits[:], 0.0, None, ALU.is_lt).then_inc(
                sem("mask_parts"), 1)
            ch.after(ch.did(v.tensor_reduce(top8, best8[:], AX.X, ALU.add)))
            v.wait_ge(sem("starts_ready"), 1)
            v.tensor_tensor_scan(R["upto_ei"], new_tile[:], mask_ei, 0.0, ALU.mult, ALU.add).then_inc(
                sem("masks_ready"), 1)
            ch.after(ch.did(v.tensor_scalar(route[:, 64:80], top8, float(np.finfo(np.float32).eps), None, ALU.max)))
            v.reciprocal(route[:, 80:96], route[:, 64:80]).then_inc(sem("top_sum_ready"), 1)
            v.tensor_tensor_scan(R["place"], new_token[:], mask, 0.0, ALU.mult, ALU.add)
            k = ch.did(v.tensor_copy(R["token"].rearrange("p (i e) -> p i e", e=NE), over(C[:, C_TOK:C_TOK + TILES])))
            v.wait_ge(sem("rank_mm"), 1)
            v.wait_ge(sem("zeroed"), 16 * TOK * TOPK // (8 * P))
            for h in range(2):
                hs = slice(512 * h, 512 * h + 512)
                ins = v.scalar_tensor_tensor(scratch[:, hs], bank[h][:], 1.0, mask[:, hs], ALU.add, ALU.mult)
            ins.then_inc(sem("rank_read"), 1)
            v.wait_ge(sem("rank_read"), 1)
            scr_i = scratch[:].bitcast(I32)
            ch.after(ch.did(v.tensor_scalar(logits_i, scratch[:], -1.0, None, ALU.add)))
            k1 = ch.did(v.tensor_scalar(scr_i, logits_i, RA - 1, None, ALU.bitwise_and))
            ch.after(k1)
            v.tensor_scalar(logits_i, logits_i, 4, None, ALU.arith_shift_right).then_inc(sem("b_index"), 1)
            ch.after(ch.did(v.tensor_copy(R["ai"], scr_i)))
            for a in range(RA):
                v.tensor_scalar(R["a"].rearrange("p i (g a e) -> p (i g) a e", a=RA, e=EG)[:, :, a, :],
                                R["ai"].rearrange("p (n e) -> p n e", e=EG), float(a), None, ALU.is_equal)
            v.wait_ge(sem("bi_ready"), 1)
            for b in range(RB):
                ch.after(ch.did(v.tensor_scalar(R["here"], R["bi"], float(b), None, ALU.is_equal)))
                v.tensor_tensor(R["b"][:, b, :], R["here"], R["token"], ALU.mult)
                ins = v.tensor_tensor(R["b"][:, RB + b, :], R["here"], R["place"], ALU.mult)
                if b + 1 < RB:
                    ch.after(ch.did(ins))
            ins.then_inc(sem("one_hots_ready"), 1)
            own = C[:, C_EXP:C_EXP + EG]
            v.wait_ge(sem("one_hots_ready"), 1)
            with v.Fori(0, NEG // 2) as it:
                ch.loop(it, 2)
                for u in range(2):
                    v.wait_ge(sem("slots_mm"), 2 * it + u + 1)
                    if u == 0:
                        v.wait_ge(sem("vector_step"), ch.off + ch.n)
                    v.tensor_tensor(picked[:, u], bank[2 + u][:, 0:2 * RB * EG].rearrange("p (b e) -> p b e", e=EG),
                                    own.unsqueeze(1).to_broadcast([P, 2 * RB, EG]), ALU.mult).then_inc(
                        sem("slots_read"), 1)
                    v.wait_ge(sem("slots_read"), 2 * it + u + 1)
                    ch.did(v.tensor_reduce(slots[:, bass.ds(2 * it + u, 1)].rearrange("p a t b -> p (a t b)"),
                                           picked[:, u], AX.X, ALU.add))
            ch.end_loop(NEG // 2)
            ch.after(ch.n)
            tok1, place1 = slots[:, :, 0, :], slots[:, :, 1, :]
            view = lambda t: t.rearrange("p (g b) -> p g b", b=RB)
            t8, pad = view(scratch[:, 0:NEG * RB]), view(scratch[:, 128:128 + NEG * RB])
            v.tensor_scalar(gather_all[:], tok1, -1.0, 0.0, ALU.add, ALU.max)
            v.scalar_tensor_tensor(t8, tok1, float(TOPK), place1, ALU.mult, ALU.add)
            ch.after(ch.did(v.tensor_scalar(pad, tok1, 0.0, float(SKIP + TOPK + 1), ALU.is_equal, ALU.mult)))
            v.scalar_tensor_tensor(scatter_all[:], t8, -float(TOPK + 1), pad, ALU.add, ALU.add).then_inc(
                sem("indices_ready"), 1)

            def columns_of(G, u, m):
                for c in range(3):
                    nb = min(4, RB - 4 * c)
                    v.wait_ge(sem("turned_x"), 3 * G + c + 1)
                    v.tensor_copy(E["xt"][:, u].rearrange("p e (b a) -> p b a e", a=RA)[:, 4 * c:4 * c + nb],
                                  bank[7 - c % 2][:, 0:P * nb].rearrange("p (b a e) -> p b a e", a=RA, e=EG)).then_inc(
                        sem("xt_ready"), 1)
                v.tensor_tensor(picked_gate[:], E["got"][:, u, :, bass.ds(D + G * EG, EG)],
                                own.unsqueeze(1).to_broadcast([P, RB, EG]), ALU.mult).then_inc(sem("picked_gates"), 1)
                v.wait_ge(sem("picked_gates"), G + 1)
                v.tensor_reduce(slot_gate[:, u, :], picked_gate[:], AX.X, ALU.add).then_inc(sem("slot_gate_ready"), 1)

            def product(G, u, j):
                n = G * EG + j
                v.wait_ge(sem("silu_ready"), n + 1)
                v.wait_ge(sem("value_mm"), n + 1)
                v.wait_ge(sem("y_mm"), n - 1 if j > 1 else G * EG)
                v.tensor_tensor(E["prod"][:, j % 2, :], bank[2 * (j % 2)][:, 0:FB * CAP], E["silu"][:, j % 2, :],
                                ALU.mult).then_inc(sem("prod_g_ready"), 1)

            def rows_back(G, u, m):
                if not isinstance(m, int) or m:
                    v.wait_ge(sem(f"scattered{u}"), 16 * RB * m)
                v.wait_ge(sem("slot_gate_ready"), G + 1)
                for c in range(3):
                    nb = min(4, RB - 4 * c)
                    v.wait_ge(sem("turned_y"), 3 * G + c + 1)
                    v.tensor_tensor(E["back"][:, u, 4 * c:4 * c + nb, :],
                                    bank[6 + c % 2][:, 0:P * nb].rearrange("p (b d) -> p b d", d=D),
                                    slot_gate[:, u, 4 * c:4 * c + nb].unsqueeze(2).to_broadcast([P, nb, D]),
                                    ALU.mult).then_inc(sem("turned_y_read"), 1)

            def expert_group(G, u, m, more):
                for j in range(EG):
                    product(G, u, j)
                if more:
                    columns_of(G + 1, 1 - u, m)
                rows_back(G, u, m)

            columns_of(0, 0, 0)
            with v.Fori(0, NEG // 2 - 1) as m:
                for u in range(2):
                    expert_group(2 * m + u, u, m, True)
            expert_group(NEG - 2, 0, NEG // 2 - 1, True)
            expert_group(NEG - 1, 1, NEG // 2 - 1, False)

            H = B["h"]
            pe_rows = C[:, C_PE:C_PE + 2 * D].rearrange("p (s d) -> p s d", s=2)
            s128 = float(np.float32(np.sqrt(np.float32(D))))

            def collect(g):
                for t in range(GT):
                    i = GT * g + t
                    v.wait_ge(sem(f"returned_in{i % 2}"), 16 * (i // 2 + 1))
                    v.tensor_reduce(H[:, g, t, :], B["returned"][:, i % 2, :].rearrange("p (k d) -> p d k", d=D), AX.X,
                                    ALU.add).then_inc(sem("returned_read"), 1)
                v.wait_ge(sem("returned_read"), GT * (g + 1))
                v.wait_ge(sem("base_ready"), g + 1)
                ch.after(ch.did(v.tensor_tensor(H[:, g], H[:, g], tiles(shared, g), ALU.add)))
                norm_stats(v, ch, g, H[:, g])

            def begin_state(g):
                norm_apply(v, NORM_COMBINE + g, g, H[:, g], tiles(x2, g), "x2_ready")
                v.wait_ge(sem("x2_ready"), g + 1)
                for h in range(2):
                    ins = v.scalar_tensor_tensor(state[:, GT * g + 2 * h:GT * g + 2 * h + 2, :],
                                                 x2[:, GT * g + 2 * h:GT * g + 2 * h + 2, :], s128, pe_rows,
                                                 ALU.mult, ALU.add)
                ins.then_inc(sem("x_ready"), 1)

            staggered([collect, begin_state])

            for g in range(GROUPS):
                v.memset(zrow(g)[:, :, 2 * D:Z], 1.0)
            blk = C[:, C_BLK:C_BLK + P]

            def encoder_layer(l, u):
                L = GROUPS * l
                v.tensor_scalar(bq_up[:, u:u + 1], layer_cols[:, u, 0:1], 1.0, None, ALU.add)
                v.tensor_scalar(kv_rows[:, u, 0:D], lrows[u][:, 0:D], 1.0, None, ALU.add)
                ch.after(ch.did(v.tensor_copy(kv_rows[:, u, D:2 * D], lrows[u][:, D:2 * D])))

                def stats1(g):
                    v.wait_ge(sem("x_ready"), L + g + 1)
                    norm_stats(v, ch, g, tiles(state, g))

                def apply1(g):
                    norm_apply(v, NORM_LAYERS + 2 * L + g, g, tiles(state, g), H[:, g], "h1_ready")

                def features(g):
                    v.wait_ge(sem("eq_ready"), L + g + 1)
                    ch.after(ch.did(v.tensor_scalar(B["eq"][:, g % 2], B["eq"][:, g % 2], 1.0, None, ALU.min)))
                    v.scalar_tensor_tensor(B["q"][:, g], bank[2][:], bq_up[:, u:u + 1], B["eq"][:, g % 2], ALU.add,
                                           ALU.max).then_inc(sem("q1_ready"), 1)
                    for h in range(2):
                        v.wait_ge(sem("kv1_mm"), 2 * (L + g) + h + 1)
                        v.tensor_tensor(zrow(g)[:, 2 * h:2 * h + 2, 0:2 * D],
                                        bank[3 + h][:].rearrange("p (i n) -> p i n", i=2),
                                        kv_rows[:, u].unsqueeze(1).to_broadcast([P, 2, 2 * D]), ALU.add).then_inc(
                            sem("z_ready"), 1)

                def features_k(g):
                    v.wait_ge(sem("ek_ready"), L + g + 1)
                    v.scalar_tensor_tensor(B["kp"][:, g], B["ek"][:, g % 2], 1.0, zrow(g)[:, :, 0:D], ALU.min,
                                           ALU.max).then_inc(sem("kp_ready"), 1)

                def mask_kv(g):
                    v.wait_ge(sem("kvsum_mm"), L + g + 1)
                    kvs = bank[5][:, 0:2 * (D + 1)].rearrange("p (b n) -> p b n", b=2)
                    v.tensor_tensor(kvm(g)[:, :, 0:D], kvs[:, :, 0:D], blk.unsqueeze(1).to_broadcast([P, 2, D]), ALU.mult)
                    v.tensor_tensor(kvm(g)[:, :, D:D + HEADS], head.unsqueeze(1).to_broadcast([P, 2, HEADS]),
                                    kvs[:, :, D:D + 1].to_broadcast([P, 2, HEADS]), ALU.mult).then_inc(
                        sem("kvm_ready"), 1)

                def divide(g):
                    s = g % 2
                    v.wait_ge(sem("num_mm"), L + g + 1)
                    for h in range(2):
                        k = ch.did(v.tensor_scalar(
                            den1[:, s, 2 * h:2 * h + 2, :],
                            bank[6 + h][:, 0:2 * (D + HEADS)].rearrange("p (i n) -> p i n", i=2)[:, :, D:D + HEADS],
                            EPS_ATTN, None, ALU.add))
                    ch.after(k)
                    ch.after(ch.did(v.reciprocal(rden1[:, s], den1[:, s])))
                    for h in range(2):
                        ins = v.tensor_tensor(
                            H[:, g, 2 * h:2 * h + 2, :].rearrange("p i (h d) -> p i h d", d=DH),
                            bank[6 + h][:, 0:2 * (D + HEADS)].rearrange("p (i n) -> p i n", i=2)[:, :, 0:D].rearrange(
                                "p i (h d) -> p i h d", d=DH),
                            rden1[:, s, 2 * h:2 * h + 2, :].unsqueeze(3).to_broadcast([P, 2, HEADS, DH]), ALU.mult)
                    ins.then_inc(sem("an1_ready"), 1)

                def residual1(g):
                    v.wait_ge(sem("out1_mm"), L + g + 1)
                    v.wait_ge(sem("plus_bo"), L + g + 1)
                    v.tensor_tensor(tiles(state, g), bank3(5 if g % 2 else 2), tiles(plus, g), ALU.add).then_inc(
                        sem("mid_ready"), 1)
                    v.wait_ge(sem("mid_ready"), L + g + 1)
                    norm_stats(v, ch, g, tiles(state, g))

                def apply2(g):
                    norm_apply(v, NORM_LAYERS + 2 * L + GROUPS + g, g, tiles(state, g), H[:, g], "h2_ready")

                def residual2(g):
                    v.wait_ge(sem("down_mm"), L + g + 1)
                    v.wait_ge(sem("plus_b2"), L + g + 1)
                    v.tensor_tensor(tiles(state, g), bank3(5 if g % 2 else 2), tiles(plus, g), ALU.add).then_inc(
                        sem("x_ready"), 1)

                staggered([stats1, apply1, features, features_k])
                staggered([mask_kv, divide])
                staggered([residual1, apply2])
                staggered([residual2])

            per = 2 * (1 + 2 * GROUPS * 2 * GT + GROUPS + 3 * GROUPS)
            with v.Fori(0, LAYERS // 2) as m:
                ch.loop(m, per)
                for u in range(2):
                    v.wait_ge(sem(f"layer_in{u}"), 48 * (m + 1))
                    encoder_layer(2 * m + u, u)
            ch.end_loop(LAYERS // 2)

            def stats_f(g):
                v.wait_ge(sem("x_ready"), GROUPS * (LAYERS + 1))
                norm_stats(v, ch, g, tiles(state, g))

            def apply_f(g):
                norm_apply(v, NORM_FINAL + g, g, tiles(state, g), H[:, g], "hf_ready")
                v.wait_ge(sem("hf_ready"), g + 1)
                v.wait_ge(sem("fin_in"), 16)
                ch.after(ch.did(v.tensor_tensor(H[:, g], H[:, g], fin_rows[:, 0:D].unsqueeze(1).to_broadcast([P, GT, D]),
                                                ALU.mult)))
                v.wait_ge(sem("plus_lnf"), g + 1)
                ch.after(ch.did(v.tensor_tensor(H[:, g], H[:, g], tiles(plus, g), ALU.add)))

            staggered([stats_f, apply_f])
            staggered([lambda g: norm_stats(v, ch, g, H[:, g]),
                       lambda g: norm_apply(v, NORM_FINAL + GROUPS + g, g, H[:, g], tiles(state, g), "x3_ready")])

            before = C[:, C_BEFORE:C_BEFORE + 2 * SEQ].rearrange("p (h n) -> p h n", h=2)
            own_s, higher, equal, place_s = (small[:, 800 + 16 * k:816 + 16 * k] for k in range(4))
            chosen_m = small[:, 864:880]
            junk = B["ek"].rearrange("p s i d -> p (s i d)")

            def choose(g):
                gs = slice(GT * g, GT * g + GT)
                v.wait_ge(sem("scores_ready"), g + 1)
                ch.after(ch.did(v.tensor_tensor(B["eq"][:, g % 2].rearrange("p (i n) -> p i n", i=GT),
                                                scores[:, g % 2].rearrange("p (i n) -> p i n", i=GT),
                                                ident.unsqueeze(1).to_broadcast([P, GT, P]), ALU.mult)))
                ch.after(ch.did(v.tensor_reduce(own_s[:, gs], B["eq"][:, g % 2].rearrange("p (i n) -> p i n", i=GT), AX.X,
                                                ALU.add)))
                for t in range(GT):
                    i = GT * g + t
                    seq = scores[:, g % 2, SEQ * (t // 2):SEQ * (t // 2 + 1)]
                    v.tensor_scalar(junk[:, 0:SEQ] if t % 2 else junk[:, SEQ:2 * SEQ], seq, own_s[:, i:i + 1], None,
                                    ALU.is_gt, ALU.add, accum_out=higher[:, i:i + 1])
                    ch.after(ch.did(v.scalar_tensor_tensor(
                        junk[:, 2 * SEQ:3 * SEQ] if t % 2 else junk[:, 3 * SEQ:4 * SEQ], seq, own_s[:, i:i + 1],
                        before[:, t % 2, :], ALU.is_equal, ALU.mult, accum_out=equal[:, i:i + 1])))
                ch.after(ch.did(v.tensor_tensor(place_s[:, gs], higher[:, gs], equal[:, gs], ALU.add)))
                v.tensor_scalar(chosen_m[:, gs], place_s[:, gs], float(KEEP), None, ALU.is_lt).then_inc(sem("chosen"), 1)

            def blend(g):
                v.wait_ge(sem("gelu_ready"), g + 1)
                v.wait_ge(sem("twice_ready"), g + 1)
                v.wait_ge(sem("chosen"), g + 1)
                gl = B["q"][:, g].rearrange("p (i d) -> p i d", d=D)
                ch.after(ch.did(v.tensor_tensor(gl, gl, tiles(state, g), ALU.add)))
                for t in range(GT):
                    i = GT * g + t
                    k = ch.did(v.copy_predicated(B["kp"][:, g, t, :], chosen_m[:, i:i + 1].bitcast(U32).to_broadcast([P, D]),
                                                 gl[:, t, :]))
                ch.after(k)
                norm_stats(v, ch, g, B["kp"][:, g])

            def finish(g):
                norm_apply(v, NORM_FINAL + 2 * GROUPS + g, g, B["kp"][:, g], H[:, g], "out_ready")

            staggered([choose, blend, finish])


def pack(inputs):
    a = {k: np.asarray(v) for k, v in inputs.items()}
    c = np.ascontiguousarray
    x = a["L0_attn_x"].reshape(TOK, D)
    wv = a["L0_attn_Wv"].T.reshape(D, HEADS, DH)
    vrep = [np.repeat(wv[:, :, e], DH, axis=1) for e in range(DH)]
    wo = a["L0_attn_Wo"].T.reshape(HEADS, DH, D).transpose(1, 0, 2).reshape(D, D)
    bv = a["L0_attn_bv"].reshape(HEADS, DH)
    l0p = np.stack([a["L0_attn_bq"], a["L0_attn_bk"]] + [np.repeat(bv[:, e], DH) for e in range(DH)], axis=1)
    sw2 = a["L0_ffn_shared_w2"].T.reshape(FB, P, D).transpose(1, 0, 2).reshape(P, FB * D)
    w1 = a["L0_ffn_expert_w1"].transpose(0, 2, 1)
    w2 = a["L0_ffn_expert_w2"].transpose(0, 2, 1).reshape(NE, FB, P, D).transpose(0, 2, 1, 3).reshape(NE, P, FB * D)
    lw2 = a["L1_attn_W2"].reshape(LAYERS, FFB, P, D).transpose(0, 2, 1, 3).reshape(LAYERS, P, FFB * D)
    b1 = a["L1_attn_b1"].reshape(LAYERS, FFB, P).transpose(0, 2, 1)
    cols = [a["L1_attn_" + n][:, :, None] for n in ("bq", "ln1_s", "ln1_b", "ln2_s", "ln2_b")]
    return {
        "cst": constants(),
        "xt0": c(x.T),
        "xr0": c(x.reshape(TILES, P, D).transpose(1, 0, 2)),
        "l0w": c(np.concatenate([a["L0_attn_Wq"].T, a["L0_attn_Wk"].T] + vrep + [wo], axis=1)),
        "l0p": c(l0p),
        "bo0": c(a["L0_attn_bo"]),
        "l0s": c(np.concatenate([a["L0_ffn_wg"].T, a["L0_ffn_shared_w1"].T, sw2], axis=1)),
        "ew": c(np.concatenate([w1, w2], axis=2)),
        "l1w": c(np.concatenate([a["L1_attn_Wq"], a["L1_attn_Wk"], a["L1_attn_Wv"], a["L1_attn_Wo"],
                                 a["L1_attn_W1"], lw2], axis=2)),
        "l1p": c(np.concatenate(cols + [b1], axis=2)),
        "l1r": c(np.stack([a["L1_attn_bk"], a["L1_attn_bv"], a["L1_attn_bo"], a["L1_attn_b2"]], axis=1)),
        "fin_r": c(np.stack([a["L1_attn_lnf_s"], a["L1_attn_lnf_b"]])),
        "mod_w": c(np.concatenate([np.repeat(a["L1_ffn_w_router"][:, None], P, axis=1), a["L1_ffn_w_block"]], axis=1)),
    }


def kernel(**inputs):
    from concourse import bacc
    from concourse.bass_utils import run_bass_kernel_spmd

    nc = bacc.Bacc("TRN2", target_bir_lowering=False, num_devices=1)
    arrays = {f"in_{k}": v for k, v in pack(inputs).items()}
    aps = [nc.dram_tensor(k, v.shape, mybir.dt.from_np(v.dtype), kind="ExternalInput").ap() for k, v in arrays.items()]
    out = nc.dram_tensor("out", (P, TILES, D), F32, kind="ExternalOutput").ap()
    program(nc, *aps, out)
    r = run_bass_kernel_spmd(nc, [arrays], core_ids=[0])
    got = r.results[0]["out"]
    return np.ascontiguousarray(got.transpose(1, 0, 2).reshape(BATCH, SEQ, D))
```

```python
from contextlib import ExitStack

import numpy as np

import concourse.bass as bass
from concourse import mybir

ALU = mybir.AluOpType
ACT = mybir.ActivationFunctionType
AX = mybir.AxisListType
F32 = mybir.dt.float32
F16 = mybir.dt.float16
I32 = mybir.dt.int32
U32 = mybir.dt.uint32

P = 128
D = 128
BATCH, SEQ = 8, 256
TOK = BATCH * SEQ
TILES = TOK // P
GT = 4
GROUP = GT * P
GROUPS = TOK // GROUP
HEADS, DH = 16, 8
NE, TOPK, CAP, FFN = 64, 8, 160, 384
FB = FFN // P
EG = 8
NEG = NE // EG
RA, RB = 16, 10
LAYERS, FF = 4, 512
FFB = FF // P
KEEP = int(SEQ * 0.75)
ARENA = 22528
EPS_LN, EPS_ATTN = 1e-5, 1e-6
ROUTED = D + NE
SKIP = 65536

C_ID, C_BLK, C_HEAD, C_SEL, C_TRI, C_ONES, C_PE, C_EXP, C_TOK, C_RESET = 0, 128, 256, 272, 528, 656, 784, 1040, 1048, 1064
C_BEFORE = C_RESET + GROUP
C_ALL = C_BEFORE + 2 * SEQ


def constants():
    c = np.zeros((P, C_ALL), np.float32)
    r = np.arange(P)
    c[:, C_ID:C_ID + P] = np.eye(P)
    same_head = (r[:, None] // DH) == (r[None, :] // DH)
    c[:, C_BLK:C_BLK + P] = same_head
    c[:, C_HEAD:C_HEAD + HEADS] = (r[:, None] // DH) == np.arange(HEADS)[None, :]
    for e in range(DH):
        s = c[:, C_SEL + 32 * e:C_SEL + 32 * e + 32]
        s[:, 16 * (e % 2):16 * (e % 2) + 16] = c[:, C_HEAD:C_HEAD + HEADS]
    c[:, C_TRI:C_TRI + P] = (r[:, None] < r[None, :]) - 1.0
    c[:, C_ONES:C_ONES + P] = 1.0
    half = D // 2
    freq = np.exp(np.arange(half, dtype=np.float32) * np.float32(-np.log(10000.0) / (half - 1))).astype(np.float32)
    pos = (np.arange(SEQ, dtype=np.float32) + 1.0)[:, None] * freq[None, :]
    pe = np.concatenate([np.sin(pos), np.cos(pos)], axis=-1).astype(np.float32)
    c[:, C_PE:C_PE + 2 * D] = pe.reshape(2, P, D).transpose(1, 0, 2).reshape(P, 2 * D)
    c[:, C_EXP:C_EXP + EG] = (r[:, None] % EG) == np.arange(EG)[None, :]
    c[:, C_TOK:C_TOK + TILES] = r[:, None] + P * np.arange(TILES)[None, :] + 1.0
    for h in range(2):
        c[:, C_BEFORE + SEQ * h:C_BEFORE + SEQ * h + SEQ] = np.arange(SEQ)[None, :] < P * h + r[:, None]
    c[:, C_RESET:C_RESET + GROUP] = (np.arange(GROUP) % SEQ != 0)
    return c


class Chain:

    def __init__(self, eng, sem):
        self.eng, self.sem, self.n, self.off = eng, sem, 0, 0

    def did(self, ins):
        ins.then_inc(self.sem, 1)
        self.n += 1
        return self.off + self.n

    def after(self, number):
        self.eng.wait_ge(self.sem, number)

    def loop(self, i, per):
        self.n0, self.per = self.n, per
        self.off = i * per

    def end_loop(self, times):
        assert self.n - self.n0 == self.per, (self.n - self.n0, self.per)
        self.n = self.n0 + times * self.per
        self.off = 0


def program(nc, cst, xt0, xr0, l0w, l0p, bo0, l0s, ew, l1w, l1p, l1r, fin_r, mod_w, out):
    with ExitStack() as ctx:
        def sb(name, shape, dt=F32):
            return ctx.enter_context(nc.sbuf_tensor(name, [P] + shape, dt))

        sems = {}

        def sem(name):
            if name not in sems:
                sems[name] = ctx.enter_context(nc.semaphore(name))
            return sems[name]

        bank = [ctx.enter_context(nc.psum_tensor(f"bank{i}", [P, 512], F32)) for i in range(8)]

        dispatch_dram = nc.dram_tensor("dispatch_rows", [TOK, ROUTED], F32).ap()
        returned_dram = nc.dram_tensor("returned_rows", [TOK * TOPK, D], F32).ap()

        C = sb("consts", [C_ALL])
        ident = C[:, C_ID:C_ID + P]
        tri16, ones16 = sb("tri16", [P], F16), sb("ones16", [P], F16)
        x1 = sb("x1", [TILES, D])
        x1t = sb("x1t", [TOK])
        shared = sb("shared", [TILES, D])
        logits = sb("logits", [TILES, NE])
        gates = sb("gates", [TILES, NE])
        ring = sb("ring", [EG, 9 * D])
        arena = sb("arena", [ARENA])

        def carve(parts, at=0):
            made = {}
            for name, shape, dt in parts:
                n = int(np.prod(shape))
                words = n if dt != F16 else n // 2
                a = arena[:, at:at + words]
                if dt != F32:
                    a = a.bitcast(dt)
                if len(shape) == 2:
                    a = a.rearrange("p (a b) -> p a b", b=shape[1])
                elif len(shape) == 3:
                    a = a.rearrange("p (a b c) -> p a b c", b=shape[1], c=shape[2])
                made[name] = a
                at += words
            assert at <= ARENA, at
            return made

        A = carve([("xt", (TOK,), F32), ("w", (2 * P + DH * P + P,), F32),
                   ("eqk", (2, GROUP), F32), ("q", (GROUPS, GROUP), F32), ("k", (GROUP,), F32),
                   ("ksum", (GROUP,), F32), ("kv", (2, GROUP), F32), ("run", (2, GROUP), F32),
                   ("prod", (2, DH, GROUP), F32), ("dk", (GROUPS, GROUP), F32), ("att", (GROUPS, GROUP), F32)])
        at_prod = TOK + 11 * P + 12 * GROUP
        T = carve([("an", (GROUPS, GROUP), F32), ("ant", (GROUPS, GROUP), F32), ("xs", (GROUPS, GROUP), F32)],
                  at_prod)
        xr = shared
        l0ps = sb("l0ps", [10])
        bq1 = sb("bq1", [2])
        bo_bc = sb("bo_bc", [D])
        sw = sb("sw", [NE + 9 * D])

        small = sb("small", [1024])
        den = small[:, 0:GROUPS * 64].rearrange("p (g n) -> p g n", g=GROUPS)
        rden = small[:, 256:256 + GROUPS * 64].rearrange("p (g n) -> p g n", g=GROUPS)
        NORMS = {"first": (0, 0), "combine": (0, GROUPS), "final": (0, 2 * GROUPS),
                 "norm1": (1, 0), "second": (1, GROUPS * LAYERS), "norm2": (2, 0), "last": (2, GROUPS * LAYERS)}
        stats = sb("stats", [6, GT, 6])
        mv = sb("mv", [6, GT, 2])
        veps = sb("veps", [6, GT])
        rstd = sb("rstd", [6, GT])
        minus_half = sb("minus_half", [GT])
        minus_one = sb("minus_one", [1])
        zeros = sb("zeros", [1024])
        scratch = zeros
        hidden = sb("hidden", [3 * FB, GROUP])
        new_tile = sb("new_tile", [TILES * NE], F16)
        new_token = sb("new_token", [TILES * NE], F16)
        route = small[:, 512:768]
        best8 = sb("best8", [TILES, 8])
        slots = sb("slots", [NEG, 2, RB])
        picked = sb("picked", [2, 2 * RB, EG])
        gather_all, scatter_all = sb("gather_all", [NEG, RB], U32), sb("scatter_all", [NEG, RB], U32)
        gather_ix, scatter_ix = sb("gather_ix", [2, RB], U32), sb("scatter_ix", [2, RB], U32)
        slot_gate = sb("slot_gate", [2, RB])
        picked_gate = sb("picked_gate", [RB, EG])
        TE = TILES * NE
        R = carve([("a", (TILES, NEG * RA * EG), F16), ("b", (2 * RB, TE), F16), ("mask_ei", (TE,), F16),
                   ("upto_ei", (TE,), F16), ("place", (TE,), F16), ("token", (TE,), F16), ("mask", (TE,), F16)])
        R["ai"], R["bi"] = R["mask_ei"], R["upto_ei"]
        at_mask = (TILES * NEG * RA * EG + 2 * RB * TE + 4 * TE) // 2
        Z = 2 * D + 1
        LW, LP = 12 * P, 9
        at_relu = ARENA - (2 * FFB * GROUP + 2 * TOPK * D)
        B = carve([("h", (GROUPS, GT, D), F32), ("ht", (GROUPS, GROUP), F32), ("q", (GROUPS, GROUP), F32),
                   ("z", (GROUPS, GT * Z), F32), ("kp", (GROUPS, GT, D), F32), ("eq", (2, GROUP), F32),
                   ("ek", (2, GT, D), F32), ("kvm", (GROUPS, 2 * (D + HEADS)), F32)])
        B.update(carve([("relu", (2, FFB, GROUP), F32)], at_relu))
        layer_cols = sb("layer_cols", [LAYERS, LP])
        bq_up = sb("bq_up", [LAYERS])
        den1, rden1 = sb("den1", [2, GT, HEADS]), sb("rden1", [2, GT, HEADS])
        got_at = [x1t[:, 0:RB * ROUTED], arena[:, at_mask:at_mask + RB * ROUTED]]
        got = [a.rearrange("p (b c) -> p b c", c=ROUTED) for a in got_at]
        E = carve([("xt", (2, EG, RB * RA), F32), ("yt", (2, RB, P), F32),
                   ("back", (2, RB, D), F32), ("silu", (2, FB * CAP), F32), ("prod", (2, FB * CAP), F32)])

        block = ctx.enter_context(nc.Block())

        def tiles(buf, g):
            return buf[:, GT * g:GT * (g + 1)]

        def cols(buf, g):
            return buf[:, bass.ds(g * GROUP, GROUP)]

        def bank3(b, n=P):
            return bank[b][:, 0:GT * n].rearrange("p (i n) -> p i n", n=n)

        def staggered(steps):
            for g in range(GROUPS + len(steps) - 1):
                for k, step in enumerate(steps):
                    if 0 <= g - k < GROUPS:
                        step(g - k)

        def norm_stats(v, ch, kind, n, g, src):
            s = 2 * NORMS[kind][0] + g % 2
            for i in range(GT):
                k = ch.did(v.bn_stats(stats[:, s, i, :], src[:, i, :]))
            ch.after(k)
            v.sem_inc(sem("stats_taken"))
            for i in range(GT):
                k = ch.did(v.bn_aggr(mv[:, s, i, :], stats[:, s, i, :]))
            ch.after(k)
            v.tensor_scalar(veps[:, s, :], mv[:, s, :, 1], EPS_LN, None, ALU.add).then_inc(
                sem(f"var{NORMS[kind][0]}_ready"), 1)

        def norm_rstd(pool, kind, n, g):
            which, before = NORMS[kind]
            s = 2 * which + g % 2
            pool.wait_ge(sem(f"var{which}_ready"), before + n + 1)
            pool.tensor_tensor(rstd[:, s, :], veps[:, s, :], minus_half[:], ALU.pow).then_inc(
                sem(f"rstd{which}_ready"), 1)

        def norm_apply(v, kind, n, g, src, dst, done):
            which, before = NORMS[kind]
            s = 2 * which + g % 2
            v.wait_ge(sem(f"rstd{which}_ready"), before + n + 1)
            for i in range(GT):
                ins = v.tensor_scalar(dst[:, i, :], src[:, i, :], mv[:, s, i, 0:1], rstd[:, s, i:i + 1],
                                      ALU.subtract, ALU.mult)
            ins.then_inc(sem(done), 1)

        def tiles_at(buf, g):
            return buf[:, bass.ds(g * GT, GT), :]

        flat_ring = ring[:].rearrange("p j n -> p (j n)")
        w_qkv, w_o = flat_ring[:, 0:3 * P], flat_ring[:, 3 * P:4 * P]
        w_up, w_down = flat_ring[:, 4 * P:8 * P], flat_ring[:, 8 * P:12 * P]
        at = LW
        lrows = flat_ring[:, at:at + 4 * LAYERS * D].rearrange("p (l n) -> p l n", l=LAYERS)
        at += 4 * LAYERS * D
        mod_sb, fin_rows = flat_ring[:, at:at + 2 * D], flat_ring[:, at + 2 * D:at + 4 * D]
        at += 4 * D
        scores = flat_ring[:, at:at + 2 * GROUP].rearrange("p (s n) -> p s n", s=2)
        at += 2 * GROUP
        spare = [hidden[:].rearrange("p a n -> p (a n)")[:, TOPK * D * k:TOPK * D * (k + 1)] for k in range(4)]
        spare += [flat_ring[:, at + TOPK * D * k:at + TOPK * D * (k + 1)] for k in range(4)]
        spare += [arena[:, at_relu + TOPK * D * k:at_relu + TOPK * D * (k + 1)] for k in range(6)]
        spare += [gates[:].rearrange("p i e -> p (i e)"), logits[:].rearrange("p i e -> p (i e)")]
        x2, state, plus = x1, shared, x1t[:].rearrange("p (i d) -> p i d", d=D)
        ITEMS = GROUPS * LAYERS

        def pipeline(eng, slot, body=None):
            for t in range(-2, GROUPS - 1):
                slot(t, t, 1)
            with eng.Fori(1, LAYERS) as l:
                if body:
                    body(l)
                for j in range(GROUPS):
                    slot(l * GROUPS + (j - 1), GROUPS - 1 + j, l)
            if body:
                body(None)
            for t in range(ITEMS - 1, ITEMS + 6):
                slot(t, t, 1)

        def item(k, back):
            return 0 <= k - back < ITEMS

        def layer_of(l, k, back):
            return l + ((k - back) // GROUPS - 1)

        def layer_col(l, k):
            return layer_cols[:, bass.ds(l, 1), k:k + 1].rearrange("p a n -> p (a n)")

        def zrow(g):
            return B["z"][:, g].rearrange("p (i n) -> p i n", n=Z)

        def kvm(g):
            return B["kvm"][:, g].rearrange("p (b n) -> p b n", b=2)

        logits_i = logits[:].rearrange("p i e -> p (i e)").bitcast(I32)

        xt, w0 = A["xt"], A["w"]
        W_Q, W_K, W_V, W_O = 0, P, 2 * P, (2 + DH) * P
        eqk, k0 = A["eqk"], A["k"]
        q_of = lambda i: A["q"][:, bass.ds(i, 1), :].rearrange("p a n -> p (a n)")
        v_banks = (2, 3, 5, 6)
        ksum, kv, run, prod = A["ksum"], A["kv"], A["run"], A["prod"][:, 0]
        dk, att = A["dk"], A["att"]
        reset = C[:, C_RESET:C_RESET + GROUP]
        head = C[:, C_HEAD:C_HEAD + HEADS]

        @block.sync
        def _(sp):
            sp.dma_start(w0, l0w).then_inc(sem("l0w_in"), 16)
            for g in range(GROUPS):
                sp.dma_start(cols(xt, g), cols(xt0, g)).then_inc(sem("xt_in"), 16)
            sp.dma_start(l0ps[:], l0p).then_inc(sem("l0p_in"), 16)
            sp.dma_start(C[:], cst).then_inc(sem("consts_in"), 16)
            sp.dma_start(xr[:], xr0).then_inc(sem("xr_in"), 16)
            sp.dma_start(bo_bc[:], bo0.partition_broadcast(P)).then_inc(sem("bo_in"), 16)
            sp.dma_start(sw[:], l0s).then_inc(sem("sw_in"), 16)
            for j in range(EG):
                sp.dma_start(ring[:, j, :], ew[j]).then_inc(sem(f"expert_in{j}"), 16)
            sp.wait_ge(sem("zeros_ready"), 1)
            zrows = returned_dram.rearrange("(n p r) d -> n p (r d)", p=P, r=8)
            for n in range(TOK * TOPK // (8 * P)):
                sp.dma_start(zrows[n], zeros[:]).then_inc(sem("zeroed"), 16)
            rows = dispatch_dram.rearrange("(i p) c -> p i c", p=P)
            sp.wait_ge(sem("x1_ready"), GROUPS)
            sp.dma_start(rows[:, :, 0:D], x1[:]).then_inc(sem("rows_out"), 16)
            sp.wait_ge(sem("gates_ready"), 1)
            sp.dma_start(rows[:, :, D:ROUTED], gates[:]).then_inc(sem("rows_out"), 16)
            with sp.Fori(1, NEG) as G:
                for j in range(EG):
                    sp.wait_ge(sem("y_mm"), G * EG + j - (EG - 1))
                    sp.dma_start(ring[:, j, :], ew[bass.ds(G * EG + j, 1)].rearrange("a p n -> (a p) n")).then_inc(
                        sem(f"expert_in{j}"), 16)
            sp.wait_ge(sem("y_mm"), NE)
            sp.dma_start(w_qkv, l1w[0][:, 0:3 * P]).then_inc(sem("qkv_in"), 16)
            sp.dma_start(layer_cols[:], l1p).then_inc(sem("cols_in"), 16)
            sp.dma_start(lrows, l1r.rearrange("l a d -> l (a d)").partition_broadcast(P)).then_inc(sem("rows_in"), 16)
            sp.dma_start(w_o, l1w[0][:, 3 * P:4 * P]).then_inc(sem("o_in"), 16)
            mine = returned_dram.rearrange("(i p k) d -> i p (k d)", p=P, k=TOPK)
            for u in range(2):
                sp.wait_ge(sem(f"scattered{u}"), 16 * RB * NEG // 2)
            for i in range(TILES):
                sp.dma_start(spare[i], mine[i]).then_inc(sem(f"returned_in{i // GT}"), 16)
            sp.dma_start(w_up, l1w[0][:, 4 * P:8 * P]).then_inc(sem("up_in"), 16)
            sp.dma_start(w_down, l1w[0][:, 8 * P:12 * P]).then_inc(sem("down_in"), 16)
            sp.dma_start(mod_sb, mod_w).then_inc(sem("mod_in"), 16)
            sp.dma_start(fin_rows, fin_r.rearrange("a d -> (a d)").partition_broadcast(P)).then_inc(sem("fin_in"), 16)
            with sp.Fori(1, LAYERS) as l:
                w = l1w[bass.ds(l, 1)].rearrange("a p n -> (a p) n")
                sp.wait_ge(sem("kv1_mm"), 2 * GROUPS * l)
                sp.dma_start(w_qkv, w[:, 0:3 * P]).then_inc(sem("qkv_in"), 16)
                sp.wait_ge(sem("out1_mm"), GROUPS * l)
                sp.dma_start(w_o, w[:, 3 * P:4 * P]).then_inc(sem("o_in"), 16)
                sp.wait_ge(sem("up_mm"), FFB * GROUPS * l)
                sp.dma_start(w_up, w[:, 4 * P:8 * P]).then_inc(sem("up_in"), 16)
                sp.wait_ge(sem("down_mm"), GROUPS * l)
                sp.dma_start(w_down, w[:, 8 * P:12 * P]).then_inc(sem("down_in"), 16)
            for g in range(GROUPS):
                sp.wait_ge(sem("out_ready"), g + 1)
                sp.dma_start(tiles(out, g), B["h"][:, g]).then_inc(sem("out_done"), 16)
            sp.wait_ge(sem("out_done"), 16 * GROUPS)

        @block.tensor
        def _(pe):
            def project_qk(i):
                if not isinstance(i, int) or i:
                    pe.wait_ge(sem("k_ready"), i)
                pe.matmul(bank[0][:], w0[:, W_Q:W_Q + P], cols(xt, i), start=True, stop=True)
                pe.matmul(bank[1][:], w0[:, W_K:W_K + P], cols(xt, i), start=True, stop=True).then_inc(
                    sem("qk_mm"), 1)

            def project_v(i):
                for e in range(DH):
                    pe.wait_ge(sem("kv_ready"), i * DH + e + 1)
                    pe.matmul(bank[v_banks[e % 4]][:], w0[:, W_V + P * e:W_V + P * e + P], cols(xt, i),
                              start=True, stop=True).then_inc(sem("v_mm"), 1)

            def sum_heads(i, last=False):
                pe.wait_ge(sem("prod_ready"), (i + 1) * DH)
                if last:
                    pe.wait_ge(sem("att_ready"), i)
                else:
                    pe.wait_ge(sem("exp_ready"), i + 2)
                for e in (0, 2, 4, 6, 1, 3, 5, 7):
                    j = e // 2
                    mm = pe.matmul(bank[4][32 * j:32 * j + 32, :], C[:, C_SEL + 32 * e:C_SEL + 32 * e + 32],
                                   prod[:, e, :], start=(e % 2 == 0), stop=(e % 2 == 1))
                mm.then_inc(sem("att_mm"), 1)

            pe.wait_ge(sem("l0w_in"), 16)
            pe.wait_ge(sem("xt_in"), 16 * GROUPS)
            project_qk(0)
            pe.wait_ge(sem("consts_in"), 16)
            with pe.Fori(0, GROUPS - 1) as i:
                project_v(i)
                project_qk(i + 1)
                sum_heads(i)
            project_v(GROUPS - 1)
            sum_heads(GROUPS - 1, True)

            pe.wait_ge(sem("dk_ready"), GROUPS)
            for t in range(TILES):
                mm = pe.matmul(bank[7][:, HEADS * t:HEADS * t + HEADS],
                               dk[:, t // GT, P * (t % GT):P * (t % GT) + P], head, start=True, stop=True)
            mm.then_inc(sem("den_mm"), 1)
            for g in range(GROUPS):
                pe.wait_ge(sem("att_ready"), g + 1)
                if g >= 2:
                    pe.wait_ge(sem("an_ready"), g - 1)
                for t in range(GT):
                    mm = pe.transpose(bank[5 + g % 2][:, P * t:P * t + P], att[:, g, P * t:P * t + P], ident)
                mm.then_inc(sem("turned_att"), 1)
            for g in range(GROUPS + 1):
                if g < GROUPS:
                    pe.wait_ge(sem("an_ready"), g + 1)
                    if g >= 2:
                        pe.wait_ge(sem("ant_ready"), g - 1)
                    for t in range(GT):
                        mm = pe.transpose(bank[3 + g % 2][:, P * t:P * t + P], T["an"][:, g, P * t:P * t + P], ident)
                    mm.then_inc(sem("turned_an"), 1)
                if g:
                    h = g - 1
                    pe.wait_ge(sem("ant_ready"), h + 1)
                    if h >= 2:
                        pe.wait_ge(sem("xs_ready"), h - 1)
                    for t in range(GT):
                        mm = pe.matmul(bank[h % 2][:, P * t:P * t + P], T["ant"][:, h, P * t:P * t + P],
                                       w0[:, W_O:W_O + P], start=True, stop=True)
                    mm.then_inc(sem("wo_mm"), 1)
            pe.wait_ge(sem("sw_in"), 16)
            for g in range(GROUPS + 1):
                if g < GROUPS:
                    pe.wait_ge(sem("x1_ready"), g + 1)
                    if g >= 2:
                        pe.wait_ge(sem("x1t_ready"), g - 1)
                    for t in range(GT):
                        mm = pe.transpose(bank[5 + g % 2][:, P * t:P * t + P], x1[:, GT * g + t, :], ident)
                    mm.then_inc(sem("turned_x1"), 1)
                if g:
                    h = g - 1
                    pe.wait_ge(sem("x1t_ready"), h + 1)
                    if h >= 2:
                        pe.wait_ge(sem("logits_ready"), h - 1)
                    for t in range(GT):
                        mm = pe.matmul(bank[3 + h % 2][:, NE * t:NE * t + NE],
                                       x1t[:, GROUP * h + P * t:GROUP * h + P * t + P], sw[:, 0:NE],
                                       start=True, stop=True)
                    mm.then_inc(sem("logits_mm"), 1)

            wg, sw1, sw2 = sw[:, 0:NE], sw[:, NE:NE + 2 * FFN], sw[:, NE + 2 * FFN:].rearrange("p (f d) -> p f d", d=D)

            def shared_expert(g):
                for f in range(FB):
                    if not isinstance(g, int) or g:
                        pe.wait_ge(sem("hidden_read"), (g - 1) * FB + f + 1)
                    pe.matmul(bank[2 + 2 * f][:], sw1[:, P * (FB + f):P * (FB + f) + P], cols(x1t, g),
                              start=True, stop=True)
                    pe.matmul(bank[3 + 2 * f][:], sw1[:, P * f:P * f + P], cols(x1t, g),
                              start=True, stop=True).then_inc(sem("hidden_mm"), 1)
                pe.wait_ge(sem("hidden_ready"), (g + 1) * FB)
                if not isinstance(g, int) or g:
                    pe.wait_ge(sem("shared_ready"), g)
                for t in range(GT):
                    for f in range(FB):
                        mm = pe.matmul(bank[0][:, P * t:P * t + P], hidden[:, 2 * FB + f, P * t:P * t + P], sw2[:, f, :],
                                       start=(f == 0), stop=(f == FB - 1))
                mm.then_inc(sem("shared_mm"), 1)

            pe.wait_ge(sem("logits_ready"), GROUPS)
            pe.wait_ge(sem("x1t_ready"), GROUPS)
            shared_expert(0)
            pe.wait_ge(sem("masks_ready"), 1)
            pe.wait_ge(sem("shared_ready"), 1)
            for h in range(2):
                pe.matmul(bank[h][:], ones16[:], R["upto_ei"].rearrange("p (e i) -> p i e", i=TILES)[:, 8 * h:8 * h + 8, :],
                          start=True, stop=False)
                mm = pe.matmul(bank[h][:], tri16[:], R["mask"][:, 512 * h:512 * h + 512], start=False, stop=True)
            mm.then_inc(sem("rank_mm"), 1)
            pe.wait_ge(sem("rank_read"), 1)
            with pe.Fori(1, GROUPS - 1) as g:
                shared_expert(g)
            a16 = R["a"].rearrange("p i (g n) -> p i g n", n=RA * EG)
            b16 = R["b"].rearrange("p b (i e) -> p b i e", e=NE)

            def find_slots(q):
                pe.wait_ge(sem("one_hots_ready"), q + 1)
                if not isinstance(q, int) or q:
                    pe.wait_ge(sem("slots_read"), q)
                for u in range(2):
                    for i in range(TILES):
                        lhs = a16[:, i, bass.ds(2 * q + u, 1), :].rearrange("p g n -> p (g n)")
                        mm = pe.matmul(bank[1][:, 2 * RB * EG * u:2 * RB * EG * (u + 1)], lhs,
                                       b16[:, :, i, bass.ds(EG * (2 * q + u), EG)],
                                       start=(i == 0), stop=(i == TILES - 1))
                mm.then_inc(sem("slots_mm"), 1)

            find_slots(0)
            shared_expert(GROUPS - 1)
            with pe.Fori(1, NEG // 2) as q:
                find_slots(q)

            def turn_inputs(G, u, m):
                pe.wait_ge(sem(f"gathered{u}"), 16 * RB * (m + 1))
                for c in range(3):
                    if c == 2:
                        pe.wait_ge(sem("xt_ready"), 3 * G + 1)
                    for b in range(4 * c, min(4 * c + 4, RB)):
                        mm = pe.transpose(bank[7 - c % 2][:, P * (b % 4):P * (b % 4) + P], got[u][:, b, 0:D], ident)
                    mm.then_inc(sem("turned_x"), 1)

            def turn_results(G, u, more):
                for c in range(3):
                    if c < 2:
                        if more:
                            pe.wait_ge(sem("xt_ready"), 3 * G + 5 + c)
                        else:
                            pe.wait_ge(sem("turned_y_read"), 3 * G)
                    else:
                        pe.wait_ge(sem("turned_y_read"), 3 * G + 1)
                    for b in range(4 * c, min(4 * c + 4, RB)):
                        mm = pe.transpose(bank[6 + c % 2][:, P * (b % 4):P * (b % 4) + P], E["yt"][:, u, b, :], ident)
                    mm.then_inc(sem("turned_y"), 1)

            def expert_hidden(G, u, j):
                n = G * EG + j
                pe.wait_ge(sem(f"expert_in{j}"), 16 * (G + 1))
                if j > 1:
                    pe.wait_ge(sem("prod_g_ready"), n - 1)
                for part in (1, 0):
                    for f in range(FB):
                        mm = pe.matmul(bank[2 * (j % 2) + part][:, CAP * f:CAP * f + CAP],
                                       ring[:, j, P * (FB * part + f):P * (FB * part + f) + P], E["xt"][:, u, j, :],
                                       start=True, stop=True)
                    mm.then_inc(sem("gate_mm" if part else "value_mm"), 1)

            def expert_result(G, u, j):
                n = G * EG + j
                pe.wait_ge(sem("prod_g_ready"), n + 1)
                if j > 1:
                    pe.wait_ge(sem("yt_ready"), n - 1)
                for f in range(FB):
                    mm = pe.matmul(bank[4 + j % 2][:, 0:CAP], ring[:, j, P * (2 * FB + f):P * (2 * FB + f) + P],
                                   E["prod"][:, j % 2, CAP * f:CAP * f + CAP], start=(f == 0), stop=(f == FB - 1))
                mm.then_inc(sem("y_mm"), 1)

            def expert_group(G, u, m, more):
                pe.wait_ge(sem("xt_ready"), 3 * (G + 1))
                for j in range(EG):
                    expert_hidden(G, u, j)
                    if j:
                        expert_result(G, u, j - 1)
                if more:
                    turn_inputs(G + 1, 1 - u, m + u)
                expert_result(G, u, EG - 1)
                pe.wait_ge(sem("yt_ready"), (G + 1) * EG)
                turn_results(G, u, more)

            turn_inputs(0, 0, 0)
            pe.wait_ge(sem("shared_ready"), GROUPS)
            pe.wait_ge(sem("slots_read"), NEG // 2)
            with pe.Fori(0, NEG // 2 - 1) as m:
                for u in range(2):
                    expert_group(2 * m + u, u, m, True)
            expert_group(NEG - 2, 0, NEG // 2 - 1, True)
            expert_group(NEG - 1, 1, NEG // 2 - 1, False)

            def turn(src, b, done):
                for t in range(GT):
                    mm = pe.transpose(bank[b][:, P * t:P * t + P], src[:, t, :], ident)
                mm.then_inc(sem(done), 1)

            def turn_norm1(n, k, g):
                pe.wait_ge(sem("h1_ready"), n + 1)
                if k >= 3:
                    pe.wait_ge(sem("h2t_ready"), n - 2)
                turn(B["h"][:, g], 0, "turned1")

            def project(n, k, g, l):
                pe.wait_ge(sem("qkv_in"), 16 * (l + 1))
                pe.wait_ge(sem("ht_ready"), n + 1)
                if k >= 2:
                    pe.wait_ge(sem("mid_ready"), n - 1)
                pe.matmul(bank[2][:], w_qkv[:, 0:P], B["ht"][:, g], start=True, stop=True).then_inc(sem("q1_mm"), 1)
                if k >= 3:
                    pe.wait_ge(sem("relu_ready"), FFB * (n - 2))
                for h in range(2):
                    for t in range(2):
                        mm = pe.matmul(bank[3 + h][:, 2 * D * t:2 * D * t + 2 * D],
                                       B["ht"][:, g, P * (2 * h + t):P * (2 * h + t) + P], w_qkv[:, P:3 * P],
                                       start=True, stop=True)
                    mm.then_inc(sem("kv1_mm"), 1)

            def sum_kv(n, k, g):
                pe.wait_ge(sem("kp_ready"), n + 1)
                pe.wait_ge(sem("x_ready"), n + 2 if k < ITEMS - 1 else ITEMS + 1)
                for t in range(GT):
                    mm = pe.matmul(bank[5][:, (D + 1) * (t // 2):(D + 1) * (t // 2 + 1)], B["kp"][:, g, t, :],
                                   zrow(g)[:, t, D:Z], start=(t % 2 == 0), stop=(t % 2 == 1))
                mm.then_inc(sem("kvsum_mm"), 1)

            def attend(n, k, g):
                pe.wait_ge(sem("kvm_ready"), n + 1)
                if k >= 2:
                    pe.wait_ge(sem("relu_ready"), FFB * (n - 1))
                for t in range(GT):
                    mm = pe.matmul(bank[6 + t // 2][:, (D + HEADS) * (t % 2):(D + HEADS) * (t % 2 + 1)],
                                   B["q"][:, g, P * t:P * t + P], kvm(g)[:, t // 2, :], start=True, stop=True)
                mm.then_inc(sem("num_mm"), 1)

            def turn_attention(n, k, g):
                pe.wait_ge(sem("an1_ready"), n + 1)
                if k >= 1:
                    pe.wait_ge(sem("at_ready"), n)
                turn(B["h"][:, g], 1, "turned2")

            def output(n, k, g, l):
                pe.wait_ge(sem("o_in"), 16 * (l + 1))
                pe.wait_ge(sem("at_ready"), n + 1)
                if k < ITEMS - 1:
                    pe.wait_ge(sem("q1_ready"), n + 2)
                else:
                    pe.wait_ge(sem("mid_ready"), n)
                for t in range(GT):
                    mm = pe.matmul(bank[2][:, P * t:P * t + P], B["ht"][:, g, P * t:P * t + P], w_o,
                                   start=True, stop=True)
                mm.then_inc(sem("out1_mm"), 1)

            def turn_norm2(n, k, g):
                pe.wait_ge(sem("h2_ready"), n + 1)
                if k < ITEMS - 2:
                    pe.wait_ge(sem("ht_ready"), n + 3)
                elif k < ITEMS - 1:
                    pe.wait_ge(sem("h2t_ready"), n)
                else:
                    pe.wait_ge(sem("gelu_ready"), 1)
                turn(B["h"][:, g], 0, "turned3")

            def up(n, k, g, l):
                pe.wait_ge(sem("up_in"), 16 * (l + 1))
                pe.wait_ge(sem("h2t_ready"), n + 1)
                for f in range(FFB):
                    if k >= ITEMS - 2 and (f < 2 or k == ITEMS - 1):
                        pe.wait_ge(sem("relu_ready"), FFB * (n - 1) + f + 1)
                    elif f == 0:
                        pe.wait_ge(sem("z_ready"), 2 * (n + 3))
                    elif f == 2:
                        pe.wait_ge(sem("an1_ready"), n + 2)
                    pe.matmul(bank[(3, 4, 6, 7)[f]][:], w_up[:, P * f:P * f + P], B["ht"][:, g], start=True,
                              stop=True).then_inc(sem("up_mm"), 1)

            def down(n, k, g, l):
                pe.wait_ge(sem("down_in"), 16 * (l + 1))
                pe.wait_ge(sem("relu_ready"), FFB * (n + 1))
                if k < ITEMS - 2:
                    pe.wait_ge(sem("kvm_ready"), n + 3)
                else:
                    pe.wait_ge(sem("x_ready"), GROUPS + n)
                for t in range(GT):
                    for f in range(FFB):
                        mm = pe.matmul(bank[5][:, P * t:P * t + P],
                                       B["relu"][:, g % 2, f, P * t:P * t + P], w_down[:, P * f:P * f + P],
                                       start=(f == 0), stop=(f == FFB - 1))
                mm.then_inc(sem("down_mm"), 1)

            def score(g):
                pe.wait_ge(sem("mod_in"), 16)
                pe.wait_ge(sem("x3_ready"), g + 1)
                if g:
                    pe.wait_ge(sem("x3t_ready"), g)
                else:
                    pe.wait_ge(sem("at_ready"), ITEMS)
                turn(state[:, GT * g:GT * g + GT], 1, "turned_x3")
                pe.wait_ge(sem("x3t_ready"), g + 1)
                if g:
                    pe.wait_ge(sem("scores_ready"), g)
                else:
                    pe.wait_ge(sem("mid_ready"), ITEMS)
                pe.matmul(bank[2][:], mod_sb[:, 0:P], B["ht"][:, g], start=True, stop=True).then_inc(
                    sem("score_mm"), 1)
                if g:
                    pe.wait_ge(sem("gelu_ready"), g)
                if g < 2:
                    pe.wait_ge(sem("h2t_ready"), ITEMS - 1 + g)
                for t in range(GT):
                    mm = pe.matmul(bank[0][:, P * t:P * t + P], B["ht"][:, g, P * t:P * t + P], mod_sb[:, P:2 * P],
                                   start=True, stop=True)
                mm.then_inc(sem("block_mm"), 1)

            def slot(t, k, l):
                g = k % GROUPS
                if item(k, 1):
                    sum_kv(t - 1, k - 1, (g - 1) % GROUPS)
                if item(k, 0):
                    turn_norm1(t, k, g)
                if item(k, 1):
                    attend(t - 1, k - 1, (g - 1) % GROUPS)
                if item(k, 0):
                    project(t, k, g, layer_of(l, k, 0))
                if item(k, 1):
                    turn_attention(t - 1, k - 1, (g - 1) % GROUPS)
                if item(k, 2):
                    turn_norm2(t - 2, k - 2, (g - 2) % GROUPS)
                if item(k, 3):
                    down(t - 3, k - 3, (g - 3) % GROUPS, layer_of(l, k, 3))
                if item(k, 1):
                    output(t - 1, k - 1, (g - 1) % GROUPS, layer_of(l, k, 1))
                if item(k, 2):
                    up(t - 2, k - 2, (g - 2) % GROUPS, layer_of(l, k, 2))
                if ITEMS <= k < ITEMS + GROUPS:
                    score(k - ITEMS)

            pipeline(pe, slot)

        @block.scalar
        def _(act):
            def exps(i):
                if not isinstance(i, int) or i:
                    act.wait_ge(sem("k_ready"), i)
                act.wait_ge(sem("qk_mm"), i + 1)
                act.activation(eqk[:, 0, :], bank[0][:], ACT.Exp, bias=l0ps[:, 0:1])
                act.activation(eqk[:, 1, :], bank[1][:], ACT.Exp, bias=l0ps[:, 1:2]).then_inc(sem("exp_ready"), 1)

            def keep_att(i):
                act.wait_ge(sem("att_mm"), i + 1)
                act.activation(att[:, bass.ds(i, 1), :].rearrange("p a n -> p (a n)"), bank[4][:],
                               ACT.Copy).then_inc(sem("att_ready"), 1)

            act.wait_ge(sem("l0p_in"), 16)
            exps(0)
            with act.Fori(0, GROUPS - 1) as i:
                exps(i + 1)
                keep_att(i)
            keep_att(GROUPS - 1)
            for g in range(GROUPS):
                act.wait_ge(sem("turned_an"), g + 1)
                act.activation(T["ant"][:, g, :], bank[3 + g % 2][:], ACT.Copy).then_inc(sem("ant_ready"), 1)
            for g in range(GROUPS + 1):
                if g < GROUPS:
                    act.wait_ge(sem("turned_x1"), g + 1)
                    act.activation(cols(x1t, g), bank[5 + g % 2][:], ACT.Copy).then_inc(sem("x1t_ready"), 1)
                if g:
                    act.wait_ge(sem("logits_mm"), g)
                    act.activation(tiles(logits, g - 1), bank3(3 + (g - 1) % 2, NE), ACT.Copy).then_inc(
                        sem("logits_ready"), 1)
            act.wait_ge(sem("shifted_ready"), 1)
            act.activation(gates[:], gates[:], ACT.Exp).then_inc(sem("gates_exp"), 1)

            def shared_halves(g):
                for f in range(FB):
                    act.wait_ge(sem("hidden_mm"), g * FB + f + 1)
                    if not isinstance(g, int) or g:
                        act.wait_ge(sem("hidden_ready"), g * FB)
                    act.activation(hidden[:, FB + f, :], bank[2 + 2 * f][:], ACT.Silu)
                    act.activation(hidden[:, f, :], bank[3 + 2 * f][:], ACT.Copy).then_inc(sem("hidden_read"), 1)

            def keep_shared(g):
                act.wait_ge(sem("shared_mm"), g + 1)
                act.activation(tiles_at(shared, g), bank3(0), ACT.Copy).then_inc(sem("shared_ready"), 1)

            shared_halves(0)
            keep_shared(0)
            act.wait_ge(sem("b_index"), 1)
            act.activation(R["bi"], logits_i, ACT.Copy).then_inc(sem("bi_ready"), 1)
            with act.Fori(1, GROUPS) as g:
                shared_halves(g)
                keep_shared(g)

            def silu_of(G, u, j):
                n = G * EG + j
                act.wait_ge(sem("gate_mm"), n + 1)
                if j > 1:
                    act.wait_ge(sem("prod_g_ready"), n - 1)
                act.activation(E["silu"][:, j % 2, :], bank[2 * (j % 2) + 1][:, 0:FB * CAP], ACT.Silu).then_inc(
                    sem("silu_ready"), 1)

            def keep_result(G, u, j):
                act.wait_ge(sem("y_mm"), G * EG + j + 1)
                if j == 0 and not (isinstance(G, int) and G < 2):
                    act.wait_ge(sem("turned_y"), 3 * (G - 1))
                act.activation(E["yt"][:, u].rearrange("p b (a e) -> p b a e", e=EG)[:, :, :, j],
                               bank[4 + j % 2][:, 0:CAP].rearrange("p (b a) -> p b a", a=RA), ACT.Copy).then_inc(
                    sem("yt_ready"), 1)

            def expert_group(G, u):
                for j in range(EG):
                    silu_of(G, u, j)
                    if j:
                        keep_result(G, u, j - 1)
                keep_result(G, u, EG - 1)

            expert_group(0, 0)
            expert_group(1, 1)
            with act.Fori(1, NEG // 2) as m:
                for u in range(2):
                    expert_group(2 * m + u, u)

            def norm1_columns(n, g, l):
                act.wait_ge(sem("turned1"), n + 1)
                act.sem_inc(sem("act_steps"))
                act.activation(B["ht"][:, g], bank[0][:], ACT.Identity, bias=layer_col(l, 2),
                               scale=layer_col(l, 1)).then_inc(sem("ht_ready"), 1)

            def exp_q(n, k, g, l):
                act.wait_ge(sem("q1_mm"), n + 1)
                if k >= 2:
                    act.wait_ge(sem("q1_ready"), n - 1)
                act.sem_inc(sem("act_steps"))
                act.activation(B["eq"][:, g % 2], bank[2][:], ACT.Exp, bias=layer_col(l, 0)).then_inc(
                    sem("eq_ready"), 1)

            def exp_k(n, k, g):
                act.wait_ge(sem("z_ready"), 2 * (n + 1))
                if k >= 2:
                    act.wait_ge(sem("kp_ready"), n - 1)
                act.activation(B["ek"][:, g % 2], zrow(g)[:, :, 0:D], ACT.Exp, bias=minus_one[:]).then_inc(
                    sem("ek_ready"), 1)

            def attention_columns(n, g):
                act.wait_ge(sem("turned2"), n + 1)
                act.activation(B["ht"][:, g], bank[1][:], ACT.Copy).then_inc(sem("at_ready"), 1)

            def norm2_columns(n, g, l):
                act.wait_ge(sem("turned3"), n + 1)
                act.sem_inc(sem("act_steps"))
                act.activation(B["ht"][:, g], bank[0][:], ACT.Identity, bias=layer_col(l, 4),
                               scale=layer_col(l, 3)).then_inc(sem("h2t_ready"), 1)

            def relus(n, g, l):
                for f in range(FFB):
                    act.wait_ge(sem("up_mm"), FFB * n + f + 1)
                    act.sem_inc(sem("act_steps"))
                    act.activation(B["relu"][:, g % 2, f], bank[(3, 4, 6, 7)[f]][:], ACT.Relu,
                                   bias=layer_col(l, 5 + f)).then_inc(sem("relu_ready"), 1)

            def gelus(g):
                act.wait_ge(sem("turned_x3"), g + 1)
                act.activation(B["ht"][:, g], bank[1][:], ACT.Copy).then_inc(sem("x3t_ready"), 1)
                if g >= 2:
                    act.wait_ge(sem("chosen"), g - 1)
                act.wait_ge(sem("score_mm"), g + 1)
                act.activation(scores[:, g % 2], bank[2][:], ACT.Copy).then_inc(sem("scores_ready"), 1)
                act.wait_ge(sem("block_mm"), g + 1)
                act.activation(B["q"][:, g].rearrange("p (i d) -> p i d", d=D), bank3(0),
                               ACT.Gelu_apprx_tanh).then_inc(sem("gelu_ready"), 1)
                act.activation(B["kp"][:, g], tiles(state, g), ACT.Copy, scale=2.0).then_inc(sem("twice_ready"), 1)

            def slot(t, k, l):
                g = k % GROUPS
                if item(k, 0):
                    norm1_columns(t, g, layer_of(l, k, 0))
                    exp_q(t, k, g, layer_of(l, k, 0))
                if item(k, 1):
                    attention_columns(t - 1, (g - 1) % GROUPS)
                if item(k, 2):
                    norm2_columns(t - 2, (g - 2) % GROUPS, layer_of(l, k, 2))
                if item(k, 0):
                    exp_k(t, k, g)
                if item(k, 2):
                    relus(t - 2, (g - 2) % GROUPS, layer_of(l, k, 2))
                if ITEMS <= k < ITEMS + GROUPS:
                    gelus(k - ITEMS)

            act.wait_ge(sem("cols_in"), 16)
            pipeline(act, slot)

        @block.gpsimd
        def _(pool):
            pool.memset(zeros[:], 0.0).then_inc(sem("zeros_ready"), 1)
            pool.memset(new_tile[:], 1.0).then_inc(sem("pool_consts"), 1)
            pool.memset(new_token[:], 1.0).then_inc(sem("pool_consts"), 1)
            pool.wait_ge(sem("pool_consts"), 2)
            pool.memset(new_tile[:].rearrange("p (e i) -> p e i", i=TILES)[:, :, 0:1], 0.0)
            pool.memset(new_token[:].rearrange("p (i e) -> p i e", e=NE)[:, :, 0:1], 0.0).then_inc(
                sem("starts_ready"), 1)
            pool.memset(minus_half[:], -0.5).then_inc(sem("pool_consts"), 1)
            pool.memset(minus_one[:], -1.0).then_inc(sem("minus_one_ready"), 1)
            pool.wait_ge(sem("pool_consts"), 3)
            pool.wait_ge(sem("xr_in"), 16)
            pool.wait_ge(sem("bo_in"), 16)
            with pool.Fori(0, GROUPS) as i:
                pool.wait_ge(sem("ksum_ready"), i + 1)
                pool.sem_inc(sem("pool_steps"))
                pool.tensor_tensor(dk[:, bass.ds(i, 1), :].rearrange("p a n -> p (a n)"), ksum, q_of(i),
                                   ALU.mult).then_inc(sem("dk_ready"), 1)
                for e in range(DH):
                    pool.wait_ge(sem("run_ready"), i * DH + e + 1)
                    pool.sem_inc(sem("pool_steps"))
                    pool.tensor_tensor(prod[:, e, :], run[:, e % 2, :], q_of(i), ALU.mult).then_inc(
                        sem("prod_ready"), 1)
            for g in range(GROUPS):
                pool.tensor_tensor(tiles(xr, g), tiles(xr, g), bo_bc[:].unsqueeze(1).to_broadcast([P, GT, D]),
                                   ALU.add).then_inc(sem("xr_ready"), 1)
            for g in range(GROUPS):
                norm_rstd(pool, "first", g, g)

            def shared_products(g):
                for f in range(FB):
                    pool.wait_ge(sem("hidden_read"), g * FB + f + 1)
                    if not isinstance(g, int) or g:
                        pool.wait_ge(sem("shared_mm"), g)
                    pool.tensor_tensor(hidden[:, 2 * FB + f, :], hidden[:, f, :], hidden[:, FB + f, :],
                                       ALU.mult).then_inc(sem("hidden_ready"), 1)

            shared_products(0)
            pool.wait_ge(sem("masks_ready"), 1)
            pool.tensor_tensor(gates[:].rearrange("p i e -> p (i e)"), gates[:].rearrange("p i e -> p (i e)"),
                               R["mask"], ALU.mult).then_inc(sem("gates_masked"), 1)
            pool.wait_ge(sem("gates_masked"), 1)
            pool.wait_ge(sem("top_sum_ready"), 1)
            pool.tensor_tensor(gates[:], gates[:], route[:, 80:96].unsqueeze(2).to_broadcast([P, TILES, NE]),
                               ALU.mult).then_inc(sem("gates_ready"), 1)
            with pool.Fori(1, GROUPS) as g:
                shared_products(g)

            def gather(G, u, m):
                if not (isinstance(G, int) and G < 2):
                    pool.wait_ge(sem("slot_gate_ready"), G - 1)
                pool.wait_ge(sem("indices_ready"), m + 1)
                pool.tensor_copy(gather_ix[:, u:u + 1, :], gather_all[:, bass.ds(G, 1), :]).then_inc(
                    sem("gather_ix_ready"), 1)
                pool.wait_ge(sem("gather_ix_ready"), G + 1)
                pool.sem_inc(sem("gather_begun"))
                pool.wait_ge(sem("rows_out"), 32)
                for b in range(RB):
                    pool.indirect_dma_start(got[u][:, b, :], None, dispatch_dram[:, :],
                                            bass.IndirectOffsetOnAxis(ap=gather_ix[:, u, b:b + 1], axis=0)).then_inc(
                        sem(f"gathered{u}"), 16)

            def scatter(G, u, m):
                if not isinstance(m, int) or m:
                    pool.wait_ge(sem(f"scattered{u}"), 16 * RB * m)
                pool.tensor_copy(scatter_ix[:, u:u + 1, :], scatter_all[:, bass.ds(G, 1), :]).then_inc(
                    sem("scatter_ix_ready"), 1)
                pool.wait_ge(sem("scatter_ix_ready"), G + 1)
                pool.wait_ge(sem("turned_y_read"), 3 * (G + 1))
                pool.sem_inc(sem("scatter_begun"))
                pool.wait_ge(sem("zeroed"), 16 * TOK * TOPK // (8 * P))
                for b in range(RB):
                    pool.indirect_dma_start(returned_dram[:, :],
                                            bass.IndirectOffsetOnAxis(ap=scatter_ix[:, u, b:b + 1], axis=0),
                                            E["back"][:, u, b, :], None, bounds_check=TOK * TOPK - 1,
                                            oob_is_err=False).then_inc(sem(f"scattered{u}"), 16)

            gather(0, 0, 0)
            gather(1, 1, 0)
            for u in range(2):
                gather(u + 2, u, 1)
                scatter(u, u, 0)
            with pool.Fori(1, NEG // 2 - 1) as m:
                for u in range(2):
                    gather(2 * m + u + 2, u, m + 1)
                    scatter(2 * m + u, u, m)
            scatter(NEG - 2, 0, NEG // 2 - 1)
            for g in range(GROUPS):
                pool.wait_ge(sem("shared_ready"), GROUPS)
                pool.tensor_tensor(tiles(shared, g), tiles(shared, g), tiles(x1, g), ALU.add).then_inc(
                    sem("base_ready"), 1)
            scatter(NEG - 1, 1, NEG // 2 - 1)

            def row_of(l, k):
                return lrows[:, bass.ds(l, 1), D * k:D * k + D].to_broadcast([P, GT, D])

            def slot(t, k, l):
                g = k % GROUPS
                if k + 2 == 0:
                    norm_rstd(pool, "combine", 0, 0)
                if item(k, -1):
                    norm_rstd(pool, "norm1", t + 1, g + 1)
                    if 0 <= k + 2 < GROUPS:
                        norm_rstd(pool, "combine", k + 2, k + 2)
                    pool.wait_ge(sem("x_ready"), t + 2)
                    pool.sem_inc(sem("pool_steps"))
                    pool.tensor_tensor(tiles(plus, (g + 1) % GROUPS), tiles(state, (g + 1) % GROUPS),
                                       row_of(layer_of(l, k, -1), 2), ALU.add).then_inc(sem("plus_bo"), 1)
                if 0 <= k - (ITEMS - 1) < GROUPS:
                    f = k - (ITEMS - 1)
                    norm_rstd(pool, "final", f, f)
                    pool.wait_ge(sem("fin_in"), 16)
                    pool.wait_ge(sem("x_ready"), ITEMS + f + 1)
                    pool.tensor_tensor(tiles(plus, f), tiles(x2, f),
                                       fin_rows[:, D:2 * D].unsqueeze(1).to_broadcast([P, GT, D]), ALU.add).then_inc(
                        sem("plus_lnf"), 1)
                if item(k, 1):
                    norm_rstd(pool, "norm2", t - 1, g - 1)
                    pool.wait_ge(sem("mid_ready"), t)
                    pool.sem_inc(sem("pool_steps"))
                    pool.tensor_tensor(tiles(plus, (g - 1) % GROUPS), tiles(state, (g - 1) % GROUPS),
                                       row_of(layer_of(l, k, 1), 3), ALU.add).then_inc(sem("plus_b2"), 1)
                if 0 <= k - (ITEMS - 1) < GROUPS:
                    norm_rstd(pool, "second", f, f)
                if 0 <= k - (ITEMS + 1) < GROUPS:
                    norm_rstd(pool, "last", k - (ITEMS + 1), k - (ITEMS + 1))

            pool.wait_ge(sem("rows_in"), 16)
            pipeline(pool, slot)

        @block.vector
        def _(v):
            ch = Chain(v, sem("vector_step"))
            v.wait_ge(sem("l0p_in"), 16)
            v.tensor_scalar(bq1[:], l0ps[:, 0:2], 1.0, None, ALU.add).then_inc(sem("bq1_ready"), 1)
            v.wait_ge(sem("bq1_ready"), 1)
            v.wait_ge(sem("consts_in"), 16)
            v.tensor_copy(tri16[:], C[:, C_TRI:C_TRI + P]).then_inc(sem("tri_ready"), 1)
            v.tensor_copy(ones16[:], C[:, C_ONES:C_ONES + P]).then_inc(sem("tri_ready"), 1)
            for _ in v_banks:
                v.sem_inc(sem("kv_ready"))
            with v.Fori(0, GROUPS) as i:
                ch.loop(i, 1)
                v.wait_ge(sem("exp_ready"), i + 1)
                e1 = ch.did(v.tensor_scalar(eqk[:], eqk[:], 1.0, None, ALU.min))
                ch.after(e1)
                v.scalar_tensor_tensor(q_of(i), bank[0][:], bq1[:, 0:1], eqk[:, 0, :], ALU.add, ALU.max).then_inc(
                    sem("q_ready"), 1)
                v.scalar_tensor_tensor(k0, bank[1][:], bq1[:, 1:2], eqk[:, 1, :], ALU.add, ALU.max).then_inc(
                    sem("k_ready"), 1)
                v.wait_ge(sem("k_ready"), i + 1)

                def kv_of(e):
                    v.wait_ge(sem("v_mm"), i * DH + e + 1)
                    if e >= 2:
                        v.wait_ge(sem("run_ready"), i * DH + e - 1)
                    v.scalar_tensor_tensor(kv[:, e % 2, :], bank[v_banks[e % 4]][:], l0ps[:, 2 + e:3 + e], k0,
                                           ALU.add, ALU.mult).then_inc(sem("kv_ready"), 1)

                kv_of(0)
                v.tensor_tensor_scan(ksum, reset, k0, 0.0, ALU.mult, ALU.add).then_inc(sem("ksum_ready"), 1)
                for e in range(DH):
                    if e + 1 < DH:
                        kv_of(e + 1)
                    v.wait_ge(sem("kv_ready"), len(v_banks) + i * DH + e + 1)
                    if e >= 2:
                        v.wait_ge(sem("prod_ready"), i * DH + e - 1)
                    v.tensor_tensor_scan(run[:, e % 2, :], reset, kv[:, e % 2, :], 0.0, ALU.mult,
                                         ALU.add).then_inc(sem("run_ready"), 1)
            ch.end_loop(GROUPS)
            v.wait_ge(sem("den_mm"), 1)
            d = ch.did(v.tensor_scalar(den, bank[7][:, 0:TILES * HEADS].rearrange("p (g n) -> p g n", g=GROUPS),
                                       EPS_ATTN, None, ALU.max))
            ch.after(d)
            d = ch.did(v.reciprocal(rden, den))
            ch.after(d)
            for g in range(GROUPS):
                v.wait_ge(sem("turned_att"), g + 1)
                r = rden[:, g, :].rearrange("p (i h) -> p i h", h=HEADS).unsqueeze(2).to_broadcast([P, GT, DH, HEADS])
                if g == 0:
                    v.wait_ge(sem("att_mm"), GROUPS)
                v.tensor_tensor(T["an"][:, g, :].rearrange("p (i e h) -> p i e h", e=DH, h=HEADS),
                                bank[5 + g % 2][:].rearrange("p (i e h) -> p i e h", e=DH, h=HEADS), r,
                                ALU.mult).then_inc(sem("an_ready"), 1)
            xs = T["xs"].rearrange("p g (i d) -> p g i d", d=D)
            for g in range(GROUPS + 1):
                if g < GROUPS:
                    v.wait_ge(sem("wo_mm"), g + 1)
                    v.wait_ge(sem("xr_ready"), g + 1)
                    v.tensor_tensor(xs[:, g], bank3(g % 2), tiles(xr, g), ALU.add).then_inc(sem("xs_ready"), 1)
                    v.wait_ge(sem("xs_ready"), g + 1)
                    norm_stats(v, ch, "first", g, g, xs[:, g])
                if g:
                    norm_apply(v, "first", g - 1, g - 1, xs[:, g - 1], tiles(x1, g - 1), "x1_ready")

            top, total, inv, top8 = route[:, 0:16], route[:, 16:32], route[:, 32:48], route[:, 48:64]
            over = lambda a: a.unsqueeze(2).to_broadcast([P, TILES, NE])
            v.wait_ge(sem("logits_ready"), GROUPS)
            ch.after(ch.did(v.tensor_reduce(top, logits[:], AX.X, ALU.max)))
            v.tensor_tensor(gates[:], logits[:], over(top), ALU.subtract).then_inc(sem("shifted_ready"), 1)
            v.wait_ge(sem("gates_exp"), 1)
            ch.after(ch.did(v.tensor_reduce(total, gates[:], AX.X, ALU.add)))
            ch.after(ch.did(v.reciprocal(inv, total)))
            ch.after(ch.did(v.tensor_tensor(gates[:], gates[:], over(inv), ALU.mult)))
            for i in range(TILES):
                k = ch.did(v.max(best8[:, i, :], gates[:, i, :]))
            ch.after(k)
            for i in range(TILES):
                k = ch.did(v.match_replace(logits[:, i, :], best8[:, i, :], gates[:, i, :], -1.0))
            ch.after(k)
            lg = logits[:].rearrange("p i e -> p (i e)")
            mask, mask_ei = R["mask"], R["mask_ei"]
            v.tensor_scalar(mask, lg, 0.0, None, ALU.is_lt).then_inc(sem("mask_parts"), 1)
            v.tensor_scalar(mask_ei.rearrange("p (e i) -> p i e", i=TILES), logits[:], 0.0, None, ALU.is_lt).then_inc(
                sem("mask_parts"), 1)
            ch.after(ch.did(v.tensor_reduce(top8, best8[:], AX.X, ALU.add)))
            v.wait_ge(sem("starts_ready"), 1)
            v.tensor_tensor_scan(R["upto_ei"], new_tile[:], mask_ei, 0.0, ALU.mult, ALU.add).then_inc(
                sem("masks_ready"), 1)
            ch.after(ch.did(v.tensor_scalar(route[:, 64:80], top8, float(np.finfo(np.float32).eps), None, ALU.max)))
            v.reciprocal(route[:, 80:96], route[:, 64:80]).then_inc(sem("top_sum_ready"), 1)
            v.tensor_tensor_scan(R["place"], new_token[:], mask, 0.0, ALU.mult, ALU.add)
            k = ch.did(v.tensor_copy(R["token"].rearrange("p (i e) -> p i e", e=NE), over(C[:, C_TOK:C_TOK + TILES])))
            v.wait_ge(sem("rank_mm"), 1)
            v.wait_ge(sem("zeroed"), 16 * TOK * TOPK // (8 * P))
            for h in range(2):
                hs = slice(512 * h, 512 * h + 512)
                ins = v.scalar_tensor_tensor(scratch[:, hs], bank[h][:], 1.0, mask[:, hs], ALU.add, ALU.mult)
            ins.then_inc(sem("rank_read"), 1)
            v.wait_ge(sem("rank_read"), 1)
            scr_i = scratch[:].bitcast(I32)
            ch.after(ch.did(v.tensor_scalar(logits_i, scratch[:], -1.0, None, ALU.add)))
            k1 = ch.did(v.tensor_scalar(scr_i, logits_i, RA - 1, None, ALU.bitwise_and))
            ch.after(k1)
            v.tensor_scalar(logits_i, logits_i, 4, None, ALU.arith_shift_right).then_inc(sem("b_index"), 1)
            ch.after(ch.did(v.tensor_copy(R["ai"], scr_i)))
            v.wait_ge(sem("bi_ready"), 1)
            a_out = R["a"].rearrange("p i (g a e) -> p i g a e", a=RA, e=EG)
            a_in = R["ai"].rearrange("p (i g e) -> p i g e", g=NEG, e=EG)
            by_tile = lambda t: t.rearrange("p (i e) -> p i e", i=TILES)
            b_in, token, place = by_tile(R["bi"]), by_tile(R["token"]), by_tile(R["place"])
            b_out = R["b"].rearrange("p b (i e) -> p b i e", e=NE)
            here = [by_tile(zeros[:, 256 + 128 * h:384 + 128 * h].bitcast(F16)) for h in range(3)]
            own = C[:, C_EXP:C_EXP + EG]

            def one_hots(q):
                experts = bass.ds(2 * EG * q, 2 * EG)
                for a in range(RA):
                    v.tensor_scalar(a_out[:, :, bass.ds(2 * q, 2), a, :], a_in[:, :, bass.ds(2 * q, 2), :], float(a),
                                    None, ALU.is_equal)
                k = ch.did(v.tensor_scalar(here[0], b_in[:, :, experts], 0.0, None, ALU.is_equal))
                for b in range(RB):
                    ch.after(k)
                    if b + 1 < RB:
                        k = ch.did(v.tensor_scalar(here[(b + 1) % 3], b_in[:, :, experts], float(b + 1), None,
                                                   ALU.is_equal))
                    v.tensor_tensor(b_out[:, b, :, experts], here[b % 3], token[:, :, experts], ALU.mult)
                    ins = v.tensor_tensor(b_out[:, RB + b, :, experts], here[b % 3], place[:, :, experts], ALU.mult)
                ins.then_inc(sem("one_hots_ready"), 1)

            def indices(q):
                v.wait_ge(sem("slots_mm"), q + 1)
                v.tensor_tensor(picked[:], bank[1][:, 0:4 * RB * EG].rearrange("p (u b e) -> p u b e", u=2, e=EG),
                                own.unsqueeze(1).unsqueeze(1).to_broadcast([P, 2, 2 * RB, EG]), ALU.mult).then_inc(
                    sem("slots_read"), 1)
                v.wait_ge(sem("slots_read"), q + 1)
                ch.after(ch.did(v.tensor_reduce(slots[:, bass.ds(2 * q, 2)].rearrange("p g t b -> p g (t b)"), picked[:], AX.X,
                                                ALU.add)))
                tok1, place1 = slots[:, bass.ds(2 * q, 2), 0, :], slots[:, bass.ds(2 * q, 2), 1, :]
                t8, pad = (zeros[:, 32 * h:32 * h + 2 * RB].rearrange("p (g b) -> p g b", b=RB) for h in range(2))
                v.tensor_scalar(gather_all[:, bass.ds(2 * q, 2)], tok1, -1.0, 0.0, ALU.add, ALU.max)
                v.scalar_tensor_tensor(t8, tok1, float(TOPK), place1, ALU.mult, ALU.add)
                ch.after(ch.did(v.tensor_scalar(pad, tok1, 0.0, float(SKIP + TOPK + 1), ALU.is_equal, ALU.mult)))
                v.scalar_tensor_tensor(scatter_all[:, bass.ds(2 * q, 2)], t8, -float(TOPK + 1), pad, ALU.add,
                                       ALU.add).then_inc(sem("indices_ready"), 1)

            one_hots(0)
            with v.Fori(1, NEG // 2) as q:
                ch.loop(q - 1, RB + 2)
                v.wait_ge(sem("one_hots_ready"), q)
                one_hots(q)
                indices(q - 1)
            ch.end_loop(NEG // 2 - 1)
            indices(NEG // 2 - 1)

            def columns_of(G, u, m):
                for c in range(3):
                    nb = min(4, RB - 4 * c)
                    v.wait_ge(sem("turned_x"), 3 * G + c + 1)
                    v.tensor_copy(E["xt"][:, u].rearrange("p e (b a) -> p b a e", a=RA)[:, 4 * c:4 * c + nb],
                                  bank[7 - c % 2][:, 0:P * nb].rearrange("p (b a e) -> p b a e", a=RA, e=EG)).then_inc(
                        sem("xt_ready"), 1)
                v.tensor_tensor(picked_gate[:], got[u][:, :, bass.ds(D + G * EG, EG)],
                                own.unsqueeze(1).to_broadcast([P, RB, EG]), ALU.mult).then_inc(sem("picked_gates"), 1)
                v.wait_ge(sem("picked_gates"), G + 1)
                v.tensor_reduce(slot_gate[:, u, :], picked_gate[:], AX.X, ALU.add).then_inc(sem("slot_gate_ready"), 1)

            def product(G, u, j):
                n = G * EG + j
                v.wait_ge(sem("silu_ready"), n + 1)
                v.wait_ge(sem("value_mm"), n + 1)
                if j > 1:
                    v.wait_ge(sem("y_mm"), n - 1)
                v.tensor_tensor(E["prod"][:, j % 2, :], bank[2 * (j % 2)][:, 0:FB * CAP], E["silu"][:, j % 2, :],
                                ALU.mult).then_inc(sem("prod_g_ready"), 1)

            def rows_back(G, u, m):
                if not isinstance(m, int) or m:
                    v.wait_ge(sem(f"scattered{u}"), 16 * RB * m)
                v.wait_ge(sem("slot_gate_ready"), G + 1)
                for c in range(3):
                    nb = min(4, RB - 4 * c)
                    v.wait_ge(sem("turned_y"), 3 * G + c + 1)
                    v.tensor_tensor(E["back"][:, u, 4 * c:4 * c + nb, :],
                                    bank[6 + c % 2][:, 0:P * nb].rearrange("p (b d) -> p b d", d=D),
                                    slot_gate[:, u, 4 * c:4 * c + nb].unsqueeze(2).to_broadcast([P, nb, D]),
                                    ALU.mult).then_inc(sem("turned_y_read"), 1)

            def expert_group(G, u, m, more):
                for j in range(EG):
                    product(G, u, j)
                if more:
                    columns_of(G + 1, 1 - u, m)
                rows_back(G, u, m)

            columns_of(0, 0, 0)
            for u in range(2):
                expert_group(u, u, 0, True)
            with v.Fori(1, NEG // 2 - 1) as m:
                for u in range(2):
                    expert_group(2 * m + u, u, m, True)
            expert_group(NEG - 2, 0, NEG // 2 - 1, True)
            expert_group(NEG - 1, 1, NEG // 2 - 1, False)

            H = B["h"]
            pe_rows = C[:, C_PE:C_PE + 2 * D].rearrange("p (s d) -> p s d", s=2)
            root_d = float(np.float32(np.sqrt(np.float32(D))))
            blk = C[:, C_BLK:C_BLK + P]

            def collect(g):
                v.wait_ge(sem(f"returned_in{g}"), 16 * GT)
                for t in range(GT):
                    k = ch.did(v.tensor_reduce(H[:, g, t, :], spare[GT * g + t].rearrange("p (k d) -> p d k", d=D), AX.X,
                                               ALU.add))
                ch.after(k)
                v.wait_ge(sem("base_ready"), g + 1)
                ch.after(ch.did(v.tensor_tensor(H[:, g], H[:, g], tiles(shared, g), ALU.add)))
                norm_stats(v, ch, "combine", g, g, H[:, g])

            def begin_state(g):
                norm_apply(v, "combine", g, g, H[:, g], tiles(x2, g), "x2_ready")
                v.wait_ge(sem("x2_ready"), g + 1)
                for h in range(2):
                    ins = v.scalar_tensor_tensor(state[:, GT * g + 2 * h:GT * g + 2 * h + 2, :],
                                                 x2[:, GT * g + 2 * h:GT * g + 2 * h + 2, :], root_d, pe_rows,
                                                 ALU.mult, ALU.add)
                ins.then_inc(sem("x_ready"), 1)

            def features(n, g, l):
                for h in range(2):
                    v.wait_ge(sem("kv1_mm"), 2 * n + h + 1)
                    v.tensor_tensor(zrow(g)[:, 2 * h:2 * h + 2, 0:2 * D],
                                    bank[3 + h][:].rearrange("p (i n) -> p i n", i=2),
                                    lrows[:, bass.ds(l, 1), 0:2 * D].to_broadcast([P, 2, 2 * D]), ALU.add).then_inc(
                        sem("z_ready"), 1)
                v.wait_ge(sem("eq_ready"), n + 1)
                ch.after(ch.did(v.tensor_scalar(B["eq"][:, g % 2], B["eq"][:, g % 2], 1.0, None, ALU.min)))
                v.scalar_tensor_tensor(B["q"][:, g], bank[2][:], bq_up[:, bass.ds(l, 1)], B["eq"][:, g % 2], ALU.add,
                                       ALU.max).then_inc(sem("q1_ready"), 1)

            def features_k(n, g):
                v.wait_ge(sem("ek_ready"), n + 1)
                v.scalar_tensor_tensor(B["kp"][:, g], B["ek"][:, g % 2], 1.0, zrow(g)[:, :, 0:D], ALU.min,
                                       ALU.max).then_inc(sem("kp_ready"), 1)

            def mask_kv(n, g):
                v.wait_ge(sem("kvsum_mm"), n + 1)
                kvs = bank[5][:, 0:2 * (D + 1)].rearrange("p (b n) -> p b n", b=2)
                v.tensor_tensor(kvm(g)[:, :, 0:D], kvs[:, :, 0:D], blk.unsqueeze(1).to_broadcast([P, 2, D]), ALU.mult)
                v.tensor_tensor(kvm(g)[:, :, D:D + HEADS], head.unsqueeze(1).to_broadcast([P, 2, HEADS]),
                                kvs[:, :, D:D + 1].to_broadcast([P, 2, HEADS]), ALU.mult).then_inc(
                    sem("kvm_ready"), 1)

            def divide(n, g):
                s = g % 2
                v.wait_ge(sem("num_mm"), n + 1)
                parts = [bank[6 + h][:, 0:2 * (D + HEADS)].rearrange("p (i n) -> p i n", i=2) for h in range(2)]
                for h in range(2):
                    k = ch.did(v.tensor_scalar(den1[:, s, 2 * h:2 * h + 2, :], parts[h][:, :, D:D + HEADS],
                                               EPS_ATTN, None, ALU.add))
                ch.after(k)
                ch.after(ch.did(v.reciprocal(rden1[:, s], den1[:, s])))
                for h in range(2):
                    ins = v.tensor_tensor(
                        H[:, g, 2 * h:2 * h + 2, :].rearrange("p i (h d) -> p i h d", d=DH),
                        parts[h][:, :, 0:D].rearrange("p i (h d) -> p i h d", d=DH),
                        rden1[:, s, 2 * h:2 * h + 2, :].unsqueeze(3).to_broadcast([P, 2, HEADS, DH]), ALU.mult)
                ins.then_inc(sem("an1_ready"), 1)

            def residual1(n, g):
                v.wait_ge(sem("out1_mm"), n + 1)
                v.wait_ge(sem("plus_bo"), n + 1)
                v.tensor_tensor(tiles(state, g), bank3(2), tiles(plus, g), ALU.add).then_inc(sem("mid_ready"), 1)
                v.wait_ge(sem("mid_ready"), n + 1)
                norm_stats(v, ch, "norm2", n, g, tiles(state, g))

            def residual2(n, g):
                v.wait_ge(sem("down_mm"), n + 1)
                v.wait_ge(sem("plus_b2"), n + 1)
                v.tensor_tensor(tiles(state, g), bank3(5), tiles(plus, g), ALU.add).then_inc(sem("x_ready"), 1)

            def apply_final(g):
                norm_apply(v, "final", g, g, tiles(state, g), H[:, g], "hf_ready")
                v.wait_ge(sem("hf_ready"), g + 1)
                v.wait_ge(sem("fin_in"), 16)
                ch.after(ch.did(v.tensor_tensor(H[:, g], H[:, g], fin_rows[:, 0:D].unsqueeze(1).to_broadcast([P, GT, D]),
                                                ALU.mult)))
                v.wait_ge(sem("plus_lnf"), g + 1)
                ch.after(ch.did(v.tensor_tensor(H[:, g], H[:, g], tiles(plus, g), ALU.add)))
                norm_stats(v, ch, "second", g, g, H[:, g])

            before = C[:, C_BEFORE:C_BEFORE + 2 * SEQ].rearrange("p (h n) -> p h n", h=2)
            own_s, higher, equal, place_s = (small[:, 800 + 16 * k:816 + 16 * k] for k in range(4))
            chosen_m = small[:, 864:880]
            junk = B["ek"].rearrange("p s i d -> p (s i d)")

            def choose(g):
                gs = slice(GT * g, GT * g + GT)
                v.wait_ge(sem("scores_ready"), g + 1)
                ch.after(ch.did(v.tensor_tensor(B["eq"][:, g % 2].rearrange("p (i n) -> p i n", i=GT),
                                                scores[:, g % 2].rearrange("p (i n) -> p i n", i=GT),
                                                ident.unsqueeze(1).to_broadcast([P, GT, P]), ALU.mult)))
                ch.after(ch.did(v.tensor_reduce(own_s[:, gs], B["eq"][:, g % 2].rearrange("p (i n) -> p i n", i=GT), AX.X,
                                                ALU.add)))
                for t in range(GT):
                    i = GT * g + t
                    seq = scores[:, g % 2, SEQ * (t // 2):SEQ * (t // 2 + 1)]
                    v.tensor_scalar(junk[:, 0:SEQ] if t % 2 else junk[:, SEQ:2 * SEQ], seq, own_s[:, i:i + 1], None,
                                    ALU.is_gt, ALU.add, accum_out=higher[:, i:i + 1])
                    ch.after(ch.did(v.scalar_tensor_tensor(
                        junk[:, 2 * SEQ:3 * SEQ] if t % 2 else junk[:, 3 * SEQ:4 * SEQ], seq, own_s[:, i:i + 1],
                        before[:, t % 2, :], ALU.is_equal, ALU.mult, accum_out=equal[:, i:i + 1])))
                ch.after(ch.did(v.tensor_tensor(place_s[:, gs], higher[:, gs], equal[:, gs], ALU.add)))
                v.tensor_scalar(chosen_m[:, gs], place_s[:, gs], float(KEEP), None, ALU.is_lt).then_inc(sem("chosen"), 1)

            def blend(g):
                v.wait_ge(sem("gelu_ready"), g + 1)
                v.wait_ge(sem("twice_ready"), g + 1)
                v.wait_ge(sem("chosen"), g + 1)
                gl = B["q"][:, g].rearrange("p (i d) -> p i d", d=D)
                ch.after(ch.did(v.tensor_tensor(gl, gl, tiles(state, g), ALU.add)))
                for t in range(GT):
                    i = GT * g + t
                    k = ch.did(v.copy_predicated(B["kp"][:, g, t, :], chosen_m[:, i:i + 1].bitcast(U32).to_broadcast([P, D]),
                                                 gl[:, t, :]))
                ch.after(k)
                norm_stats(v, ch, "last", g, g, B["kp"][:, g])

            def slot(t, k, l):
                g = k % GROUPS
                if item(k, 1):
                    mask_kv(t - 1, (g - 1) % GROUPS)
                if item(k, 2):
                    n2, g2 = t - 2, (g - 2) % GROUPS
                    norm_apply(v, "norm2", n2, g2, tiles(state, g2), H[:, g2], "h2_ready")
                if item(k, 1):
                    divide(t - 1, (g - 1) % GROUPS)
                if ITEMS <= k < ITEMS + GROUPS:
                    f = k - ITEMS
                    norm_apply(v, "second", f, f, H[:, f], tiles(state, f), "x3_ready")
                if item(k, 0):
                    features(t, g, layer_of(l, k, 0))
                    features_k(t, g)
                if item(k, 3):
                    residual2(t - 3, (g - 3) % GROUPS)
                if 0 <= k + 1 < GROUPS:
                    begin_state(k + 1)
                if item(k, -1):
                    g1 = (g + 1) % GROUPS
                    v.wait_ge(sem("x_ready"), t + 2)
                    norm_stats(v, ch, "norm1", t + 1, g1, tiles(state, g1))
                if 0 <= k - (ITEMS - 1) < GROUPS:
                    f = k - (ITEMS - 1)
                    v.wait_ge(sem("x_ready"), ITEMS + f + 1)
                    norm_stats(v, ch, "final", f, f, tiles(state, f))
                if item(k, 1):
                    residual1(t - 1, (g - 1) % GROUPS)
                if 0 <= k + 2 < GROUPS:
                    collect(k + 2)
                if item(k, -1):
                    norm_apply(v, "norm1", t + 1, g1, tiles(state, g1), H[:, g1], "h1_ready")
                if 0 <= k - (ITEMS - 1) < GROUPS:
                    apply_final(f)
                if 0 <= k - (ITEMS + 1) < GROUPS:
                    choose(k - (ITEMS + 1))
                    blend(k - (ITEMS + 1))
                    f = k - (ITEMS + 1)
                    norm_apply(v, "last", f, f, B["kp"][:, f], H[:, f], "out_ready")

            for u in range(2):
                v.wait_ge(sem(f"scattered{u}"), 16 * RB * NEG // 2)
            for g in range(GROUPS):
                v.memset(zrow(g)[:, :, 2 * D:Z], 1.0)
            v.wait_ge(sem("cols_in"), 16)
            v.wait_ge(sem("rows_in"), 16)
            v.tensor_scalar(bq_up[:], layer_cols[:, :, 0], 1.0, None, ALU.add)
            ch.after(ch.did(v.tensor_scalar(lrows[:, :, 0:D], lrows[:, :, 0:D], 1.0, None, ALU.add)))
            steps = GROUPS * (2 * 2 * GT + 1 + 3)

            def body(l):
                if l is None:
                    ch.end_loop(LAYERS - 1)
                else:
                    ch.loop(l - 1, steps)

            pipeline(v, slot, body)


def pack(inputs):
    a = {k: np.asarray(v) for k, v in inputs.items()}
    c = np.ascontiguousarray
    x = a["L0_attn_x"].reshape(TOK, D)
    wv = a["L0_attn_Wv"].T.reshape(D, HEADS, DH)
    vrep = [np.repeat(wv[:, :, e], DH, axis=1) for e in range(DH)]
    wo = a["L0_attn_Wo"].T.reshape(HEADS, DH, D).transpose(1, 0, 2).reshape(D, D)
    bv = a["L0_attn_bv"].reshape(HEADS, DH)
    l0p = np.stack([a["L0_attn_bq"], a["L0_attn_bk"]] + [np.repeat(bv[:, e], DH) for e in range(DH)], axis=1)
    sw2 = a["L0_ffn_shared_w2"].T.reshape(FB, P, D).transpose(1, 0, 2).reshape(P, FB * D)
    w1 = a["L0_ffn_expert_w1"].transpose(0, 2, 1)
    w2 = a["L0_ffn_expert_w2"].transpose(0, 2, 1).reshape(NE, FB, P, D).transpose(0, 2, 1, 3).reshape(NE, P, FB * D)
    lw2 = a["L1_attn_W2"].reshape(LAYERS, FFB, P, D).transpose(0, 2, 1, 3).reshape(LAYERS, P, FFB * D)
    b1 = a["L1_attn_b1"].reshape(LAYERS, FFB, P).transpose(0, 2, 1)
    cols = [a["L1_attn_" + n][:, :, None] for n in ("bq", "ln1_s", "ln1_b", "ln2_s", "ln2_b")]
    return {
        "cst": constants(),
        "xt0": c(x.T),
        "xr0": c(x.reshape(TILES, P, D).transpose(1, 0, 2)),
        "l0w": c(np.concatenate([a["L0_attn_Wq"].T, a["L0_attn_Wk"].T] + vrep + [wo], axis=1)),
        "l0p": c(l0p),
        "bo0": c(a["L0_attn_bo"]),
        "l0s": c(np.concatenate([a["L0_ffn_wg"].T, a["L0_ffn_shared_w1"].T, sw2], axis=1)),
        "ew": c(np.concatenate([w1, w2], axis=2)),
        "l1w": c(np.concatenate([a["L1_attn_Wq"], a["L1_attn_Wk"], a["L1_attn_Wv"], a["L1_attn_Wo"],
                                 a["L1_attn_W1"], lw2], axis=2)),
        "l1p": c(np.concatenate(cols + [b1], axis=2).transpose(1, 0, 2)),
        "l1r": c(np.stack([a["L1_attn_bk"], a["L1_attn_bv"], a["L1_attn_bo"], a["L1_attn_b2"]], axis=1)),
        "fin_r": c(np.stack([a["L1_attn_lnf_s"], a["L1_attn_lnf_b"]])),
        "mod_w": c(np.concatenate([np.repeat(a["L1_ffn_w_router"][:, None], P, axis=1), a["L1_ffn_w_block"]], axis=1)),
    }


def kernel(**inputs):
    from concourse import bacc
    from concourse.bass_utils import run_bass_kernel_spmd

    nc = bacc.Bacc("TRN2", target_bir_lowering=False, num_devices=1)
    arrays = {f"in_{k}": v for k, v in pack(inputs).items()}
    aps = [nc.dram_tensor(k, v.shape, mybir.dt.from_np(v.dtype), kind="ExternalInput").ap() for k, v in arrays.items()]
    out = nc.dram_tensor("out", (P, TILES, D), F32, kind="ExternalOutput").ap()
    program(nc, *aps, out)
    r = run_bass_kernel_spmd(nc, [arrays], core_ids=[0])
    got = r.results[0]["out"]
    return np.ascontiguousarray(got.transpose(1, 0, 2).reshape(BATCH, SEQ, D))
```

```python
from contextlib import ExitStack

import numpy as np

import concourse.bass as bass
from concourse import mybir

ALU = mybir.AluOpType
ACT = mybir.ActivationFunctionType
AX = mybir.AxisListType
F32 = mybir.dt.float32
F16 = mybir.dt.float16
I32 = mybir.dt.int32
U32 = mybir.dt.uint32

P = 128
D = 128
BATCH, SEQ = 8, 256
TOK = BATCH * SEQ
TILES = TOK // P
GT = 4
GROUP = GT * P
GROUPS = TOK // GROUP
HEADS, DH = 16, 8
NE, TOPK, CAP, FFN = 64, 8, 160, 384
FB = FFN // P
EG = 8
NEG = NE // EG
RA, RB = 16, 10
LAYERS, FF = 4, 512
FFB = FF // P
KEEP = int(SEQ * 0.75)
ARENA = 22528
EPS_LN, EPS_ATTN = 1e-5, 1e-6
ROUTED = D + NE
SKIP = 65536

C_RESET, C_HEAD, C_SEL = 0, GROUP, GROUP + HEADS
C_ID = C_SEL + 32 * DH
C_BLK, C_TRI, C_ONES, C_PE = (C_ID + P * k for k in range(1, 5))
C_EXP = C_PE + 2 * D
C_TOK = C_EXP + EG
C_BEFORE = C_TOK + TILES
C_ALL = C_BEFORE + 2 * SEQ


def constants():
    c = np.zeros((P, C_ALL), np.float32)
    r = np.arange(P)
    c[:, C_ID:C_ID + P] = np.eye(P)
    same_head = (r[:, None] // DH) == (r[None, :] // DH)
    c[:, C_BLK:C_BLK + P] = same_head
    c[:, C_HEAD:C_HEAD + HEADS] = (r[:, None] // DH) == np.arange(HEADS)[None, :]
    for e in range(DH):
        s = c[:, C_SEL + 32 * e:C_SEL + 32 * e + 32]
        s[:, 16 * (e % 2):16 * (e % 2) + 16] = c[:, C_HEAD:C_HEAD + HEADS]
    c[:, C_TRI:C_TRI + P] = (r[:, None] < r[None, :]) - 1.0
    c[:, C_ONES:C_ONES + P] = 1.0
    half = D // 2
    freq = np.exp(np.arange(half, dtype=np.float32) * np.float32(-np.log(10000.0) / (half - 1))).astype(np.float32)
    pos = (np.arange(SEQ, dtype=np.float32) + 1.0)[:, None] * freq[None, :]
    pe = np.concatenate([np.sin(pos), np.cos(pos)], axis=-1).astype(np.float32)
    c[:, C_PE:C_PE + 2 * D] = pe.reshape(2, P, D).transpose(1, 0, 2).reshape(P, 2 * D)
    c[:, C_EXP:C_EXP + EG] = (r[:, None] % EG) == np.arange(EG)[None, :]
    c[:, C_TOK:C_TOK + TILES] = r[:, None] + P * np.arange(TILES)[None, :] + 1.0
    for h in range(2):
        c[:, C_BEFORE + SEQ * h:C_BEFORE + SEQ * h + SEQ] = np.arange(SEQ)[None, :] < P * h + r[:, None]
    c[:, C_RESET:C_RESET + GROUP] = (np.arange(GROUP) % SEQ != 0)
    return c


class Chain:

    def __init__(self, eng, sem):
        self.eng, self.sem, self.n, self.off = eng, sem, 0, 0

    def did(self, ins):
        ins.then_inc(self.sem, 1)
        self.n += 1
        return self.off + self.n

    def after(self, number):
        self.eng.wait_ge(self.sem, number)

    def loop(self, i, per):
        self.n0, self.per = self.n, per
        self.off = i * per

    def end_loop(self, times):
        assert self.n - self.n0 == self.per, (self.n - self.n0, self.per)
        self.n = self.n0 + times * self.per
        self.off = 0


def program(nc, cst, xt0, xr0, l0w, l0p, bo0, l0s, ew, l1w, l1p, l1r, fin_r, mod_w, out):
    with ExitStack() as ctx:
        def sb(name, shape, dt=F32):
            return ctx.enter_context(nc.sbuf_tensor(name, [P] + shape, dt))

        sems = {}

        def sem(name):
            if name not in sems:
                sems[name] = ctx.enter_context(nc.semaphore(name))
            return sems[name]

        bank = [ctx.enter_context(nc.psum_tensor(f"bank{i}", [P, 512], F32)) for i in range(8)]

        dispatch_dram = nc.dram_tensor("dispatch_rows", [TOK, ROUTED], F32).ap()
        returned_dram = nc.dram_tensor("returned_rows", [TOK * TOPK, D], F32).ap()

        C = sb("consts", [C_ALL])
        ident = C[:, C_ID:C_ID + P]
        tri16, ones16 = sb("tri16", [P], F16), sb("ones16", [P], F16)
        x1 = sb("x1", [TILES, D])
        x1t = sb("x1t", [TOK])
        shared = sb("shared", [TILES, D])
        logits = sb("logits", [TILES, NE])
        gates = sb("gates", [TILES, NE])
        ring = sb("ring", [EG, 9 * D])
        arena = sb("arena", [ARENA])

        def carve(parts, at=0):
            made = {}
            for name, shape, dt in parts:
                n = int(np.prod(shape))
                words = n if dt != F16 else n // 2
                a = arena[:, at:at + words]
                if dt != F32:
                    a = a.bitcast(dt)
                if len(shape) == 2:
                    a = a.rearrange("p (a b) -> p a b", b=shape[1])
                elif len(shape) == 3:
                    a = a.rearrange("p (a b c) -> p a b c", b=shape[1], c=shape[2])
                made[name] = a
                at += words
            assert at <= ARENA, at
            return made

        A = carve([("xt", (TOK,), F32), ("w", (2 * P + DH * P + P,), F32),
                   ("eqk", (2, GROUP), F32), ("q", (GROUPS, GROUP), F32), ("k", (GROUP,), F32),
                   ("ksum", (GROUP,), F32), ("kv", (3, GROUP), F32), ("run", (3, GROUP), F32),
                   ("dk", (GROUPS, GROUP), F32), ("att", (GROUPS, GROUP), F32), ("an", (GROUPS, GROUP), F32),
                   ("prod", (DH, GROUP), F32)])
        at_prod = TOK + (3 + DH) * P + (2 + GROUPS + 1 + 1 + 3 + 3 + 3 * GROUPS) * GROUP
        T = carve([("ant", (GROUPS, GROUP), F32), ("xs", (GROUPS, GROUP), F32)], at_prod)
        xr = shared
        l0ps = sb("l0ps", [10])
        bq1 = sb("bq1", [2])
        bo_bc = sb("bo_bc", [D])
        sw = sb("sw", [NE + 9 * D])

        small = sb("small", [1024])
        den = small[:, 0:GROUPS * 64].rearrange("p (g n) -> p g n", g=GROUPS)
        rden = small[:, 256:256 + GROUPS * 64].rearrange("p (g n) -> p g n", g=GROUPS)
        NORMS = {"first": (0, 0), "combine": (0, GROUPS), "final": (0, 2 * GROUPS),
                 "norm1": (1, 0), "second": (1, GROUPS * LAYERS), "norm2": (2, 0), "last": (2, GROUPS * LAYERS)}
        stats = sb("stats", [6, GT, 6])
        mv = sb("mv", [6, GT, 2])
        veps = sb("veps", [6, GT])
        rstd = sb("rstd", [6, GT])
        neg_mean, shift = sb("neg_mean", [6, GT]), sb("shift", [6, GT])
        minus_half = sb("minus_half", [GT])
        minus_one = sb("minus_one", [1])
        zeros = sb("zeros", [1024])
        scratch = zeros
        hidden = sb("hidden", [3 * FB, GROUP])
        new_tile = sb("new_tile", [TILES * NE], F16)
        new_token = sb("new_token", [TILES * NE], F16)
        route = small[:, 512:768]
        best8 = sb("best8", [TILES, 8])
        slots = sb("slots", [NEG, 2, RB])
        picked = sb("picked", [2, 2 * RB, EG])
        gather_all, scatter_all = sb("gather_all", [NEG, RB], U32), sb("scatter_all", [NEG, RB], U32)
        gather_ix, scatter_ix = sb("gather_ix", [2, RB], U32), sb("scatter_ix", [2, RB], U32)
        slot_gate = sb("slot_gate", [2, RB])
        picked_gate = sb("picked_gate", [RB, EG])
        TE = TILES * NE
        R = carve([("a", (TILES, NEG * RA * EG), F16), ("b", (2 * RB, TE), F16), ("mask_ei", (TE,), F16),
                   ("upto_ei", (TE,), F16), ("place", (TE,), F16), ("token", (TE,), F16), ("mask", (TE,), F16)])
        R["ai"], R["bi"] = R["mask_ei"], R["upto_ei"]
        at_mask = (TILES * NEG * RA * EG + 2 * RB * TE + 4 * TE) // 2
        Z = 2 * D + 1
        LW, LP = 12 * P, 9
        at_relu = ARENA - (2 * FFB * GROUP + 2 * TOPK * D)
        B = carve([("h", (GROUPS, GT, D), F32), ("ht", (GROUPS, GROUP), F32), ("q", (GROUPS, GROUP), F32),
                   ("z", (GROUPS, GT * Z), F32), ("kp", (GROUPS, GT, D), F32), ("eq", (2, GROUP), F32),
                   ("ek", (2, GT, D), F32), ("kvm", (GROUPS, 2 * (D + HEADS)), F32)])
        B.update(carve([("relu", (2, FFB, GROUP), F32)], at_relu))
        layer_cols = sb("layer_cols", [LAYERS, LP])
        bq_up = sb("bq_up", [LAYERS])
        den1, rden1 = sb("den1", [2, GT, HEADS]), sb("rden1", [2, GT, HEADS])
        got_at = [x1t[:, 0:RB * ROUTED], arena[:, at_mask:at_mask + RB * ROUTED]]
        got = [a.rearrange("p (b c) -> p b c", c=ROUTED) for a in got_at]
        E = carve([("xt", (2, EG, RB * RA), F32), ("yt", (2, RB, P), F32),
                   ("back", (2, RB, D), F32), ("silu", (2, FB * CAP), F32), ("prod", (2, FB * CAP), F32)])

        block = ctx.enter_context(nc.Block())

        def tiles(buf, g):
            return buf[:, GT * g:GT * (g + 1)]

        def cols(buf, g):
            return buf[:, bass.ds(g * GROUP, GROUP)]

        def bank3(b, n=P):
            return bank[b][:, 0:GT * n].rearrange("p (i n) -> p i n", n=n)

        def norm_stats(v, ch, kind, n, g, src):
            s = 2 * NORMS[kind][0] + g % 2
            for i in range(GT):
                k = ch.did(v.bn_stats(stats[:, s, i, :], src[:, i, :]))
            ch.after(k)
            v.sem_inc(sem("stats_taken"))
            for i in range(GT):
                k = ch.did(v.bn_aggr(mv[:, s, i, :], stats[:, s, i, :]))
            ch.after(k)
            if kind in ("second", "last"):
                v.tensor_scalar(neg_mean[:, s, :], mv[:, s, :, 0], -1.0, None, ALU.mult)
            v.tensor_scalar(veps[:, s, :], mv[:, s, :, 1], EPS_LN, None, ALU.add).then_inc(
                sem(f"var{NORMS[kind][0]}_ready"), 1)

        def norm_rstd(pool, kind, n, g):
            which, before = NORMS[kind]
            s = 2 * which + g % 2
            pool.wait_ge(sem(f"var{which}_ready"), before + n + 1)
            pool.tensor_tensor(rstd[:, s, :], veps[:, s, :], minus_half[:], ALU.pow).then_inc(
                sem(f"rstd{which}_ready"), 1)

        def norm_shift(pool, kind, n, g):
            which, before = NORMS[kind]
            s = 2 * which + g % 2
            pool.wait_ge(sem(f"rstd{which}_ready"), before + n + 1)
            pool.tensor_tensor(shift[:, s, :], neg_mean[:, s, :], rstd[:, s, :], ALU.mult).then_inc(
                sem(f"shift_{kind}"), 1)

        def norm_apply_scalar(act, kind, n, g, src, dst, done):
            s = 2 * NORMS[kind][0] + g % 2
            act.wait_ge(sem(f"shift_{kind}"), n + 1)
            for i in range(GT):
                ins = act.activation(dst[:, i, :], src[:, i, :], ACT.Identity, bias=shift[:, s, i:i + 1],
                                     scale=rstd[:, s, i:i + 1])
            ins.then_inc(sem(done), 1)

        def norm_apply(v, kind, n, g, src, dst, done):
            which, before = NORMS[kind]
            s = 2 * which + g % 2
            v.wait_ge(sem(f"rstd{which}_ready"), before + n + 1)
            for i in range(GT):
                ins = v.tensor_scalar(dst[:, i, :], src[:, i, :], mv[:, s, i, 0:1], rstd[:, s, i:i + 1],
                                      ALU.subtract, ALU.mult)
            ins.then_inc(sem(done), 1)

        RESULTS_AT, INPUTS_AT = (1, 2, 3), (4, 5, 6)

        def expert_groups(eng, group):
            for G in range(3):
                group(G, G % 2, G // 2)
            with eng.Fori(1, NEG // 2 - 1) as m:
                group(2 * m + 1, 1, m)
                group(2 * m + 2, 0, m + 1)
            group(NEG - 1, 1, NEG // 2 - 1)

        def tiles_at(buf, g):
            return buf[:, bass.ds(g * GT, GT), :]

        flat_ring = ring[:].rearrange("p j n -> p (j n)")
        w_qkv, w_o = flat_ring[:, 0:3 * P], flat_ring[:, 3 * P:4 * P]
        w_up, w_down = flat_ring[:, 4 * P:8 * P], flat_ring[:, 8 * P:12 * P]
        at = LW
        lrows = flat_ring[:, at:at + 4 * LAYERS * D].rearrange("p (l n) -> p l n", l=LAYERS)
        at += 4 * LAYERS * D
        mod_sb, fin_rows = flat_ring[:, at:at + 2 * D], flat_ring[:, at + 2 * D:at + 4 * D]
        at += 4 * D
        scores = flat_ring[:, at:at + 2 * GROUP].rearrange("p (s n) -> p s n", s=2)
        at += 2 * GROUP
        spare = [hidden[:].rearrange("p a n -> p (a n)")[:, TOPK * D * k:TOPK * D * (k + 1)] for k in range(4)]
        spare += [flat_ring[:, at + TOPK * D * k:at + TOPK * D * (k + 1)] for k in range(4)]
        spare += [arena[:, at_relu + TOPK * D * k:at_relu + TOPK * D * (k + 1)] for k in range(6)]
        spare += [gates[:].rearrange("p i e -> p (i e)"), logits[:].rearrange("p i e -> p (i e)")]
        x2, state, plus = x1, shared, x1t[:].rearrange("p (i d) -> p i d", d=D)
        ITEMS = GROUPS * LAYERS

        def pipeline(eng, slot, body=None):
            for t in range(-2, GROUPS - 1):
                slot(t, t, 1)
            with eng.Fori(1, LAYERS) as l:
                if body:
                    body(l)
                for j in range(GROUPS):
                    slot(l * GROUPS + (j - 1), GROUPS - 1 + j, l)
            if body:
                body(None)
            for t in range(ITEMS - 1, ITEMS + 6):
                slot(t, t, 1)

        def item(k, back):
            return 0 <= k - back < ITEMS

        def layer_of(l, k, back):
            return l + ((k - back) // GROUPS - 1)

        def layer_col(l, k):
            return layer_cols[:, bass.ds(l, 1), k:k + 1].rearrange("p a n -> p (a n)")

        def zrow(g):
            return B["z"][:, g].rearrange("p (i n) -> p i n", n=Z)

        def kvm(g):
            return B["kvm"][:, g].rearrange("p (b n) -> p b n", b=2)

        logits_i = logits[:].rearrange("p i e -> p (i e)").bitcast(I32)

        xt, w0 = A["xt"], A["w"]
        W_Q, W_K, W_V, W_O = 0, P, 2 * P, (2 + DH) * P
        eqk, k0 = A["eqk"], A["k"]
        q_of = lambda i: A["q"][:, bass.ds(i, 1), :].rearrange("p a n -> p (a n)")
        v_banks = (2, 3, 5, 6)
        ksum, kv, run, prod = A["ksum"], A["kv"], A["run"], A["prod"]
        dk, att = A["dk"], A["att"]
        reset = C[:, C_RESET:C_RESET + GROUP]
        head = C[:, C_HEAD:C_HEAD + HEADS]

        @block.sync
        def _(sp):
            sp.dma_start(w0[:, 0:W_V], l0w[:, 0:W_V]).then_inc(sem("qk_w_in"), 16)
            sp.dma_start(cols(xt, 0), cols(xt0, 0)).then_inc(sem("first_xt_in"), 16)
            sp.dma_start(l0ps[:], l0p).then_inc(sem("l0p_in"), 16)
            sp.dma_start(w0[:, W_V:], l0w[:, W_V:]).then_inc(sem("vo_w_in"), 16)
            sp.dma_start(C[:, 0:C_ID], cst[:, 0:C_ID]).then_inc(sem("first_consts_in"), 16)
            sp.dma_start(xt[:, GROUP:], xt0[:, GROUP:]).then_inc(sem("xt_in"), 16)
            sp.dma_start(C[:, C_ID:], cst[:, C_ID:]).then_inc(sem("consts_in"), 16)
            sp.dma_start(xr[:], xr0).then_inc(sem("xr_in"), 16)
            sp.dma_start(bo_bc[:], bo0.partition_broadcast(P)).then_inc(sem("bo_in"), 16)
            sp.dma_start(sw[:], l0s).then_inc(sem("sw_in"), 16)
            for j in range(EG):
                sp.dma_start(ring[:, j, :], ew[j]).then_inc(sem(f"expert_in{j}"), 16)
            sp.wait_ge(sem("zeros_ready"), 1)
            zrows = returned_dram.rearrange("(n p r) d -> n p (r d)", p=P, r=8)
            for n in range(TOK * TOPK // (8 * P)):
                sp.dma_start(zrows[n], zeros[:]).then_inc(sem("zeroed"), 16)
            rows = dispatch_dram.rearrange("(i p) c -> p i c", p=P)
            sp.wait_ge(sem("x1_ready"), GROUPS)
            sp.dma_start(rows[:, :, 0:D], x1[:]).then_inc(sem("rows_out"), 16)
            sp.wait_ge(sem("gates_ready"), 1)
            sp.dma_start(rows[:, :, D:ROUTED], gates[:]).then_inc(sem("rows_out"), 16)
            with sp.Fori(1, NEG) as G:
                for j in range(EG):
                    sp.wait_ge(sem("y_mm"), G * EG + j - (EG - 1))
                    sp.dma_start(ring[:, j, :], ew[bass.ds(G * EG + j, 1)].rearrange("a p n -> (a p) n")).then_inc(
                        sem(f"expert_in{j}"), 16)
            sp.wait_ge(sem("y_mm"), NE)
            sp.dma_start(w_qkv, l1w[0][:, 0:3 * P]).then_inc(sem("qkv_in"), 16)
            sp.dma_start(layer_cols[:], l1p).then_inc(sem("cols_in"), 16)
            sp.dma_start(lrows, l1r.rearrange("l a d -> l (a d)").partition_broadcast(P)).then_inc(sem("rows_in"), 16)
            sp.dma_start(w_o, l1w[0][:, 3 * P:4 * P]).then_inc(sem("o_in"), 16)
            mine = returned_dram.rearrange("(i p k) d -> i p (k d)", p=P, k=TOPK)
            for u in range(2):
                sp.wait_ge(sem(f"scattered{u}"), 16 * RB * NEG // 2)
            for i in range(TILES):
                sp.dma_start(spare[i], mine[i]).then_inc(sem(f"returned_in{i // GT}"), 16)
            sp.dma_start(w_up, l1w[0][:, 4 * P:8 * P]).then_inc(sem("up_in"), 16)
            sp.dma_start(w_down, l1w[0][:, 8 * P:12 * P]).then_inc(sem("down_in"), 16)
            sp.dma_start(mod_sb, mod_w).then_inc(sem("mod_in"), 16)
            sp.dma_start(fin_rows, fin_r.rearrange("a d -> (a d)").partition_broadcast(P)).then_inc(sem("fin_in"), 16)
            with sp.Fori(1, LAYERS) as l:
                w = l1w[bass.ds(l, 1)].rearrange("a p n -> (a p) n")
                sp.wait_ge(sem("kv1_mm"), 2 * GROUPS * l)
                sp.dma_start(w_qkv, w[:, 0:3 * P]).then_inc(sem("qkv_in"), 16)
                sp.wait_ge(sem("out1_mm"), GROUPS * l)
                sp.dma_start(w_o, w[:, 3 * P:4 * P]).then_inc(sem("o_in"), 16)
                sp.wait_ge(sem("up_mm"), FFB * GROUPS * l)
                sp.dma_start(w_up, w[:, 4 * P:8 * P]).then_inc(sem("up_in"), 16)
                sp.wait_ge(sem("down_mm"), GROUPS * l)
                sp.dma_start(w_down, w[:, 8 * P:12 * P]).then_inc(sem("down_in"), 16)
            for g in range(GROUPS):
                sp.wait_ge(sem("out_ready"), g + 1)
                sp.dma_start(tiles(out, g), B["h"][:, g]).then_inc(sem("out_done"), 16)
            sp.wait_ge(sem("out_done"), 16 * GROUPS)

        @block.tensor
        def _(pe):
            def project_qk(i):
                if not isinstance(i, int) or i:
                    pe.wait_ge(sem("k_ready"), i)
                pe.matmul(bank[0][:], w0[:, W_Q:W_Q + P], cols(xt, i), start=True, stop=True)
                pe.matmul(bank[1][:], w0[:, W_K:W_K + P], cols(xt, i), start=True, stop=True).then_inc(
                    sem("qk_mm"), 1)

            def project_v(i, features):
                for e in features:
                    pe.wait_ge(sem("kv_ready"), i * DH + e + 1)
                    pe.matmul(bank[v_banks[e % 4]][:], w0[:, W_V + P * e:W_V + P * e + P], cols(xt, i),
                              start=True, stop=True).then_inc(sem("v_mm"), 1)

            def sum_heads(i, last=False):
                pe.wait_ge(sem("prod_ready"), (i + 1) * DH + 2)
                if last:
                    pe.wait_ge(sem("att_ready"), i)
                else:
                    pe.wait_ge(sem("exp_ready"), i + 2)
                for e in (0, 2, 4, 6, 1, 3, 5, 7):
                    j = e // 2
                    mm = pe.matmul(bank[4][32 * j:32 * j + 32, :], C[:, C_SEL + 32 * e:C_SEL + 32 * e + 32],
                                   prod[:, e, :], start=(e % 2 == 0), stop=(e % 2 == 1))
                mm.then_inc(sem("att_mm"), 1)

            pe.wait_ge(sem("qk_w_in"), 16)
            pe.wait_ge(sem("first_xt_in"), 16)
            project_qk(0)
            pe.wait_ge(sem("vo_w_in"), 16)
            project_v(0, range(DH))
            pe.wait_ge(sem("first_consts_in"), 16)
            pe.wait_ge(sem("xt_in"), 16)
            with pe.Fori(0, GROUPS - 1) as i:
                project_qk(i + 1)
                project_v(i + 1, range(DH // 2))
                sum_heads(i)
                project_v(i + 1, range(DH // 2, DH))

            pe.wait_ge(sem("dk_ready"), GROUPS)
            for t in range(TILES):
                mm = pe.matmul(bank[7][:, HEADS * t:HEADS * t + HEADS],
                               dk[:, t // GT, P * (t % GT):P * (t % GT) + P], head, start=True, stop=True)
            mm.then_inc(sem("den_mm"), 1)
            pe.wait_ge(sem("kv_ready"), len(v_banks) + GROUPS * DH)
            pe.wait_ge(sem("consts_in"), 16)
            for g in range(GROUPS):
                if g == GROUPS - 1:
                    sum_heads(g, True)
                pe.wait_ge(sem("att_ready"), g + 1)
                if g >= 2:
                    pe.wait_ge(sem("an_ready"), g - 1)
                for t in range(GT):
                    mm = pe.transpose(bank[5 + g % 2][:, P * t:P * t + P], att[:, g, P * t:P * t + P], ident)
                mm.then_inc(sem("turned_att"), 1)
            for g in range(GROUPS + 1):
                if g < GROUPS:
                    pe.wait_ge(sem("an_ready"), g + 1)
                    if g >= 2:
                        pe.wait_ge(sem("ant_ready"), g - 1)
                    for t in range(GT):
                        mm = pe.transpose(bank[3 + g % 2][:, P * t:P * t + P], A["an"][:, g, P * t:P * t + P], ident)
                    mm.then_inc(sem("turned_an"), 1)
                if g:
                    h = g - 1
                    pe.wait_ge(sem("ant_ready"), h + 1)
                    if h >= 2:
                        pe.wait_ge(sem("xs_ready"), h - 1)
                    for t in range(GT):
                        mm = pe.matmul(bank[h % 2][:, P * t:P * t + P], T["ant"][:, h, P * t:P * t + P],
                                       w0[:, W_O:W_O + P], start=True, stop=True)
                    mm.then_inc(sem("wo_mm"), 1)
            pe.wait_ge(sem("sw_in"), 16)
            for g in range(GROUPS + 1):
                if g < GROUPS:
                    pe.wait_ge(sem("x1_ready"), g + 1)
                    if g >= 2:
                        pe.wait_ge(sem("x1t_ready"), g - 1)
                    for t in range(GT):
                        mm = pe.transpose(bank[5 + g % 2][:, P * t:P * t + P], x1[:, GT * g + t, :], ident)
                    mm.then_inc(sem("turned_x1"), 1)
                if g:
                    h = g - 1
                    pe.wait_ge(sem("x1t_ready"), h + 1)
                    if h >= 2:
                        pe.wait_ge(sem("logits_ready"), h - 1)
                    for t in range(GT):
                        mm = pe.matmul(bank[3 + h % 2][:, NE * t:NE * t + NE],
                                       x1t[:, GROUP * h + P * t:GROUP * h + P * t + P], sw[:, 0:NE],
                                       start=True, stop=True)
                    mm.then_inc(sem("logits_mm"), 1)

            sw1, sw2 = sw[:, NE:NE + 2 * FFN], sw[:, NE + 2 * FFN:].rearrange("p (f d) -> p f d", d=D)

            def shared_hidden(g):
                for f in range(FB):
                    if not isinstance(g, int) or g:
                        pe.wait_ge(sem("hidden_read"), (g - 1) * FB + f + 1)
                    pe.matmul(bank[2 + 2 * f][:], sw1[:, P * (FB + f):P * (FB + f) + P], cols(x1t, g),
                              start=True, stop=True)
                    pe.matmul(bank[3 + 2 * f][:], sw1[:, P * f:P * f + P], cols(x1t, g),
                              start=True, stop=True).then_inc(sem("hidden_mm"), 1)

            def shared_rows(g):
                pe.wait_ge(sem("hidden_ready"), (g + 1) * FB)
                if not isinstance(g, int) or g:
                    pe.wait_ge(sem("shared_ready"), g)
                for t in range(GT):
                    for f in range(FB):
                        mm = pe.matmul(bank[0][:, P * t:P * t + P], hidden[:, 2 * FB + f, P * t:P * t + P],
                                       sw2[:, f, :], start=(f == 0), stop=(f == FB - 1))
                mm.then_inc(sem("shared_mm"), 1)

            pe.wait_ge(sem("logits_ready"), GROUPS)
            pe.wait_ge(sem("x1t_ready"), GROUPS)
            shared_hidden(0)
            shared_hidden(1)
            shared_rows(0)
            pe.wait_ge(sem("masks_ready"), 1)
            pe.wait_ge(sem("shared_ready"), 1)
            for h in range(2):
                upto = R["upto_ei"].rearrange("p (e i) -> p i e", i=TILES)[:, 8 * h:8 * h + 8, :]
                pe.matmul(bank[h][:], ones16[:], upto, start=True, stop=False)
                mm = pe.matmul(bank[h][:], tri16[:], R["mask"][:, 512 * h:512 * h + 512], start=False, stop=True)
            mm.then_inc(sem("rank_mm"), 1)
            pe.wait_ge(sem("rank_read"), 1)
            shared_hidden(2)
            shared_rows(1)
            a16 = R["a"].rearrange("p i (g n) -> p i g n", n=RA * EG)
            b16 = R["b"].rearrange("p b (i e) -> p b i e", e=NE)

            def find_slots(q):
                pe.wait_ge(sem("one_hots_ready"), q + 1)
                if not isinstance(q, int) or q:
                    pe.wait_ge(sem("slots_read"), q)
                for u in range(2):
                    for i in range(TILES):
                        lhs = a16[:, i, bass.ds(2 * q + u, 1), :].rearrange("p g n -> p (g n)")
                        mm = pe.matmul(bank[1][:, 2 * RB * EG * u:2 * RB * EG * (u + 1)], lhs,
                                       b16[:, :, i, bass.ds(EG * (2 * q + u), EG)],
                                       start=(i == 0), stop=(i == TILES - 1))
                mm.then_inc(sem("slots_mm"), 1)

            find_slots(0)
            shared_hidden(3)
            find_slots(1)
            with pe.Fori(2, NEG // 2) as q:
                shared_rows(q)
                find_slots(q)

            def turn_inputs(G, u, m, c):
                if c == 0:
                    pe.wait_ge(sem(f"gathered{u}"), 16 * RB * (m + 1))
                    if not isinstance(G, int) or G > 1:
                        pe.wait_ge(sem("turned_y_read"), 3 * (G - 1))
                elif c == 2:
                    pe.wait_ge(sem("xt_ready"), 3 * G + 1)
                for b in range(4 * c, min(4 * c + 4, RB)):
                    mm = pe.transpose(bank[7 - c % 2][:, P * (b % 4):P * (b % 4) + P], got[u][:, b, 0:D], ident)
                mm.then_inc(sem("turned_x"), 1)

            def turn_results(G, u, c):
                if c == 0:
                    pe.wait_ge(sem("yt_ready"), (G + 1) * EG)
                    pe.wait_ge(sem("xt_ready"), 3 * G + 6 if not isinstance(G, int) or G < NEG - 1 else 3 * NEG)
                elif c == 2:
                    pe.wait_ge(sem("turned_y_read"), 3 * G + 1)
                for b in range(4 * c, min(4 * c + 4, RB)):
                    mm = pe.transpose(bank[6 + c % 2][:, P * (b % 4):P * (b % 4) + P], E["yt"][:, u, b, :], ident)
                mm.then_inc(sem("turned_y"), 1)

            def expert_hidden(G, u, j):
                n = G * EG + j
                pe.wait_ge(sem(f"expert_in{j}"), 16 * (G + 1))
                if not isinstance(n, int) or n > 1:
                    pe.wait_ge(sem("prod_g_ready"), n - 1)
                for part in (1, 0):
                    for f in range(FB):
                        mm = pe.matmul(bank[2 * (j % 2) + part][:, CAP * f:CAP * f + CAP],
                                       ring[:, j, P * (FB * part + f):P * (FB * part + f) + P], E["xt"][:, u, j, :],
                                       start=True, stop=True)
                    mm.then_inc(sem("gate_mm" if part else "value_mm"), 1)

            def expert_result(G, u, j):
                n = G * EG + j
                pe.wait_ge(sem("prod_g_ready"), n + 1)
                if not isinstance(n, int) or n > 1:
                    pe.wait_ge(sem("yt_ready"), n - 1)
                for f in range(FB):
                    mm = pe.matmul(bank[4 + j % 2][:, 0:CAP], ring[:, j, P * (2 * FB + f):P * (2 * FB + f) + P],
                                   E["prod"][:, j % 2, CAP * f:CAP * f + CAP], start=(f == 0), stop=(f == FB - 1))
                mm.then_inc(sem("y_mm"), 1)

            def expert_group(G, u, m):
                pe.wait_ge(sem("xt_ready"), 3 * (G + 1))
                for j in range(EG):
                    expert_hidden(G, u, j)
                    if j:
                        expert_result(G, u, j - 1)
                    if j in RESULTS_AT and (not isinstance(G, int) or G > 0):
                        turn_results(G - 1, 1 - u, RESULTS_AT.index(j))
                    if j in INPUTS_AT and (not isinstance(G, int) or G < NEG - 1):
                        turn_inputs(G + 1, 1 - u, m + u, INPUTS_AT.index(j))
                expert_result(G, u, EG - 1)

            for c in range(3):
                turn_inputs(0, 0, 0, c)
            pe.wait_ge(sem("shared_ready"), GROUPS)
            pe.wait_ge(sem("slots_read"), NEG // 2)
            expert_groups(pe, expert_group)
            for c in range(3):
                turn_results(NEG - 1, 1, c)

            def turn(src, b, done):
                for t in range(GT):
                    mm = pe.transpose(bank[b][:, P * t:P * t + P], src[:, t, :], ident)
                mm.then_inc(sem(done), 1)

            def turn_norm1(n, k, g):
                pe.wait_ge(sem("h1_ready"), n + 1)
                if k >= 3:
                    pe.wait_ge(sem("h2t_ready"), n - 2)
                turn(B["h"][:, g], 0, "turned1")

            def project(n, k, g, l):
                pe.wait_ge(sem("qkv_in"), 16 * (l + 1))
                pe.wait_ge(sem("ht_ready"), n + 1)
                if k >= 2:
                    pe.wait_ge(sem("mid_ready"), n - 1)
                pe.matmul(bank[2][:], w_qkv[:, 0:P], B["ht"][:, g], start=True, stop=True).then_inc(sem("q1_mm"), 1)
                if k >= 3:
                    pe.wait_ge(sem("relu_ready"), FFB * (n - 2))
                for h in range(2):
                    for t in range(2):
                        mm = pe.matmul(bank[3 + h][:, 2 * D * t:2 * D * t + 2 * D],
                                       B["ht"][:, g, P * (2 * h + t):P * (2 * h + t) + P], w_qkv[:, P:3 * P],
                                       start=True, stop=True)
                    mm.then_inc(sem("kv1_mm"), 1)

            def sum_kv(n, k, g):
                pe.wait_ge(sem("kp_ready"), n + 1)
                pe.wait_ge(sem("x_ready"), n + 2 if k < ITEMS - 1 else ITEMS + 1)
                for t in range(GT):
                    mm = pe.matmul(bank[5][:, (D + 1) * (t // 2):(D + 1) * (t // 2 + 1)], B["kp"][:, g, t, :],
                                   zrow(g)[:, t, D:Z], start=(t % 2 == 0), stop=(t % 2 == 1))
                mm.then_inc(sem("kvsum_mm"), 1)

            def attend(n, k, g):
                pe.wait_ge(sem("kvm_ready"), n + 1)
                if k >= 2:
                    pe.wait_ge(sem("relu_ready"), FFB * (n - 1))
                for t in range(GT):
                    mm = pe.matmul(bank[6 + t // 2][:, (D + HEADS) * (t % 2):(D + HEADS) * (t % 2 + 1)],
                                   B["q"][:, g, P * t:P * t + P], kvm(g)[:, t // 2, :], start=True, stop=True)
                mm.then_inc(sem("num_mm"), 1)

            def turn_attention(n, k, g):
                pe.wait_ge(sem("an1_ready"), n + 1)
                if k >= 1:
                    pe.wait_ge(sem("at_ready"), n)
                turn(B["h"][:, g], 1, "turned2")

            def output(n, k, g, l):
                pe.wait_ge(sem("o_in"), 16 * (l + 1))
                pe.wait_ge(sem("at_ready"), n + 1)
                if k < ITEMS - 1:
                    pe.wait_ge(sem("q1_ready"), n + 2)
                else:
                    pe.wait_ge(sem("mid_ready"), n)
                for t in range(GT):
                    mm = pe.matmul(bank[2][:, P * t:P * t + P], B["ht"][:, g, P * t:P * t + P], w_o,
                                   start=True, stop=True)
                mm.then_inc(sem("out1_mm"), 1)

            def turn_norm2(n, k, g):
                pe.wait_ge(sem("h2_ready"), n + 1)
                if k < ITEMS - 2:
                    pe.wait_ge(sem("ht_ready"), n + 3)
                elif k < ITEMS - 1:
                    pe.wait_ge(sem("h2t_ready"), n)
                else:
                    pe.wait_ge(sem("gelu_ready"), 1)
                turn(B["h"][:, g], 0, "turned3")

            def up(n, k, g, l):
                pe.wait_ge(sem("up_in"), 16 * (l + 1))
                pe.wait_ge(sem("h2t_ready"), n + 1)
                for f in range(FFB):
                    if k >= ITEMS - 2 and (f < 2 or k == ITEMS - 1):
                        pe.wait_ge(sem("relu_ready"), FFB * (n - 1) + f + 1)
                    elif f == 0:
                        pe.wait_ge(sem("z_ready"), 2 * (n + 3))
                    elif f == 2:
                        pe.wait_ge(sem("an1_ready"), n + 2)
                    pe.matmul(bank[(3, 4, 6, 7)[f]][:], w_up[:, P * f:P * f + P], B["ht"][:, g], start=True,
                              stop=True).then_inc(sem("up_mm"), 1)

            def down(n, k, g, l):
                pe.wait_ge(sem("down_in"), 16 * (l + 1))
                pe.wait_ge(sem("relu_ready"), FFB * (n + 1))
                if k < ITEMS - 2:
                    pe.wait_ge(sem("kvm_ready"), n + 3)
                else:
                    pe.wait_ge(sem("x_ready"), GROUPS + n)
                for t in range(GT):
                    for f in range(FFB):
                        mm = pe.matmul(bank[5][:, P * t:P * t + P],
                                       B["relu"][:, g % 2, f, P * t:P * t + P], w_down[:, P * f:P * f + P],
                                       start=(f == 0), stop=(f == FFB - 1))
                mm.then_inc(sem("down_mm"), 1)

            def score(g):
                pe.wait_ge(sem("mod_in"), 16)
                pe.wait_ge(sem("x3_ready"), g + 1)
                if g:
                    pe.wait_ge(sem("x3t_ready"), g)
                else:
                    pe.wait_ge(sem("at_ready"), ITEMS)
                turn(state[:, GT * g:GT * g + GT], 1, "turned_x3")
                pe.wait_ge(sem("x3t_ready"), g + 1)
                if g:
                    pe.wait_ge(sem("scores_ready"), g)
                else:
                    pe.wait_ge(sem("mid_ready"), ITEMS)
                pe.matmul(bank[2][:], mod_sb[:, 0:P], B["ht"][:, g], start=True, stop=True).then_inc(
                    sem("score_mm"), 1)
                if g:
                    pe.wait_ge(sem("gelu_ready"), g)
                if g < 2:
                    pe.wait_ge(sem("h2t_ready"), ITEMS - 1 + g)
                for t in range(GT):
                    mm = pe.matmul(bank[0][:, P * t:P * t + P], B["ht"][:, g, P * t:P * t + P], mod_sb[:, P:2 * P],
                                   start=True, stop=True)
                mm.then_inc(sem("block_mm"), 1)

            def slot(t, k, l):
                g = k % GROUPS
                if item(k, 1):
                    sum_kv(t - 1, k - 1, (g - 1) % GROUPS)
                if item(k, 0):
                    turn_norm1(t, k, g)
                if item(k, 1):
                    attend(t - 1, k - 1, (g - 1) % GROUPS)
                if item(k, 0):
                    project(t, k, g, layer_of(l, k, 0))
                if item(k, 1):
                    turn_attention(t - 1, k - 1, (g - 1) % GROUPS)
                if item(k, 2):
                    turn_norm2(t - 2, k - 2, (g - 2) % GROUPS)
                if item(k, 3):
                    down(t - 3, k - 3, (g - 3) % GROUPS, layer_of(l, k, 3))
                if item(k, 1):
                    output(t - 1, k - 1, (g - 1) % GROUPS, layer_of(l, k, 1))
                if item(k, 2):
                    up(t - 2, k - 2, (g - 2) % GROUPS, layer_of(l, k, 2))
                if ITEMS <= k < ITEMS + GROUPS:
                    score(k - ITEMS)

            pipeline(pe, slot)

        @block.scalar
        def _(act):
            def exps(i):
                if not isinstance(i, int) or i:
                    act.wait_ge(sem("k_ready"), i)
                act.wait_ge(sem("qk_mm"), i + 1)
                act.activation(eqk[:, 0, :], bank[0][:], ACT.Exp, bias=l0ps[:, 0:1])
                act.activation(eqk[:, 1, :], bank[1][:], ACT.Exp, bias=l0ps[:, 1:2]).then_inc(sem("exp_ready"), 1)

            def keep_att(i):
                act.wait_ge(sem("att_mm"), i + 1)
                act.activation(att[:, bass.ds(i, 1), :].rearrange("p a n -> p (a n)"), bank[4][:],
                               ACT.Copy).then_inc(sem("att_ready"), 1)

            act.wait_ge(sem("l0p_in"), 16)
            exps(0)
            with act.Fori(0, GROUPS - 1) as i:
                exps(i + 1)
                keep_att(i)
            keep_att(GROUPS - 1)
            for g in range(GROUPS):
                act.wait_ge(sem("turned_an"), g + 1)
                act.activation(T["ant"][:, g, :], bank[3 + g % 2][:], ACT.Copy).then_inc(sem("ant_ready"), 1)
            for g in range(GROUPS + 1):
                if g < GROUPS:
                    act.wait_ge(sem("turned_x1"), g + 1)
                    act.activation(cols(x1t, g), bank[5 + g % 2][:], ACT.Copy).then_inc(sem("x1t_ready"), 1)
                if g:
                    act.wait_ge(sem("logits_mm"), g)
                    act.activation(tiles(logits, g - 1), bank3(3 + (g - 1) % 2, NE), ACT.Copy).then_inc(
                        sem("logits_ready"), 1)
            act.wait_ge(sem("shifted_ready"), 1)
            act.activation(gates[:], gates[:], ACT.Exp).then_inc(sem("gates_exp"), 1)

            def shared_halves(g):
                for f in range(FB):
                    act.wait_ge(sem("hidden_mm"), g * FB + f + 1)
                    if not isinstance(g, int) or g:
                        act.wait_ge(sem("hidden_ready"), g * FB)
                    act.activation(hidden[:, FB + f, :], bank[2 + 2 * f][:], ACT.Silu)
                    act.activation(hidden[:, f, :], bank[3 + 2 * f][:], ACT.Copy).then_inc(sem("hidden_read"), 1)

            def keep_shared(g):
                act.wait_ge(sem("shared_mm"), g + 1)
                act.activation(tiles_at(shared, g), bank3(0), ACT.Copy).then_inc(sem("shared_ready"), 1)

            shared_halves(0)
            shared_halves(1)
            keep_shared(0)
            act.wait_ge(sem("b_index"), 1)
            act.activation(R["bi"], logits_i, ACT.Copy).then_inc(sem("bi_ready"), 1)
            with act.Fori(2, GROUPS) as g:
                shared_halves(g)
                keep_shared(g - 1)
            keep_shared(GROUPS - 1)

            def silu_of(G, u, j):
                n = G * EG + j
                act.wait_ge(sem("gate_mm"), n + 1)
                if not isinstance(n, int) or n > 1:
                    act.wait_ge(sem("prod_g_ready"), n - 1)
                act.activation(E["silu"][:, j % 2, :], bank[2 * (j % 2) + 1][:, 0:FB * CAP], ACT.Silu).then_inc(
                    sem("silu_ready"), 1)

            def keep_result(G, u, j):
                act.wait_ge(sem("y_mm"), G * EG + j + 1)
                if j == 0 and not (isinstance(G, int) and G < 2):
                    act.wait_ge(sem("turned_y"), 3 * (G - 1))
                act.activation(E["yt"][:, u].rearrange("p b (a e) -> p b a e", e=EG)[:, :, :, j],
                               bank[4 + j % 2][:, 0:CAP].rearrange("p (b a) -> p b a", a=RA), ACT.Copy).then_inc(
                    sem("yt_ready"), 1)

            def expert_group(G, u):
                for j in range(EG):
                    silu_of(G, u, j)
                    if j:
                        keep_result(G, u, j - 1)
                keep_result(G, u, EG - 1)

            expert_group(0, 0)
            expert_group(1, 1)
            with act.Fori(1, NEG // 2) as m:
                for u in range(2):
                    expert_group(2 * m + u, u)

            def norm1_columns(n, g, l):
                act.wait_ge(sem("turned1"), n + 1)
                act.sem_inc(sem("act_steps"))
                act.activation(B["ht"][:, g], bank[0][:], ACT.Identity, bias=layer_col(l, 2),
                               scale=layer_col(l, 1)).then_inc(sem("ht_ready"), 1)

            def exp_q(n, k, g, l):
                act.wait_ge(sem("q1_mm"), n + 1)
                if k >= 2:
                    act.wait_ge(sem("q1_ready"), n - 1)
                act.sem_inc(sem("act_steps"))
                act.activation(B["eq"][:, g % 2], bank[2][:], ACT.Exp, bias=layer_col(l, 0)).then_inc(
                    sem("eq_ready"), 1)

            def exp_k(n, k, g):
                act.wait_ge(sem("z_ready"), 2 * (n + 1))
                if k >= 2:
                    act.wait_ge(sem("kp_ready"), n - 1)
                act.activation(B["ek"][:, g % 2], zrow(g)[:, :, 0:D], ACT.Exp, bias=minus_one[:]).then_inc(
                    sem("ek_ready"), 1)

            def attention_columns(n, g):
                act.wait_ge(sem("turned2"), n + 1)
                act.activation(B["ht"][:, g], bank[1][:], ACT.Copy).then_inc(sem("at_ready"), 1)

            def norm2_columns(n, g, l):
                act.wait_ge(sem("turned3"), n + 1)
                act.sem_inc(sem("act_steps"))
                act.activation(B["ht"][:, g], bank[0][:], ACT.Identity, bias=layer_col(l, 4),
                               scale=layer_col(l, 3)).then_inc(sem("h2t_ready"), 1)

            def relus(n, g, l):
                for f in range(FFB):
                    act.wait_ge(sem("up_mm"), FFB * n + f + 1)
                    act.sem_inc(sem("act_steps"))
                    act.activation(B["relu"][:, g % 2, f], bank[(3, 4, 6, 7)[f]][:], ACT.Relu,
                                   bias=layer_col(l, 5 + f)).then_inc(sem("relu_ready"), 1)

            def gelus(g):
                norm_apply_scalar(act, "second", g, g, B["h"][:, g], tiles(state, g), "x3_ready")
                act.wait_ge(sem("turned_x3"), g + 1)
                act.activation(B["ht"][:, g], bank[1][:], ACT.Copy).then_inc(sem("x3t_ready"), 1)
                if g >= 2:
                    act.wait_ge(sem("chosen"), g - 1)
                act.wait_ge(sem("score_mm"), g + 1)
                act.activation(scores[:, g % 2], bank[2][:], ACT.Copy).then_inc(sem("scores_ready"), 1)
                act.wait_ge(sem("block_mm"), g + 1)
                act.activation(B["q"][:, g].rearrange("p (i d) -> p i d", d=D), bank3(0),
                               ACT.Gelu_apprx_tanh).then_inc(sem("gelu_ready"), 1)
                act.activation(B["kp"][:, g], tiles(state, g), ACT.Copy, scale=2.0).then_inc(sem("twice_ready"), 1)

            def slot(t, k, l):
                g = k % GROUPS
                if item(k, 0):
                    norm1_columns(t, g, layer_of(l, k, 0))
                    exp_q(t, k, g, layer_of(l, k, 0))
                if item(k, 1):
                    attention_columns(t - 1, (g - 1) % GROUPS)
                if item(k, 2):
                    norm2_columns(t - 2, (g - 2) % GROUPS, layer_of(l, k, 2))
                if item(k, 0):
                    exp_k(t, k, g)
                if item(k, 2):
                    relus(t - 2, (g - 2) % GROUPS, layer_of(l, k, 2))
                if ITEMS <= k < ITEMS + GROUPS:
                    gelus(k - ITEMS)
                if 0 <= k - (ITEMS + 1) < GROUPS:
                    f = k - (ITEMS + 1)
                    norm_apply_scalar(act, "last", f, f, B["kp"][:, f], B["h"][:, f], "out_ready")

            act.wait_ge(sem("cols_in"), 16)
            pipeline(act, slot)

        @block.gpsimd
        def _(pool):
            pool.memset(zeros[:], 0.0).then_inc(sem("zeros_ready"), 1)
            pool.memset(new_tile[:], 1.0).then_inc(sem("pool_consts"), 1)
            pool.memset(new_token[:], 1.0).then_inc(sem("pool_consts"), 1)
            pool.wait_ge(sem("pool_consts"), 2)
            pool.memset(new_tile[:].rearrange("p (e i) -> p e i", i=TILES)[:, :, 0:1], 0.0)
            pool.memset(new_token[:].rearrange("p (i e) -> p i e", e=NE)[:, :, 0:1], 0.0).then_inc(
                sem("starts_ready"), 1)
            pool.memset(minus_half[:], -0.5).then_inc(sem("pool_consts"), 1)
            pool.memset(minus_one[:], -1.0).then_inc(sem("minus_one_ready"), 1)
            pool.wait_ge(sem("pool_consts"), 3)
            pool.wait_ge(sem("xr_in"), 16)
            pool.wait_ge(sem("bo_in"), 16)
            for _ in range(2):
                pool.sem_inc(sem("prod_ready"))
            with pool.Fori(0, GROUPS) as i:
                pool.wait_ge(sem("ksum_ready"), i + 1)
                pool.sem_inc(sem("pool_steps"))
                pool.tensor_tensor(dk[:, bass.ds(i, 1), :].rearrange("p a n -> p (a n)"), ksum, q_of(i),
                                   ALU.mult).then_inc(sem("dk_ready"), 1)
                for e in range(DH):
                    pool.wait_ge(sem("run_ready"), i * DH + e + 1)
                    if e == 0:
                        pool.wait_ge(sem("v_mm"), i * DH + DH // 2 + 1)
                    pool.sem_inc(sem("pool_steps"))
                    pool.tensor_tensor(prod[:, e, :], run[:, e % 3, :], q_of(i), ALU.mult).then_inc(
                        sem("prod_ready"), 1)
            for g in range(GROUPS):
                pool.tensor_tensor(tiles(xr, g), tiles(xr, g), bo_bc[:].unsqueeze(1).to_broadcast([P, GT, D]),
                                   ALU.add).then_inc(sem("xr_ready"), 1)
            for g in range(GROUPS):
                norm_rstd(pool, "first", g, g)

            def shared_products(g):
                for f in range(FB):
                    pool.wait_ge(sem("hidden_read"), g * FB + f + 1)
                    if not isinstance(g, int) or g:
                        pool.wait_ge(sem("shared_mm"), g)
                    pool.tensor_tensor(hidden[:, 2 * FB + f, :], hidden[:, f, :], hidden[:, FB + f, :],
                                       ALU.mult).then_inc(sem("hidden_ready"), 1)

            shared_products(0)
            pool.wait_ge(sem("masks_ready"), 1)
            pool.tensor_tensor(gates[:].rearrange("p i e -> p (i e)"), gates[:].rearrange("p i e -> p (i e)"),
                               R["mask"], ALU.mult).then_inc(sem("gates_masked"), 1)
            pool.wait_ge(sem("gates_masked"), 1)
            pool.wait_ge(sem("top_sum_ready"), 1)
            pool.tensor_tensor(gates[:], gates[:], route[:, 80:96].unsqueeze(2).to_broadcast([P, TILES, NE]),
                               ALU.mult).then_inc(sem("gates_ready"), 1)
            with pool.Fori(1, GROUPS) as g:
                shared_products(g)

            def gather(G, u, m):
                if not (isinstance(G, int) and G < 2):
                    pool.wait_ge(sem("slot_gate_ready"), G - 1)
                pool.wait_ge(sem("indices_ready"), m + 1)
                pool.tensor_copy(gather_ix[:, u:u + 1, :], gather_all[:, bass.ds(G, 1), :]).then_inc(
                    sem("gather_ix_ready"), 1)
                pool.wait_ge(sem("gather_ix_ready"), G + 1)
                pool.sem_inc(sem("gather_begun"))
                pool.wait_ge(sem("rows_out"), 32)
                for b in range(RB):
                    pool.indirect_dma_start(got[u][:, b, :], None, dispatch_dram[:, :],
                                            bass.IndirectOffsetOnAxis(ap=gather_ix[:, u, b:b + 1], axis=0)).then_inc(
                        sem(f"gathered{u}"), 16)

            def scatter(G, u, m):
                if not isinstance(m, int) or m:
                    pool.wait_ge(sem(f"scattered{u}"), 16 * RB * m)
                pool.tensor_copy(scatter_ix[:, u:u + 1, :], scatter_all[:, bass.ds(G, 1), :]).then_inc(
                    sem("scatter_ix_ready"), 1)
                pool.wait_ge(sem("scatter_ix_ready"), G + 1)
                pool.wait_ge(sem("turned_y_read"), 3 * (G + 1))
                pool.sem_inc(sem("scatter_begun"))
                pool.wait_ge(sem("zeroed"), 16 * TOK * TOPK // (8 * P))
                for b in range(RB):
                    pool.indirect_dma_start(returned_dram[:, :],
                                            bass.IndirectOffsetOnAxis(ap=scatter_ix[:, u, b:b + 1], axis=0),
                                            E["back"][:, u, b, :], None, bounds_check=TOK * TOPK - 1,
                                            oob_is_err=False).then_inc(sem(f"scattered{u}"), 16)

            gather(0, 0, 0)
            gather(1, 1, 0)
            for u in range(2):
                gather(u + 2, u, 1)
                scatter(u, u, 0)
            with pool.Fori(1, NEG // 2 - 1) as m:
                for u in range(2):
                    gather(2 * m + u + 2, u, m + 1)
                    scatter(2 * m + u, u, m)
            scatter(NEG - 2, 0, NEG // 2 - 1)
            for g in range(GROUPS):
                pool.wait_ge(sem("shared_ready"), GROUPS)
                pool.tensor_tensor(tiles(shared, g), tiles(shared, g), tiles(x1, g), ALU.add).then_inc(
                    sem("base_ready"), 1)
            scatter(NEG - 1, 1, NEG // 2 - 1)

            def row_of(l, k):
                return lrows[:, bass.ds(l, 1), D * k:D * k + D].to_broadcast([P, GT, D])

            def slot(t, k, l):
                g = k % GROUPS
                if item(k, 2):
                    norm_rstd(pool, "norm2", t - 2, g - 2)
                    pool.wait_ge(sem("mid_ready"), t - 1)
                    pool.sem_inc(sem("pool_steps"))
                    pool.tensor_tensor(tiles(plus, (g - 2) % GROUPS), tiles(state, (g - 2) % GROUPS),
                                       row_of(layer_of(l, k, 2), 3), ALU.add).then_inc(sem("plus_b2"), 1)
                if 0 <= k + 2 < GROUPS:
                    sum_last_tile(k + 2)
                if k + 2 == 0:
                    norm_rstd(pool, "combine", 0, 0)
                if item(k, -1):
                    norm_rstd(pool, "norm1", t + 1, g + 1)
                    if 0 <= k + 2 < GROUPS:
                        norm_rstd(pool, "combine", k + 2, k + 2)
                    pool.wait_ge(sem("x_ready"), t + 2)
                    pool.sem_inc(sem("pool_steps"))
                    pool.tensor_tensor(tiles(plus, (g + 1) % GROUPS), tiles(state, (g + 1) % GROUPS),
                                       row_of(layer_of(l, k, -1), 2), ALU.add).then_inc(sem("plus_bo"), 1)
                if 0 <= k - (ITEMS - 1) < GROUPS:
                    f = k - (ITEMS - 1)
                    norm_rstd(pool, "final", f, f)
                    pool.wait_ge(sem("fin_in"), 16)
                    pool.wait_ge(sem("x_ready"), ITEMS + f + 1)
                    pool.tensor_tensor(tiles(plus, f), tiles(x2, f),
                                       fin_rows[:, D:2 * D].unsqueeze(1).to_broadcast([P, GT, D]), ALU.add).then_inc(
                        sem("plus_lnf"), 1)
                if 0 <= k - (ITEMS - 1) < GROUPS:
                    norm_rstd(pool, "second", f, f)
                    norm_shift(pool, "second", f, f)
                if 0 <= k - (ITEMS + 1) < GROUPS:
                    f = k - (ITEMS + 1)
                    pool.wait_ge(sem("gelu_ready"), f + 1)
                    pool.tensor_tensor(B["q"][:, f], B["q"][:, f], tiles(state, f).rearrange("p i d -> p (i d)"),
                                       ALU.add).then_inc(sem("processed_ready"), 1)
                    norm_rstd(pool, "last", f, f)
                    norm_shift(pool, "last", f, f)

            def sum_last_tile(g):
                rows = spare[GT * g + GT - 1]
                pool.wait_ge(sem(f"returned_in{g}"), 16 * GT)
                for h, width in enumerate((4 * D, 2 * D, D)):
                    dst = rows[:, 0:width] if width > D else B["h"][:, g, GT - 1, :]
                    pool.tensor_tensor(dst, rows[:, 0:width], rows[:, width:2 * width], ALU.add).then_inc(
                        sem("pool_sums"), 1)
                    pool.wait_ge(sem("pool_sums"), 3 * g + h + 1)

            pool.wait_ge(sem("rows_in"), 16)
            pipeline(pool, slot)

        @block.vector
        def _(v):
            ch = Chain(v, sem("vector_step"))
            v.wait_ge(sem("l0p_in"), 16)
            v.tensor_scalar(bq1[:], l0ps[:, 0:2], 1.0, None, ALU.add).then_inc(sem("bq1_ready"), 1)
            v.wait_ge(sem("bq1_ready"), 1)
            v.wait_ge(sem("first_consts_in"), 16)
            for _ in v_banks:
                v.sem_inc(sem("kv_ready"))
            with v.Fori(0, GROUPS) as i:
                ch.loop(i, 1)
                v.wait_ge(sem("exp_ready"), i + 1)
                e1 = ch.did(v.tensor_scalar(eqk[:], eqk[:], 1.0, None, ALU.min))
                ch.after(e1)
                v.scalar_tensor_tensor(q_of(i), bank[0][:], bq1[:, 0:1], eqk[:, 0, :], ALU.add, ALU.max).then_inc(
                    sem("q_ready"), 1)
                v.scalar_tensor_tensor(k0, bank[1][:], bq1[:, 1:2], eqk[:, 1, :], ALU.add, ALU.max).then_inc(
                    sem("k_ready"), 1)
                v.wait_ge(sem("k_ready"), i + 1)

                def kv_of(e):
                    v.wait_ge(sem("v_mm"), i * DH + e + 1)
                    if e >= 3:
                        v.wait_ge(sem("run_ready"), i * DH + e - 2)
                    v.scalar_tensor_tensor(kv[:, e % 3, :], bank[v_banks[e % 4]][:], l0ps[:, 2 + e:3 + e], k0,
                                           ALU.add, ALU.mult).then_inc(sem("kv_ready"), 1)

                kv_of(0)
                v.tensor_tensor_scan(ksum, reset, k0, 0.0, ALU.mult, ALU.add).then_inc(sem("ksum_ready"), 1)
                for e in range(DH):
                    if e + 1 < DH:
                        kv_of(e + 1)
                    v.wait_ge(sem("kv_ready"), len(v_banks) + i * DH + e + 1)
                    if e != 2:
                        v.wait_ge(sem("prod_ready"), i * DH + (e - 2 if e >= 3 else e - 1) + 2)
                    v.tensor_tensor_scan(run[:, e % 3, :], reset, kv[:, e % 3, :], 0.0, ALU.mult,
                                         ALU.add).then_inc(sem("run_ready"), 1)
            ch.end_loop(GROUPS)
            v.wait_ge(sem("consts_in"), 16)
            v.tensor_copy(tri16[:], C[:, C_TRI:C_TRI + P])
            v.tensor_copy(ones16[:], C[:, C_ONES:C_ONES + P])
            v.wait_ge(sem("den_mm"), 1)
            d = ch.did(v.tensor_scalar(den, bank[7][:, 0:TILES * HEADS].rearrange("p (g n) -> p g n", g=GROUPS),
                                       EPS_ATTN, None, ALU.max))
            ch.after(d)
            d = ch.did(v.reciprocal(rden, den))
            ch.after(d)
            for g in range(GROUPS):
                v.wait_ge(sem("turned_att"), g + 1)
                r = rden[:, g, :].rearrange("p (i h) -> p i h", h=HEADS).unsqueeze(2).to_broadcast([P, GT, DH, HEADS])
                v.tensor_tensor(A["an"][:, g, :].rearrange("p (i e h) -> p i e h", e=DH, h=HEADS),
                                bank[5 + g % 2][:].rearrange("p (i e h) -> p i e h", e=DH, h=HEADS), r,
                                ALU.mult).then_inc(sem("an_ready"), 1)
            xs = T["xs"].rearrange("p g (i d) -> p g i d", d=D)
            for g in range(GROUPS + 1):
                if g < GROUPS:
                    v.wait_ge(sem("wo_mm"), g + 1)
                    v.wait_ge(sem("xr_ready"), g + 1)
                    v.tensor_tensor(xs[:, g], bank3(g % 2), tiles(xr, g), ALU.add).then_inc(sem("xs_ready"), 1)
                    v.wait_ge(sem("xs_ready"), g + 1)
                    norm_stats(v, ch, "first", g, g, xs[:, g])
                if g:
                    norm_apply(v, "first", g - 1, g - 1, xs[:, g - 1], tiles(x1, g - 1), "x1_ready")

            top, total, inv, top8 = route[:, 0:16], route[:, 16:32], route[:, 32:48], route[:, 48:64]
            over = lambda a: a.unsqueeze(2).to_broadcast([P, TILES, NE])
            v.wait_ge(sem("logits_ready"), GROUPS)
            ch.after(ch.did(v.tensor_reduce(top, logits[:], AX.X, ALU.max)))
            v.tensor_tensor(gates[:], logits[:], over(top), ALU.subtract).then_inc(sem("shifted_ready"), 1)
            v.wait_ge(sem("gates_exp"), 1)
            ch.after(ch.did(v.tensor_reduce(total, gates[:], AX.X, ALU.add)))
            ch.after(ch.did(v.reciprocal(inv, total)))
            ch.after(ch.did(v.tensor_tensor(gates[:], gates[:], over(inv), ALU.mult)))
            for i in range(TILES):
                k = ch.did(v.max(best8[:, i, :], gates[:, i, :]))
            ch.after(k)
            for i in range(TILES):
                k = ch.did(v.match_replace(logits[:, i, :], best8[:, i, :], gates[:, i, :], -1.0))
            ch.after(k)
            lg = logits[:].rearrange("p i e -> p (i e)")
            mask, mask_ei = R["mask"], R["mask_ei"]
            v.tensor_scalar(mask, lg, 0.0, None, ALU.is_lt).then_inc(sem("mask_parts"), 1)
            v.tensor_scalar(mask_ei.rearrange("p (e i) -> p i e", i=TILES), logits[:], 0.0, None, ALU.is_lt).then_inc(
                sem("mask_parts"), 1)
            ch.after(ch.did(v.tensor_reduce(top8, best8[:], AX.X, ALU.add)))
            v.wait_ge(sem("starts_ready"), 1)
            v.tensor_tensor_scan(R["upto_ei"], new_tile[:], mask_ei, 0.0, ALU.mult, ALU.add).then_inc(
                sem("masks_ready"), 1)
            ch.after(ch.did(v.tensor_scalar(route[:, 64:80], top8, float(np.finfo(np.float32).eps), None, ALU.max)))
            v.reciprocal(route[:, 80:96], route[:, 64:80]).then_inc(sem("top_sum_ready"), 1)
            v.tensor_tensor_scan(R["place"], new_token[:], mask, 0.0, ALU.mult, ALU.add)
            k = ch.did(v.tensor_copy(R["token"].rearrange("p (i e) -> p i e", e=NE), over(C[:, C_TOK:C_TOK + TILES])))
            v.wait_ge(sem("rank_mm"), 1)
            v.wait_ge(sem("zeroed"), 16 * TOK * TOPK // (8 * P))
            for h in range(2):
                hs = slice(512 * h, 512 * h + 512)
                ins = v.scalar_tensor_tensor(scratch[:, hs], bank[h][:], 1.0, mask[:, hs], ALU.add, ALU.mult)
            ins.then_inc(sem("rank_read"), 1)
            v.wait_ge(sem("rank_read"), 1)
            scr_i = scratch[:].bitcast(I32)
            ch.after(ch.did(v.tensor_scalar(logits_i, scratch[:], -1.0, None, ALU.add)))
            k1 = ch.did(v.tensor_scalar(scr_i, logits_i, RA - 1, None, ALU.bitwise_and))
            ch.after(k1)
            v.tensor_scalar(logits_i, logits_i, 4, None, ALU.arith_shift_right).then_inc(sem("b_index"), 1)
            ch.after(ch.did(v.tensor_copy(R["ai"], scr_i)))
            v.wait_ge(sem("bi_ready"), 1)
            a_out = R["a"].rearrange("p i (g a e) -> p i g a e", a=RA, e=EG)
            a_in = R["ai"].rearrange("p (i g e) -> p i g e", g=NEG, e=EG)
            by_tile = lambda t: t.rearrange("p (i e) -> p i e", i=TILES)
            b_in, token, place = by_tile(R["bi"]), by_tile(R["token"]), by_tile(R["place"])
            b_out = R["b"].rearrange("p b (i e) -> p b i e", e=NE)
            here = [by_tile(zeros[:, 256 + 128 * h:384 + 128 * h].bitcast(F16)) for h in range(3)]
            own = C[:, C_EXP:C_EXP + EG]

            def one_hots(q):
                experts = bass.ds(2 * EG * q, 2 * EG)
                for a in range(RA):
                    v.tensor_scalar(a_out[:, :, bass.ds(2 * q, 2), a, :], a_in[:, :, bass.ds(2 * q, 2), :], float(a),
                                    None, ALU.is_equal)
                k = ch.did(v.tensor_scalar(here[0], b_in[:, :, experts], 0.0, None, ALU.is_equal))
                for b in range(RB):
                    ch.after(k)
                    if b + 1 < RB:
                        k = ch.did(v.tensor_scalar(here[(b + 1) % 3], b_in[:, :, experts], float(b + 1), None,
                                                   ALU.is_equal))
                    v.tensor_tensor(b_out[:, b, :, experts], here[b % 3], token[:, :, experts], ALU.mult)
                    ins = v.tensor_tensor(b_out[:, RB + b, :, experts], here[b % 3], place[:, :, experts], ALU.mult)
                ins.then_inc(sem("one_hots_ready"), 1)

            def indices(q):
                v.wait_ge(sem("slots_mm"), q + 1)
                v.tensor_tensor(picked[:], bank[1][:, 0:4 * RB * EG].rearrange("p (u b e) -> p u b e", u=2, e=EG),
                                own.unsqueeze(1).unsqueeze(1).to_broadcast([P, 2, 2 * RB, EG]), ALU.mult).then_inc(
                    sem("slots_read"), 1)
                v.wait_ge(sem("slots_read"), q + 1)
                ch.after(ch.did(v.tensor_reduce(slots[:, bass.ds(2 * q, 2)].rearrange("p g t b -> p g (t b)"), picked[:], AX.X,
                                                ALU.add)))
                tok1, place1 = slots[:, bass.ds(2 * q, 2), 0, :], slots[:, bass.ds(2 * q, 2), 1, :]
                t8, pad = (zeros[:, 32 * h:32 * h + 2 * RB].rearrange("p (g b) -> p g b", b=RB) for h in range(2))
                v.tensor_scalar(gather_all[:, bass.ds(2 * q, 2)], tok1, -1.0, 0.0, ALU.add, ALU.max)
                v.scalar_tensor_tensor(t8, tok1, float(TOPK), place1, ALU.mult, ALU.add)
                ch.after(ch.did(v.tensor_scalar(pad, tok1, 0.0, float(SKIP + TOPK + 1), ALU.is_equal, ALU.mult)))
                v.scalar_tensor_tensor(scatter_all[:, bass.ds(2 * q, 2)], t8, -float(TOPK + 1), pad, ALU.add,
                                       ALU.add).then_inc(sem("indices_ready"), 1)

            one_hots(0)
            with v.Fori(1, NEG // 2) as q:
                ch.loop(q - 1, RB + 2)
                v.wait_ge(sem("one_hots_ready"), q)
                one_hots(q)
                indices(q - 1)
            ch.end_loop(NEG // 2 - 1)
            indices(NEG // 2 - 1)

            def columns_of(G, u, c):
                nb = min(4, RB - 4 * c)
                v.wait_ge(sem("turned_x"), 3 * G + c + 1)
                v.tensor_copy(E["xt"][:, u].rearrange("p e (b a) -> p b a e", a=RA)[:, 4 * c:4 * c + nb],
                              bank[7 - c % 2][:, 0:P * nb].rearrange("p (b a e) -> p b a e", a=RA, e=EG)).then_inc(
                    sem("xt_ready"), 1)
                if c == 2:
                    v.tensor_tensor(picked_gate[:], got[u][:, :, bass.ds(D + G * EG, EG)],
                                    own.unsqueeze(1).to_broadcast([P, RB, EG]), ALU.mult).then_inc(
                        sem("picked_gates"), 1)
                    v.wait_ge(sem("picked_gates"), G + 1)
                    v.tensor_reduce(slot_gate[:, u, :], picked_gate[:], AX.X, ALU.add).then_inc(
                        sem("slot_gate_ready"), 1)

            def product(G, u, j):
                n = G * EG + j
                v.wait_ge(sem("silu_ready"), n + 1)
                v.wait_ge(sem("value_mm"), n + 1)
                if not isinstance(n, int) or n > 1:
                    v.wait_ge(sem("y_mm"), n - 1)
                v.tensor_tensor(E["prod"][:, j % 2, :], bank[2 * (j % 2)][:, 0:FB * CAP], E["silu"][:, j % 2, :],
                                ALU.mult).then_inc(sem("prod_g_ready"), 1)

            def rows_back(G, u, m, c):
                if c == 0:
                    if not isinstance(m, int) or m:
                        v.wait_ge(sem(f"scattered{u}"), 16 * RB * m)
                    v.wait_ge(sem("slot_gate_ready"), G + 1)
                nb = min(4, RB - 4 * c)
                v.wait_ge(sem("turned_y"), 3 * G + c + 1)
                v.tensor_tensor(E["back"][:, u, 4 * c:4 * c + nb, :],
                                bank[6 + c % 2][:, 0:P * nb].rearrange("p (b d) -> p b d", d=D),
                                slot_gate[:, u, 4 * c:4 * c + nb].unsqueeze(2).to_broadcast([P, nb, D]),
                                ALU.mult).then_inc(sem("turned_y_read"), 1)

            def expert_group(G, u, m):
                for j in range(EG):
                    product(G, u, j)
                    if j in RESULTS_AT and (not isinstance(G, int) or G > 0):
                        rows_back(G - 1, 1 - u, m if u else m - 1, RESULTS_AT.index(j))
                    if j in INPUTS_AT and (not isinstance(G, int) or G < NEG - 1):
                        columns_of(G + 1, 1 - u, INPUTS_AT.index(j))

            for c in range(3):
                columns_of(0, 0, c)
            expert_groups(v, expert_group)
            for c in range(3):
                rows_back(NEG - 1, 1, NEG // 2 - 1, c)

            H = B["h"]
            pe_rows = C[:, C_PE:C_PE + 2 * D].rearrange("p (s d) -> p s d", s=2)
            root_d = float(np.float32(np.sqrt(np.float32(D))))
            blk = C[:, C_BLK:C_BLK + P]

            def collect(g):
                v.wait_ge(sem(f"returned_in{g}"), 16 * GT)
                for t in range(GT - 1):
                    k = ch.did(v.tensor_reduce(H[:, g, t, :], spare[GT * g + t].rearrange("p (k d) -> p d k", d=D), AX.X,
                                               ALU.add))
                ch.after(k)
                v.wait_ge(sem("pool_sums"), 3 * (g + 1))
                v.wait_ge(sem("base_ready"), g + 1)
                ch.after(ch.did(v.tensor_tensor(H[:, g], H[:, g], tiles(shared, g), ALU.add)))
                norm_stats(v, ch, "combine", g, g, H[:, g])

            def begin_state(g):
                norm_apply(v, "combine", g, g, H[:, g], tiles(x2, g), "x2_ready")
                v.wait_ge(sem("x2_ready"), g + 1)
                for h in range(2):
                    ins = v.scalar_tensor_tensor(state[:, GT * g + 2 * h:GT * g + 2 * h + 2, :],
                                                 x2[:, GT * g + 2 * h:GT * g + 2 * h + 2, :], root_d, pe_rows,
                                                 ALU.mult, ALU.add)
                ins.then_inc(sem("x_ready"), 1)

            def features(n, g, l):
                for h in range(2):
                    v.wait_ge(sem("kv1_mm"), 2 * n + h + 1)
                    v.tensor_tensor(zrow(g)[:, 2 * h:2 * h + 2, 0:2 * D],
                                    bank[3 + h][:].rearrange("p (i n) -> p i n", i=2),
                                    lrows[:, bass.ds(l, 1), 0:2 * D].to_broadcast([P, 2, 2 * D]), ALU.add).then_inc(
                        sem("z_ready"), 1)
                v.wait_ge(sem("eq_ready"), n + 1)
                ch.after(ch.did(v.tensor_scalar(B["eq"][:, g % 2], B["eq"][:, g % 2], 1.0, None, ALU.min)))
                v.scalar_tensor_tensor(B["q"][:, g], bank[2][:], bq_up[:, bass.ds(l, 1)], B["eq"][:, g % 2], ALU.add,
                                       ALU.max).then_inc(sem("q1_ready"), 1)

            def features_k(n, g):
                v.wait_ge(sem("ek_ready"), n + 1)
                v.scalar_tensor_tensor(B["kp"][:, g], B["ek"][:, g % 2], 1.0, zrow(g)[:, :, 0:D], ALU.min,
                                       ALU.max).then_inc(sem("kp_ready"), 1)

            def mask_kv(n, g):
                v.wait_ge(sem("kvsum_mm"), n + 1)
                kvs = bank[5][:, 0:2 * (D + 1)].rearrange("p (b n) -> p b n", b=2)
                v.tensor_tensor(kvm(g)[:, :, 0:D], kvs[:, :, 0:D], blk.unsqueeze(1).to_broadcast([P, 2, D]), ALU.mult)
                v.tensor_tensor(kvm(g)[:, :, D:D + HEADS], head.unsqueeze(1).to_broadcast([P, 2, HEADS]),
                                kvs[:, :, D:D + 1].to_broadcast([P, 2, HEADS]), ALU.mult).then_inc(
                    sem("kvm_ready"), 1)

            def divide(n, g):
                s = g % 2
                v.wait_ge(sem("num_mm"), n + 1)
                parts = [bank[6 + h][:, 0:2 * (D + HEADS)].rearrange("p (i n) -> p i n", i=2) for h in range(2)]
                for h in range(2):
                    k = ch.did(v.tensor_scalar(den1[:, s, 2 * h:2 * h + 2, :], parts[h][:, :, D:D + HEADS],
                                               EPS_ATTN, None, ALU.add))
                ch.after(k)
                ch.after(ch.did(v.reciprocal(rden1[:, s], den1[:, s])))
                for h in range(2):
                    ins = v.tensor_tensor(
                        H[:, g, 2 * h:2 * h + 2, :].rearrange("p i (h d) -> p i h d", d=DH),
                        parts[h][:, :, 0:D].rearrange("p i (h d) -> p i h d", d=DH),
                        rden1[:, s, 2 * h:2 * h + 2, :].unsqueeze(3).to_broadcast([P, 2, HEADS, DH]), ALU.mult)
                ins.then_inc(sem("an1_ready"), 1)

            def residual1(n, g):
                v.wait_ge(sem("out1_mm"), n + 1)
                v.wait_ge(sem("plus_bo"), n + 1)
                v.tensor_tensor(tiles(state, g), bank3(2), tiles(plus, g), ALU.add).then_inc(sem("mid_ready"), 1)

            def residual2(n, g):
                v.wait_ge(sem("down_mm"), n + 1)
                v.wait_ge(sem("plus_b2"), n + 1)
                v.tensor_tensor(tiles(state, g), bank3(5), tiles(plus, g), ALU.add).then_inc(sem("x_ready"), 1)

            def apply_final(g):
                b = 2 * NORMS["final"][0] + g % 2
                v.wait_ge(sem("fin_in"), 16)
                for t in range(GT):
                    k = ch.did(v.scalar_tensor_tensor(H[:, g, t, :], tiles(state, g)[:, t, :], mv[:, b, t, 0:1],
                                                      fin_rows[:, 0:D], ALU.subtract, ALU.mult))
                v.wait_ge(sem("rstd0_ready"), NORMS["final"][1] + g + 1)
                v.wait_ge(sem("plus_lnf"), g + 1)
                ch.after(k)
                for t in range(GT):
                    k = ch.did(v.scalar_tensor_tensor(H[:, g, t, :], H[:, g, t, :], rstd[:, b, t:t + 1],
                                                      tiles(plus, g)[:, t, :], ALU.mult, ALU.add))
                ch.after(k)
                norm_stats(v, ch, "second", g, g, H[:, g])

            before = C[:, C_BEFORE:C_BEFORE + 2 * SEQ].rearrange("p (h n) -> p h n", h=2)
            own_s, higher, equal, place_s = (small[:, 800 + 16 * k:816 + 16 * k] for k in range(4))
            chosen_m = small[:, 864:880]
            junk = B["ek"].rearrange("p s i d -> p (s i d)")

            def choose(g):
                gs = slice(GT * g, GT * g + GT)
                v.wait_ge(sem("scores_ready"), g + 1)
                for t in range(GT):
                    k = ch.did(v.scalar_tensor_tensor(B["eq"][:, g % 2, P * t:P * t + P],
                                                      scores[:, g % 2, P * t:P * t + P], 1.0, ident, ALU.mult, ALU.mult,
                                                      accum_out=own_s[:, GT * g + t:GT * g + t + 1]))
                ch.after(k)
                for t in range(GT):
                    i = GT * g + t
                    seq = scores[:, g % 2, SEQ * (t // 2):SEQ * (t // 2 + 1)]
                    v.tensor_scalar(junk[:, 0:SEQ] if t % 2 else junk[:, SEQ:2 * SEQ], seq, own_s[:, i:i + 1], None,
                                    ALU.is_gt, ALU.add, accum_out=higher[:, i:i + 1])
                    ch.after(ch.did(v.scalar_tensor_tensor(
                        junk[:, 2 * SEQ:3 * SEQ] if t % 2 else junk[:, 3 * SEQ:4 * SEQ], seq, own_s[:, i:i + 1],
                        before[:, t % 2, :], ALU.is_equal, ALU.mult, accum_out=equal[:, i:i + 1])))
                ch.after(ch.did(v.tensor_tensor(place_s[:, gs], higher[:, gs], equal[:, gs], ALU.add)))
                v.tensor_scalar(chosen_m[:, gs], place_s[:, gs], float(KEEP), None, ALU.is_lt).then_inc(sem("chosen"), 1)

            def blend(g):
                v.wait_ge(sem("processed_ready"), g + 1)
                v.wait_ge(sem("twice_ready"), g + 1)
                v.wait_ge(sem("chosen"), g + 1)
                gl = B["q"][:, g].rearrange("p (i d) -> p i d", d=D)
                for t in range(GT):
                    i = GT * g + t
                    k = ch.did(v.copy_predicated(B["kp"][:, g, t, :], chosen_m[:, i:i + 1].bitcast(U32).to_broadcast([P, D]),
                                                 gl[:, t, :]))
                ch.after(k)
                norm_stats(v, ch, "last", g, g, B["kp"][:, g])

            def slot(t, k, l):
                g = k % GROUPS
                if item(k, 1):
                    mask_kv(t - 1, (g - 1) % GROUPS)
                if item(k, 2):
                    n2, g2 = t - 2, (g - 2) % GROUPS
                    v.wait_ge(sem("mid_ready"), n2 + 1)
                    norm_stats(v, ch, "norm2", n2, g2, tiles(state, g2))
                if item(k, 1):
                    divide(t - 1, (g - 1) % GROUPS)
                if item(k, 2):
                    norm_apply(v, "norm2", n2, g2, tiles(state, g2), H[:, g2], "h2_ready")
                if item(k, 0):
                    features(t, g, layer_of(l, k, 0))
                    features_k(t, g)
                if item(k, 3):
                    residual2(t - 3, (g - 3) % GROUPS)
                if 0 <= k + 1 < GROUPS:
                    begin_state(k + 1)
                if item(k, -1):
                    g1 = (g + 1) % GROUPS
                    v.wait_ge(sem("x_ready"), t + 2)
                    norm_stats(v, ch, "norm1", t + 1, g1, tiles(state, g1))
                if 0 <= k - (ITEMS - 1) < GROUPS:
                    f = k - (ITEMS - 1)
                    v.wait_ge(sem("x_ready"), ITEMS + f + 1)
                    norm_stats(v, ch, "final", f, f, tiles(state, f))
                if item(k, 1):
                    residual1(t - 1, (g - 1) % GROUPS)
                if 0 <= k + 2 < GROUPS:
                    collect(k + 2)
                if item(k, -1):
                    norm_apply(v, "norm1", t + 1, g1, tiles(state, g1), H[:, g1], "h1_ready")
                if 0 <= k - (ITEMS + 1) < GROUPS:
                    choose(k - (ITEMS + 1))
                if 0 <= k - (ITEMS - 1) < GROUPS:
                    apply_final(f)
                if 0 <= k - (ITEMS + 1) < GROUPS:
                    blend(k - (ITEMS + 1))

            for u in range(2):
                v.wait_ge(sem(f"scattered{u}"), 16 * RB * NEG // 2)
            for g in range(GROUPS):
                v.memset(zrow(g)[:, :, 2 * D:Z], 1.0)
            v.wait_ge(sem("cols_in"), 16)
            v.wait_ge(sem("rows_in"), 16)
            v.tensor_scalar(bq_up[:], layer_cols[:, :, 0], 1.0, None, ALU.add)
            ch.after(ch.did(v.tensor_scalar(lrows[:, :, 0:D], lrows[:, :, 0:D], 1.0, None, ALU.add)))
            steps = GROUPS * (2 * 2 * GT + 1 + 3)

            def body(l):
                if l is None:
                    ch.end_loop(LAYERS - 1)
                else:
                    ch.loop(l - 1, steps)

            pipeline(v, slot, body)


def pack(inputs):
    a = {k: np.asarray(v) for k, v in inputs.items()}
    c = np.ascontiguousarray
    x = a["L0_attn_x"].reshape(TOK, D)
    wv = a["L0_attn_Wv"].T.reshape(D, HEADS, DH)
    vrep = [np.repeat(wv[:, :, e], DH, axis=1) for e in range(DH)]
    wo = a["L0_attn_Wo"].T.reshape(HEADS, DH, D).transpose(1, 0, 2).reshape(D, D)
    bv = a["L0_attn_bv"].reshape(HEADS, DH)
    l0p = np.stack([a["L0_attn_bq"], a["L0_attn_bk"]] + [np.repeat(bv[:, e], DH) for e in range(DH)], axis=1)
    sw2 = a["L0_ffn_shared_w2"].T.reshape(FB, P, D).transpose(1, 0, 2).reshape(P, FB * D)
    w1 = a["L0_ffn_expert_w1"].transpose(0, 2, 1)
    w2 = a["L0_ffn_expert_w2"].transpose(0, 2, 1).reshape(NE, FB, P, D).transpose(0, 2, 1, 3).reshape(NE, P, FB * D)
    lw2 = a["L1_attn_W2"].reshape(LAYERS, FFB, P, D).transpose(0, 2, 1, 3).reshape(LAYERS, P, FFB * D)
    b1 = a["L1_attn_b1"].reshape(LAYERS, FFB, P).transpose(0, 2, 1)
    cols = [a["L1_attn_" + n][:, :, None] for n in ("bq", "ln1_s", "ln1_b", "ln2_s", "ln2_b")]
    return {
        "cst": constants(),
        "xt0": c(x.T),
        "xr0": c(x.reshape(TILES, P, D).transpose(1, 0, 2)),
        "l0w": c(np.concatenate([a["L0_attn_Wq"].T, a["L0_attn_Wk"].T] + vrep + [wo], axis=1)),
        "l0p": c(l0p),
        "bo0": c(a["L0_attn_bo"]),
        "l0s": c(np.concatenate([a["L0_ffn_wg"].T, a["L0_ffn_shared_w1"].T, sw2], axis=1)),
        "ew": c(np.concatenate([w1, w2], axis=2)),
        "l1w": c(np.concatenate([a["L1_attn_Wq"], a["L1_attn_Wk"], a["L1_attn_Wv"], a["L1_attn_Wo"],
                                 a["L1_attn_W1"], lw2], axis=2)),
        "l1p": c(np.concatenate(cols + [b1], axis=2).transpose(1, 0, 2)),
        "l1r": c(np.stack([a["L1_attn_bk"], a["L1_attn_bv"], a["L1_attn_bo"], a["L1_attn_b2"]], axis=1)),
        "fin_r": c(np.stack([a["L1_attn_lnf_s"], a["L1_attn_lnf_b"]])),
        "mod_w": c(np.concatenate([np.repeat(a["L1_ffn_w_router"][:, None], P, axis=1), a["L1_ffn_w_block"]], axis=1)),
    }


def kernel(**inputs):
    from concourse import bacc
    from concourse.bass_utils import run_bass_kernel_spmd

    nc = bacc.Bacc("TRN2", target_bir_lowering=False, num_devices=1)
    arrays = {f"in_{k}": v for k, v in pack(inputs).items()}
    aps = [nc.dram_tensor(k, v.shape, mybir.dt.from_np(v.dtype), kind="ExternalInput").ap() for k, v in arrays.items()]
    out = nc.dram_tensor("out", (P, TILES, D), F32, kind="ExternalOutput").ap()
    program(nc, *aps, out)
    r = run_bass_kernel_spmd(nc, [arrays], core_ids=[0])
    got = r.results[0]["out"]
    return np.ascontiguousarray(got.transpose(1, 0, 2).reshape(BATCH, SEQ, D))
```
